# Optimizing a Trainium2 kernel written in Bass

```python
import numpy as np
import jax
import jax.numpy as jnp

def _softmax(x, axis=-1):
    return jax.nn.softmax(x, axis=axis)

def _gelu(x):
    return jax.nn.gelu(x, approximate=True)

def _silu(x):
    return jax.nn.silu(x)

def _sigmoid(x):
    return jax.nn.sigmoid(x)

def _layernorm(x, axis=-1, eps=1e-05):
    m = jnp.mean(x, axis=axis, keepdims=True)
    v = jnp.var(x, axis=axis, keepdims=True)
    return (x - m) / jnp.sqrt(v + eps)

def _scatter_add(tgt, idx, src, axis=0):
    return tgt.at[idx].add(src)

def _segment_sum(src, seg, n):
    return jax.ops.segment_sum(src, seg, n)
kernel_name = 'mk_prb_d2_jaxref_r8_c65623'

def setup_inputs(seed: int=0):
    np.random.seed(seed)
    _w = jnp.asarray

    def _L0_attn_setup():
        import jax, jax.numpy as jnp
        import numpy as np
        B, T, DIM = (4, 512, 128)
        HEADS, HEAD_DIM = (16, 64)
        CHUNK, STRIDE = (64, 64)
        GATING = 1.0
        key = jax.random.key(seed)
        ks = jax.random.split(key, 9)
        s = 0.02
        return {'x': jax.random.normal(ks[0], (B, T, DIM), jnp.float32), 'Wq': jax.random.normal(ks[1], (DIM, HEADS * HEAD_DIM), jnp.float32) * s, 'bq': jax.random.normal(ks[2], (HEADS * HEAD_DIM,), jnp.float32) * s, 'Wk': jax.random.normal(ks[3], (DIM, HEADS * HEAD_DIM), jnp.float32) * s, 'bk': jax.random.normal(ks[4], (HEADS * HEAD_DIM,), jnp.float32) * s, 'Wv': jax.random.normal(ks[5], (DIM, HEADS * HEAD_DIM), jnp.float32) * s, 'bv': jax.random.normal(ks[6], (HEADS * HEAD_DIM,), jnp.float32) * s, 'Wo': jax.random.normal(ks[7], (HEADS * HEAD_DIM, DIM), jnp.float32) * s, 'bo': jax.random.normal(ks[8], (DIM,), jnp.float32) * s}
    _L0_attn_in = _L0_attn_setup()

    def _L0_ffn_setup():
        import jax, jax.numpy as jnp
        import numpy as np
        DIM = 128
        NQ = 16
        NKV = 4
        HD = DIM // NQ
        HID = 256
        E = 8
        B, S = (1, 128)
        EPS = 1e-06

        def rmsnorm(x, w):
            ms = jnp.mean(x * x, axis=-1, keepdims=True)
            return w * (x * jax.lax.rsqrt(ms + EPS))

        def rope_tables(seq_len, head_dim):
            inv_freq = 1.0 / 10000.0 ** (jnp.arange(0, head_dim, 2, dtype=jnp.float32) / head_dim)
            t = jnp.arange(seq_len, dtype=jnp.float32)
            freqs = jnp.einsum('i,j->ij', t, inv_freq)
            return (jnp.cos(freqs), jnp.sin(freqs))

        def apply_rope(x, cos, sin):
            c = cos[None, :, None, :]
            s = sin[None, :, None, :]
            half = x.shape[-1] // 2
            x1, x2 = (x[..., :half], x[..., half:])
            return jnp.concatenate([x1 * c - x2 * s, x1 * s + x2 * c], axis=-1)

        def _forward(x, ln1_w, ln2_w, Wq, bq, Wk, bk, Wv, bv, qn_w, kn_w, Wg, bg, Wo, bo, Wr, br, W1, b1, W2, b2):
            batch, seq, _ = x.shape
            cos, sin = rope_tables(seq, HD)
            h = rmsnorm(x, ln1_w)
            q = (h @ Wq + bq).reshape(batch, seq, NQ, HD)
            k = (h @ Wk + bk).reshape(batch, seq, NKV, HD)
            v = (h @ Wv + bv).reshape(batch, seq, NKV, HD)
            q = rmsnorm(apply_rope(q, cos, sin), qn_w)
            k = rmsnorm(apply_rope(k, cos, sin), kn_w)
            rep = NQ // NKV
            k = jnp.repeat(k, rep, axis=2)
            v = jnp.repeat(v, rep, axis=2)
            scores = jnp.einsum('bthd,bshd->bhts', q, k) / np.sqrt(HD)
            causal = jnp.tril(jnp.ones((seq, seq), dtype=bool))
            scores = jnp.where(causal[None, None], scores, -jnp.inf)
            attn = jax.nn.softmax(scores, axis=-1)
            out = jnp.einsum('bhts,bshd->bthd', attn, v)
            gate = jax.nn.sigmoid(out @ Wg + bg)
            out = (out * gate).reshape(batch, seq, DIM)
            x = x + out @ Wo + bo
            h2 = rmsnorm(x, ln2_w)
            logits = h2 @ Wr + br
            top1 = jnp.argmax(logits, axis=-1).reshape(-1)
            xt = h2.reshape(-1, DIM)
            u = jnp.einsum('td,edf->tef', xt, W1) + b1
            u1, u2 = (u[..., :HID], u[..., HID:])
            act = u1 * jax.nn.sigmoid(u2)
            y_all = jnp.einsum('teh,ehd->ted', act, W2) + b2
            y = jnp.take_along_axis(y_all, top1[:, None, None], axis=1)[:, 0, :]
            return x + y.reshape(batch, seq, DIM)
        key = jax.random.key(seed)
        ks = jax.random.split(key, 20)
        sc = lambda fan_in: 1.0 / np.sqrt(fan_in)
        d = {}
        d['x'] = jax.random.normal(ks[0], (B, S, DIM), dtype=jnp.float32)
        d['ln1_w'] = jnp.ones((DIM,), jnp.float32)
        d['ln2_w'] = jnp.ones((DIM,), jnp.float32)
        d['Wq'] = jax.random.normal(ks[1], (DIM, DIM), jnp.float32) * sc(DIM)
        d['bq'] = jnp.zeros((DIM,), jnp.float32)
        d['Wk'] = jax.random.normal(ks[2], (DIM, HD * NKV), jnp.float32) * sc(DIM)
        d['bk'] = jnp.zeros((HD * NKV,), jnp.float32)
        d['Wv'] = jax.random.normal(ks[3], (DIM, HD * NKV), jnp.float32) * sc(DIM)
        d['bv'] = jnp.zeros((HD * NKV,), jnp.float32)
        d['qn_w'] = jnp.ones((HD,), jnp.float32)
        d['kn_w'] = jnp.ones((HD,), jnp.float32)
        d['Wg'] = jax.random.normal(ks[4], (HD, HD), jnp.float32) * sc(HD)
        d['bg'] = jnp.zeros((HD,), jnp.float32)
        d['Wo'] = jax.random.normal(ks[5], (DIM, DIM), jnp.float32) * sc(DIM)
        d['bo'] = jnp.zeros((DIM,), jnp.float32)
        d['Wr'] = jax.random.normal(ks[6], (DIM, E), jnp.float32) * sc(DIM)
        d['br'] = jnp.zeros((E,), jnp.float32)
        d['W1'] = jax.random.normal(ks[7], (E, DIM, 2 * HID), jnp.float32) * sc(DIM)
        d['b1'] = jnp.zeros((E, 2 * HID), jnp.float32)
        d['W2'] = jax.random.normal(ks[8], (E, HID, DIM), jnp.float32) * sc(HID)
        d['b2'] = jnp.zeros((E, DIM), jnp.float32)
        return d
    _L0_ffn_in = _L0_ffn_setup()

    def _L1_attn_setup():
        import jax, jax.numpy as jnp
        import numpy as np
        D_MODEL = 128
        D_STATE = 128
        HEAD_DIM = 64
        EXPAND = 2
        K = 4
        N_GROUPS = 1
        D_INNER = EXPAND * D_MODEL
        N_HEADS = D_INNER // HEAD_DIM
        D_PROJ = 2 * D_INNER + 2 * N_GROUPS * D_STATE + N_HEADS
        EPS = 1e-06

        def _rmsnorm(x, w):
            return x * jax.lax.rsqrt(jnp.mean(x * x, axis=-1, keepdims=True) + EPS) * w
        key = jax.random.key(seed)
        ks = jax.random.split(key, 8)
        B, L = (2, 256)
        x = jax.random.normal(ks[0], (B, L, D_MODEL), jnp.float32)
        norm_w = jnp.ones((D_MODEL,), jnp.float32)
        in_proj_w = jax.random.normal(ks[1], (D_PROJ, D_MODEL), jnp.float32) / np.sqrt(D_MODEL).astype(np.float32)
        conv_w = jax.random.normal(ks[2], (D_INNER, K), jnp.float32) / np.sqrt(K).astype(np.float32)
        conv_b = jnp.zeros((D_INNER,), jnp.float32)
        A_log = jnp.log(jax.random.uniform(ks[3], (N_HEADS,), jnp.float32) * 15.0 + 1.0)
        D = jnp.ones((N_HEADS,), jnp.float32)
        dt_bias = jnp.log(jax.random.uniform(ks[4], (N_HEADS,), jnp.float32) * 0.099 + 0.001)
        out_proj_w = jax.random.normal(ks[5], (D_MODEL, D_INNER), jnp.float32) / np.sqrt(D_INNER).astype(np.float32)
        return dict(x=x, norm_w=norm_w, in_proj_w=in_proj_w, conv_w=conv_w, conv_b=conv_b, A_log=A_log, D=D, dt_bias=dt_bias, out_proj_w=out_proj_w)
    _L1_attn_in = _L1_attn_setup()

    def _L1_ffn_setup():
        import jax, jax.numpy as jnp
        import numpy as np
        D_IN, D_HID = (128, 512)

        def _ternary(key, shape):
            return jax.random.randint(key, shape, -1, 2).astype(jnp.float32)

        def _tlin(x, w, s):
            return jnp.einsum('bsi,oi->bso', x, w) * s
        key = jax.random.key(seed)
        ks = jax.random.split(key, 12)
        inv = lambda fan: 1.0 / np.sqrt(fan).astype(np.float32)
        return {'x': jax.random.normal(ks[0], (4, 256, D_IN), dtype=jnp.float32), 'w1_w': _ternary(ks[1], (D_HID, D_IN)), 'w1_s': jax.random.uniform(ks[2], (D_HID,), dtype=jnp.float32) * inv(D_IN), 'w2_w': _ternary(ks[3], (D_HID, D_IN)), 'w2_s': jax.random.uniform(ks[4], (D_HID,), dtype=jnp.float32) * inv(D_IN), 'h1_w': _ternary(ks[5], (D_HID, D_HID)), 'h1_s': jax.random.uniform(ks[6], (D_HID,), dtype=jnp.float32) * inv(D_HID), 'h2_w': _ternary(ks[7], (D_HID, D_HID)), 'h2_s': jax.random.uniform(ks[8], (D_HID,), dtype=jnp.float32) * inv(D_HID), 'w3_w': _ternary(ks[9], (D_IN, D_HID)), 'w3_s': jax.random.uniform(ks[10], (D_IN,), dtype=jnp.float32) * inv(D_HID)}
    _L1_ffn_in = _L1_ffn_setup()
    _d = {'L0_attn_x': _L0_attn_in['x'], 'L0_attn_Wq': _L0_attn_in['Wq'], 'L0_attn_bq': _L0_attn_in['bq'], 'L0_attn_Wk': _L0_attn_in['Wk'], 'L0_attn_bk': _L0_attn_in['bk'], 'L0_attn_Wv': _L0_attn_in['Wv'], 'L0_attn_bv': _L0_attn_in['bv'], 'L0_attn_Wo': _L0_attn_in['Wo'], 'L0_attn_bo': _L0_attn_in['bo'], 'L0_ffn_ln1_w': _L0_ffn_in['ln1_w'], 'L0_ffn_ln2_w': _L0_ffn_in['ln2_w'], 'L0_ffn_Wq': _L0_ffn_in['Wq'], 'L0_ffn_bq': _L0_ffn_in['bq'], 'L0_ffn_Wk': _L0_ffn_in['Wk'], 'L0_ffn_bk': _L0_ffn_in['bk'], 'L0_ffn_Wv': _L0_ffn_in['Wv'], 'L0_ffn_bv': _L0_ffn_in['bv'], 'L0_ffn_qn_w': _L0_ffn_in['qn_w'], 'L0_ffn_kn_w': _L0_ffn_in['kn_w'], 'L0_ffn_Wg': _L0_ffn_in['Wg'], 'L0_ffn_bg': _L0_ffn_in['bg'], 'L0_ffn_Wo': _L0_ffn_in['Wo'], 'L0_ffn_bo': _L0_ffn_in['bo'], 'L0_ffn_Wr': _L0_ffn_in['Wr'], 'L0_ffn_br': _L0_ffn_in['br'], 'L0_ffn_W1': _L0_ffn_in['W1'], 'L0_ffn_b1': _L0_ffn_in['b1'], 'L0_ffn_W2': _L0_ffn_in['W2'], 'L0_ffn_b2': _L0_ffn_in['b2'], 'L1_attn_norm_w': _L1_attn_in['norm_w'], 'L1_attn_in_proj_w': _L1_attn_in['in_proj_w'], 'L1_attn_conv_w': _L1_attn_in['conv_w'], 'L1_attn_conv_b': _L1_attn_in['conv_b'], 'L1_attn_A_log': _L1_attn_in['A_log'], 'L1_attn_D': _L1_attn_in['D'], 'L1_attn_dt_bias': _L1_attn_in['dt_bias'], 'L1_attn_out_proj_w': _L1_attn_in['out_proj_w'], 'L1_ffn_w1_w': _L1_ffn_in['w1_w'], 'L1_ffn_w1_s': _L1_ffn_in['w1_s'], 'L1_ffn_w2_w': _L1_ffn_in['w2_w'], 'L1_ffn_w2_s': _L1_ffn_in['w2_s'], 'L1_ffn_h1_w': _L1_ffn_in['h1_w'], 'L1_ffn_h1_s': _L1_ffn_in['h1_s'], 'L1_ffn_h2_w': _L1_ffn_in['h2_w'], 'L1_ffn_h2_s': _L1_ffn_in['h2_s'], 'L1_ffn_w3_w': _L1_ffn_in['w3_w'], 'L1_ffn_w3_s': _L1_ffn_in['w3_s']}
    _x0 = _d['L0_attn_x']
    _d['L0_attn_x'] = jax.random.normal(jax.random.fold_in(jax.random.key(seed), 1), (1, 2048, 128), dtype=_x0.dtype)
    del _x0
    return _d

def reference(L0_attn_x, L0_attn_Wq, L0_attn_bq, L0_attn_Wk, L0_attn_bk, L0_attn_Wv, L0_attn_bv, L0_attn_Wo, L0_attn_bo, L0_ffn_ln1_w, L0_ffn_ln2_w, L0_ffn_Wq, L0_ffn_bq, L0_ffn_Wk, L0_ffn_bk, L0_ffn_Wv, L0_ffn_bv, L0_ffn_qn_w, L0_ffn_kn_w, L0_ffn_Wg, L0_ffn_bg, L0_ffn_Wo, L0_ffn_bo, L0_ffn_Wr, L0_ffn_br, L0_ffn_W1, L0_ffn_b1, L0_ffn_W2, L0_ffn_b2, L1_attn_norm_w, L1_attn_in_proj_w, L1_attn_conv_w, L1_attn_conv_b, L1_attn_A_log, L1_attn_D, L1_attn_dt_bias, L1_attn_out_proj_w, L1_ffn_w1_w, L1_ffn_w1_s, L1_ffn_w2_w, L1_ffn_w2_s, L1_ffn_h1_w, L1_ffn_h1_s, L1_ffn_h2_w, L1_ffn_h2_s, L1_ffn_w3_w, L1_ffn_w3_s):

    def _L0_attn_ref(x, Wq, bq, Wk, bk, Wv, bv, Wo, bo):
        import jax, jax.numpy as jnp
        import numpy as np
        B, T, DIM = (4, 512, 128)
        HEADS, HEAD_DIM = (16, 64)
        CHUNK, STRIDE = (64, 64)
        GATING = 1.0
        b, t, _ = x.shape
        inner = HEADS * HEAD_DIM
        ends = jnp.arange(0, t, STRIDE, dtype=jnp.int64)
        starts = jnp.clip(ends - CHUNK + 1, 0)
        x_f = x.astype(jnp.float32)
        cs = jnp.cumsum(x_f, axis=1)
        end_sum = cs[:, ends]
        prev_idx = jnp.clip(starts - 1, 0)
        prev_sum = cs[:, prev_idx] * (starts > 0).astype(jnp.float32)[None, :, None]
        lengths = (ends - starts + 1).astype(jnp.float32)[None, :, None]
        summary = ((end_sum - prev_sum) / jnp.maximum(lengths, 1.0)).astype(x.dtype)
        q = (x @ Wq + bq).reshape(b, t, HEADS, HEAD_DIM).transpose(0, 2, 1, 3)
        k = (summary @ Wk + bk).reshape(b, -1, HEADS, HEAD_DIM).transpose(0, 2, 1, 3)
        v = (summary @ Wv + bv).reshape(b, -1, HEADS, HEAD_DIM).transpose(0, 2, 1, 3)
        positions = jnp.arange(t, dtype=jnp.int64)[:, None]
        allowed = ends[None, :] <= positions
        scale = 1.0 / np.sqrt(HEAD_DIM)
        scores = jnp.einsum('bhtd,bhcd->bhtc', q, k) * scale
        scores = jnp.where(allowed[None, None], scores, -jnp.inf)
        attn = jax.nn.softmax(scores, axis=-1)
        out = jnp.einsum('bhtc,bhcd->bhtd', attn, v)
        out = out.transpose(0, 2, 1, 3).reshape(b, t, inner)
        out = out @ Wo + bo
        return out * GATING

    def _L0_ffn_ref(x, ln1_w, ln2_w, Wq, bq, Wk, bk, Wv, bv, qn_w, kn_w, Wg, bg, Wo, bo, Wr, br, W1, b1, W2, b2):
        import jax, jax.numpy as jnp
        import numpy as np
        DIM = 128
        NQ = 16
        NKV = 4
        HD = DIM // NQ
        HID = 256
        E = 8
        B, S = (1, 128)
        EPS = 1e-06

        def rmsnorm(x, w):
            ms = jnp.mean(x * x, axis=-1, keepdims=True)
            return w * (x * jax.lax.rsqrt(ms + EPS))

        def rope_tables(seq_len, head_dim):
            inv_freq = 1.0 / 10000.0 ** (jnp.arange(0, head_dim, 2, dtype=jnp.float32) / head_dim)
            t = jnp.arange(seq_len, dtype=jnp.float32)
            freqs = jnp.einsum('i,j->ij', t, inv_freq)
            return (jnp.cos(freqs), jnp.sin(freqs))

        def apply_rope(x, cos, sin):
            c = cos[None, :, None, :]
            s = sin[None, :, None, :]
            half = x.shape[-1] // 2
            x1, x2 = (x[..., :half], x[..., half:])
            return jnp.concatenate([x1 * c - x2 * s, x1 * s + x2 * c], axis=-1)

        def _forward(x, ln1_w, ln2_w, Wq, bq, Wk, bk, Wv, bv, qn_w, kn_w, Wg, bg, Wo, bo, Wr, br, W1, b1, W2, b2):
            batch, seq, _ = x.shape
            cos, sin = rope_tables(seq, HD)
            h = rmsnorm(x, ln1_w)
            q = (h @ Wq + bq).reshape(batch, seq, NQ, HD)
            k = (h @ Wk + bk).reshape(batch, seq, NKV, HD)
            v = (h @ Wv + bv).reshape(batch, seq, NKV, HD)
            q = rmsnorm(apply_rope(q, cos, sin), qn_w)
            k = rmsnorm(apply_rope(k, cos, sin), kn_w)
            rep = NQ // NKV
            k = jnp.repeat(k, rep, axis=2)
            v = jnp.repeat(v, rep, axis=2)
            scores = jnp.einsum('bthd,bshd->bhts', q, k) / np.sqrt(HD)
            causal = jnp.tril(jnp.ones((seq, seq), dtype=bool))
            scores = jnp.where(causal[None, None], scores, -jnp.inf)
            attn = jax.nn.softmax(scores, axis=-1)
            out = jnp.einsum('bhts,bshd->bthd', attn, v)
            gate = jax.nn.sigmoid(out @ Wg + bg)
            out = (out * gate).reshape(batch, seq, DIM)
            x = x + out @ Wo + bo
            h2 = rmsnorm(x, ln2_w)
            logits = h2 @ Wr + br
            top1 = jnp.argmax(logits, axis=-1).reshape(-1)
            xt = h2.reshape(-1, DIM)
            u = jnp.einsum('td,edf->tef', xt, W1) + b1
            u1, u2 = (u[..., :HID], u[..., HID:])
            act = u1 * jax.nn.sigmoid(u2)
            y_all = jnp.einsum('teh,ehd->ted', act, W2) + b2
            y = jnp.take_along_axis(y_all, top1[:, None, None], axis=1)[:, 0, :]
            return x + y.reshape(batch, seq, DIM)
        return _forward(x, ln1_w, ln2_w, Wq, bq, Wk, bk, Wv, bv, qn_w, kn_w, Wg, bg, Wo, bo, Wr, br, W1, b1, W2, b2)

    def _L1_attn_ref(x, norm_w, in_proj_w, conv_w, conv_b, A_log, D, dt_bias, out_proj_w):
        import jax, jax.numpy as jnp
        import numpy as np
        D_MODEL = 128
        D_STATE = 128
        HEAD_DIM = 64
        EXPAND = 2
        K = 4
        N_GROUPS = 1
        D_INNER = EXPAND * D_MODEL
        N_HEADS = D_INNER // HEAD_DIM
        D_PROJ = 2 * D_INNER + 2 * N_GROUPS * D_STATE + N_HEADS
        EPS = 1e-06

        def _rmsnorm(x, w):
            return x * jax.lax.rsqrt(jnp.mean(x * x, axis=-1, keepdims=True) + EPS) * w
        batch, L, _ = x.shape
        residual = x
        xn = _rmsnorm(x, norm_w)
        proj = jnp.einsum('bld,pd->blp', xn, in_proj_w)
        i = 0
        z = proj[:, :, i:i + D_INNER]
        i += D_INNER
        x_ssm = proj[:, :, i:i + D_INNER]
        i += D_INNER
        bc = N_GROUPS * D_STATE
        Bm = proj[:, :, i:i + bc].reshape(batch, L, N_GROUPS, D_STATE)
        i += bc
        Cm = proj[:, :, i:i + bc].reshape(batch, L, N_GROUPS, D_STATE)
        i += bc
        dt_raw = proj[:, :, i:i + N_HEADS]
        xp = jnp.pad(x_ssm, ((0, 0), (K - 1, 0), (0, 0)))
        x_conv = conv_b
        for k in range(K):
            x_conv = x_conv + xp[:, k:k + L, :] * conv_w[:, k]
        x_conv = jax.nn.silu(x_conv)
        xh = x_conv.reshape(batch, L, N_HEADS, HEAD_DIM)
        dt = jax.nn.softplus(dt_raw + dt_bias)
        dA = jnp.exp(-jnp.exp(A_log) * dt)
        dtx = dt[..., None] * xh
        gidx = jnp.arange(N_HEADS) // (N_HEADS // N_GROUPS)
        Bg = Bm[:, :, gidx, :]
        Cg = Cm[:, :, gidx, :]

        def step(h, inp):
            dA_t, dtx_t, B_t, C_t = inp
            h = h * dA_t[:, :, None, None] + dtx_t[..., None] * B_t[:, :, None, :]
            y_t = jnp.einsum('bhpn,bhn->bhp', h, C_t)
            return (h, y_t)
        h0 = jnp.zeros((batch, N_HEADS, HEAD_DIM, D_STATE), jnp.float32)
        xs = (jnp.swapaxes(dA, 0, 1), jnp.swapaxes(dtx, 0, 1), jnp.swapaxes(Bg, 0, 1), jnp.swapaxes(Cg, 0, 1))
        _, ys = jax.lax.scan(step, h0, xs)
        y = jnp.swapaxes(ys, 0, 1) + D[None, None, :, None] * xh
        y = y.reshape(batch, L, D_INNER) * jax.nn.silu(z)
        return residual + jnp.einsum('bli,di->bld', y, out_proj_w)

    def _L1_ffn_ref(x, w1_w, w1_s, w2_w, w2_s, h1_w, h1_s, h2_w, h2_s, w3_w, w3_s):
        import jax, jax.numpy as jnp
        import numpy as np
        D_IN, D_HID = (128, 512)

        def _ternary(key, shape):
            return jax.random.randint(key, shape, -1, 2).astype(jnp.float32)

        def _tlin(x, w, s):
            return jnp.einsum('bsi,oi->bso', x, w) * s
        h = jax.nn.silu(_tlin(x, w1_w, w1_s)) * _tlin(x, w2_w, w2_s)
        h = jax.nn.gelu(_tlin(h, h1_w, h1_s), approximate=False)
        h = jax.nn.gelu(_tlin(h, h2_w, h2_s), approximate=False)
        return _tlin(h, w3_w, w3_s)
    x = L0_attn_x
    xn = _layernorm(x, axis=-1)
    x = x + _L0_attn_ref(xn, L0_attn_Wq, L0_attn_bq, L0_attn_Wk, L0_attn_bk, L0_attn_Wv, L0_attn_bv, L0_attn_Wo, L0_attn_bo) + _L0_ffn_ref(xn, L0_ffn_ln1_w, L0_ffn_ln2_w, L0_ffn_Wq, L0_ffn_bq, L0_ffn_Wk, L0_ffn_bk, L0_ffn_Wv, L0_ffn_bv, L0_ffn_qn_w, L0_ffn_kn_w, L0_ffn_Wg, L0_ffn_bg, L0_ffn_Wo, L0_ffn_bo, L0_ffn_Wr, L0_ffn_br, L0_ffn_W1, L0_ffn_b1, L0_ffn_W2, L0_ffn_b2)
    xn = _layernorm(x, axis=-1)
    x = x + _L1_attn_ref(xn, L1_attn_norm_w, L1_attn_in_proj_w, L1_attn_conv_w, L1_attn_conv_b, L1_attn_A_log, L1_attn_D, L1_attn_dt_bias, L1_attn_out_proj_w) + _L1_ffn_ref(xn, L1_ffn_w1_w, L1_ffn_w1_s, L1_ffn_w2_w, L1_ffn_w2_s, L1_ffn_h1_w, L1_ffn_h1_s, L1_ffn_h2_w, L1_ffn_h2_s, L1_ffn_w3_w, L1_ffn_w3_s)
    return x

_drawn_inputs = setup_inputs


def setup_inputs(seed=0):
    import zlib

    import numpy as np

    out = dict(_drawn_inputs(seed))
    spreads = {'L0_ffn_ln1_w': (1.0, 0.2),
     'L0_ffn_ln2_w': (1.0, 0.2),
     'L0_ffn_bq': (0.0, 0.1),
     'L0_ffn_bk': (0.0, 0.1),
     'L0_ffn_bv': (0.0, 0.1),
     'L0_ffn_qn_w': (1.0, 0.2),
     'L0_ffn_kn_w': (1.0, 0.2),
     'L0_ffn_bg': (0.0, 0.1),
     'L0_ffn_bo': (0.0, 0.1),
     'L0_ffn_br': (0.0, 0.1),
     'L0_ffn_b1': (0.0, 0.1),
     'L0_ffn_b2': (0.0, 0.1),
     'L1_attn_norm_w': (1.0, 0.2),
     'L1_attn_conv_b': (0.0, 0.1),
     'L1_attn_D': (1.0, 0.2)}
    factors = {}
    for name, (base, spread) in spreads.items():
        noise = np.random.default_rng([zlib.crc32(name.encode()), seed]).standard_normal(out[name].shape)
        drawn = base * np.exp(spread * noise) if base else spread * noise
        out[name] = jnp.asarray(drawn.astype(out[name].dtype))
    for name, factor in factors.items():
        out[name] = (out[name] * factor).astype(out[name].dtype)
    return out
```

```python
from contextlib import ExitStack

import numpy as np

import concourse.bass as bass
import concourse.mybir as mybir

F32 = mybir.dt.float32
BF16 = mybir.dt.bfloat16
ALU = mybir.AluOpType
ACT = mybir.ActivationFunctionType
X_AXIS = mybir.AxisListType.X

P = 128
T = 2048
D = 128
NT = T // P
TB = 512
NB = T // TB
TPB = TB // P

HEADS, HD = 16, 64
NC = 32
CHUNK = 64
HC = HEADS * HD // P

NQ, NKV, QD = 16, 4, 8
REP = NQ // NKV
QKV_W = NQ * QD + 2 * NKV * QD
NSPLIT = 3
KV_W = NKV * QD

E, HID = 8, 256
FC = HID // P

DI, NH, PD = 256, 4, 64
KW = 4
MI = DI // P

FH = 512
FO = FH // P

LN_EPS, RMS_EPS = 1e-5, 1e-6
BIG = 1e30


class Steps:

    def __init__(self, eng, sem):
        self.eng, self.sem, self.n = eng, sem, 0

    def mark(self, instruction):
        instruction.then_inc(self.sem, 1)
        self.n += 1
        return self.n

    def settle(self):
        self.eng.wait_ge(self.sem, self.n)

    def alone(self, instruction):
        self.mark(instruction)
        self.settle()


def over(ap, n):
    return ap.unsqueeze(len(ap.shape)).broadcast_to(list(ap.shape) + [n])


def along(ap, n):
    return ap.unsqueeze(1).broadcast_to([ap.shape[0], n] + list(ap.shape[1:]))


def build(nc, io, out):
    ctx = ExitStack()
    with ctx:
        def sb(name, cols, dt=F32, rows=P):
            return ctx.enter_context(nc.sbuf_tensor(name, [rows, cols], dt))

        def sem(name):
            return ctx.enter_context(nc.semaphore(name))

        res = sb("res", NT * D)[:, :].rearrange("p (i d) -> p i d", i=NT)
        xn = sb("xn", NT * D)[:, :].rearrange("p (i d) -> p i d", i=NT)
        xnT = sb("xnT", T)[:, :]
        consts = sb("consts", 2 * P + 2 * NT * 4)
        ident = consts[:, 0:P]
        tri = consts[:, P:2 * P]
        cosT = consts[:, 2 * P:2 * P + 4 * NT].rearrange("p (i f) -> p i f", i=NT)
        sinT = consts[:, 2 * P + 4 * NT:].rearrange("p (i f) -> p i f", i=NT)
        identb = sb("identb", P, BF16)[:, :]
        small = sb("small", 512)
        stats = sb("stats", NT * 6)[:, :].rearrange("p (i s) -> p i s", i=NT)
        mv = small[:, 0:32].rearrange("p (i s) -> p i s", i=NT)
        sd, rstd, ms, sd2, hs = (small[:, 32 + 16 * k:48 + 16 * k] for k in range(5))
        bo_bc = small[:, 128:256]
        bo0_bc = small[:, 256:384]
        w3s_bc = small[:, 384:512]
        row = sb("row", 1024)
        bqkv = row[:, 0:QKV_W]
        qn_bc, kn_bc = row[:, 192:200], row[:, 200:208]
        kw = row[:, 208:216]
        shift = row[:, 216:217]
        mx2 = row[:, 217:219]
        ln1 = row[:, 220:221]
        ln2 = row[:, 221:222]
        bgc = row[:, 222:223]
        br_bc = row[:, 224:232]
        rank = row[:, 232:240]
        b1c = row[:, 240:272].rearrange("p (e k) -> p e k", e=E)
        wr = row[:, 272:280]
        normw = row[:, 280:281]
        convw = row[:, 284:292].rearrange("p (m k) -> p m k", m=MI)
        convb = row[:, 292:294]
        d2 = row[:, 294:296]
        dtb = row[:, 296:300]
        alog = row[:, 300:304]
        w1s, w2s = row[:, 304:308], row[:, 308:312]
        h1s, h2s = row[:, 312:316], row[:, 316:320]
        zero = row[:, 320:321]
        wg = row[:, 384:512]
        wo = row[:, 512:640]
        b2 = row[0:E, 640:768]
        oneEf = row[0:E, 768:896]
        w1sh = row[:, 896:900]
        s12 = row[:, 900:904]

        r1 = sb("r1", 14400)
        r2 = sb("r2", 20480)
        r3 = sb("r3", 10080)

        qkv = r1[:, 0:3072].rearrange("p (i c) -> p i c", i=NT)
        rot = r1[:, 3072:5632].rearrange("p (i h d) -> p i h d", i=NT, d=QD)
        rotf = r1[:, 3072:5632].rearrange("p (i c) -> p i c", i=NT)
        rot_a = r1[:, 5632:6912].rearrange("p (i h d) -> p i h d", i=NT, d=4)
        rot_b = r1[:, 6912:8192].rearrange("p (i h d) -> p i h d", i=NT, d=4)
        sq = r1[:, 5632:8192].rearrange("p (i h d) -> p i h d", i=NT, d=QD)
        qs = r1[:, 5632:8704].bitcast(BF16).rearrange("p (i s c) -> p i s c", i=NT, s=NSPLIT)
        ks = r1[:, 8704:9472].bitcast(BF16).rearrange("p (i s c) -> p i s c", i=NT, s=NSPLIT)
        qT = r1[:, 0:3072].bitcast(BF16).rearrange("p (s t) -> p s t", s=NSPLIT)
        kT = r1[:, 9472:10496].bitcast(BF16)
        ssq = r1[:, 10496:10816]
        rr = r1[:, 10816:11136]
        wqkv = r1[:, 11136:11328]
        probs = r1[:, 0:6144].rearrange("p (b h t) -> p b h t", b=6, h=2)
        outT = r1[:, 6144:14336].rearrange("p (n t) -> p n t", n=NKV * NB)
        qst = r2[:, 0:16384].bitcast(BF16).rearrange("p (h t) -> p h t", h=NQ)
        kst = r2[:, 16384:20480].bitcast(BF16).rearrange("p (g t) -> p g t", g=NKV)
        vp = r3[:, 0:2048].rearrange("p (i g m) -> p i g m", i=NT, g=NKV)
        wqT = r1[:, 12416:13440].rearrange("p (j d) -> p j d", j=HC)
        kbd = r1[:, 13440:13952].rearrange("p (j a c) -> p j a c", j=HC, a=2)
        kvb = r1[:, 13952:14208].rearrange("p (j c) -> p j c", j=HC)
        s0 = 2048
        wk0 = r3[:, s0:s0 + 1024]
        wv0 = r3[:, s0 + 1024:s0 + 2048]
        wo0 = r3[:, s0 + 2048:s0 + 3072].rearrange("p (j d) -> p j d", j=HC)
        vbd = r3[:, s0 + 3072:s0 + 3584].rearrange("p (j a c) -> p j a c", j=HC, a=2)
        gmat = r3[:, s0 + 3584:s0 + 4096].rearrange("p (h c) -> p h c", h=HEADS)
        g0 = r3[:, s0 + 4096:s0 + 4608].rearrange("p (h c) -> p h c", h=HEADS)
        vw = r3[:, s0 + 4608:s0 + 5120].rearrange("p (q d) -> p q d", q=4)
        sc = r3[:, s0 + 5120:s0 + 6144].rearrange("p (b h c) -> p b h c", b=2, h=HEADS)
        pr = r3[:, s0 + 6144:s0 + 7168].rearrange("p (b n) -> p b n", b=2)
        s1 = s0 + 7168
        summT = r3[:, s1:s1 + NC]
        bq0 = r3[:, s1 + 32:s1 + 40]
        bk0 = r3[:, s1 + 40:s1 + 48]
        bv0 = r3[:, s1 + 48:s1 + 56]
        smx = r3[:, s1 + 64:s1 + 96].rearrange("p (b h) -> p b h", b=2)
        ssm_ = r3[:, s1 + 96:s1 + 128].rearrange("p (b h) -> p b h", b=2)
        ptr = r1[:, 11392:12416].rearrange("p (b n) -> p b n", b=2)

        vc = r3[:, 9344:9856].rearrange("p (i m) -> p i m", i=NT)

        att = r2[:, 0:2048].rearrange("p (i c) -> p i c", i=NT)
        oT = r2[:, 2048:4096]
        gate = r2[:, 4096:6144]
        sqm = r2[:, 6144:8192].rearrange("p (i d) -> p i d", i=NT)
        h2 = r2[:, 8192:10240].rearrange("p (i d) -> p i d", i=NT)
        w1 = r1[:, 0:4096].rearrange("p (e f) -> p e f", e=E)
        w2 = r1[:, 4096:6144].rearrange("p (e c d) -> p e c d", e=E, c=FC)
        h2T = r3[:, 2048:4096]
        m0 = 4096
        rden = r3[:, m0:m0 + 32].rearrange("p (b n) -> p b n", b=2)
        ssq2, sdm, hs2 = (r3[:, m0 + 32 + 16 * k:m0 + 48 + 16 * k] for k in range(3))
        lg, eq, rk, oh = (r3[:, m0 + 128 + 128 * k:m0 + 256 + 128 * k].rearrange("p (i e) -> p i e", e=E)
                          for k in range(4))
        lmx = r3[:, m0 + 96:m0 + 112]
        lmx2 = r3[:, m0 + 112:m0 + 128]
        ohT = r3[0:E, m0 + 640:m0 + 640 + T]
        pen = r3[0:E, m0 + 640 + T:m0 + 640 + T + T // 2].bitcast(BF16)
        onee = r3[0:E, m0 + 640 + T + T // 2:m0 + 640 + T + T // 2 + 512].bitcast(BF16).rearrange(
            "p (e m) -> p e m", e=E)
        sg = r2[:, 10240:11776].rearrange("p (b t) -> p b t", b=3)
        am = r2[:, 11776:13312].rearrange("p (b t) -> p b t", b=3)
        yT = r2[:, 13312:13824]

        inp = r2[:, 0:772]
        owT = r2[:, 772:1028].rearrange("p (m d) -> p m d", m=MI)
        f1 = r2[:, 1028:1540]
        f2 = r2[:, 1540:2052]
        fh1 = r2[:, 2052:4100].rearrange("p (k o) -> p k o", k=FO)
        fh2 = r2[:, 4100:6148].rearrange("p (k o) -> p k o", k=FO)
        f3 = r2[:, 6148:6660].rearrange("p (k d) -> p k d", k=FO)
        fa = r2[:, 6660:8708].rearrange("p (k t) -> p k t", k=FO)
        fb = r2[:, 8708:10756].rearrange("p (k t) -> p k t", k=FO)
        fth = r2[:, 10756:11780].rearrange("p (b t) -> p b t", b=2)
        fst = r2[:, 11780:12292].rearrange("p (i d) -> p i d", i=TPB)
        xsT = r2[:, 12292:14340]
        xs = r2[:, 14340:16388].rearrange("p (i d) -> p i d", i=NT)
        btd = r2[:, 16388:18500].rearrange("p (i c) -> p i c", i=NT)
        z2 = r1[:, 0:4096].rearrange("p (m t) -> p m t", m=MI)
        xp = r1[:, 4096:8200].rearrange("p (m t) -> p m t", m=MI)
        xc = r1[:, 8200:12296].rearrange("p (m t) -> p m t", m=MI)
        CT = r1[:, 12296:14344]
        BT = r3[:, 0:2048]
        k0 = 2048
        dt, av, cums, du, dl = (r3[:, k0 + 64 * k:k0 + 64 * k + 64].rearrange("p (i h) -> p i h", i=NT)
                                for k in range(5))
        ea = r3[:, k0 + 320:k0 + 324]
        th = r3[:, k0 + 512:k0 + 1536].rearrange("p (b t) -> p b t", b=2)
        c0 = k0 + 1536
        thc = r3[:, c0 + 256:c0 + 1280].rearrange("p (m t) -> p m t", m=MI)
        ft1 = r2[:, 18500:19524].rearrange("p (b t) -> p b t", b=2)
        gm = r3[:, c0:c0 + 256].rearrange("p (b t) -> p b t", b=2)
        ed = r3[:, c0 + 256:c0 + 1280].rearrange("p (b h t) -> p b h t", b=2, h=NH)
        ec = r3[:, c0 + 1280:c0 + 2304].rearrange("p (b h t) -> p b h t", b=2, h=NH)
        mm = r3[:, c0 + 2304:c0 + 3328].rearrange("p (b h t) -> p b h t", b=2, h=NH)
        cs = r3[:, c0 + 3328:c0 + 4352].rearrange("p (b h t) -> p b h t", b=2, h=NH)
        dtx = r3[:, c0 + 4352:c0 + 4864].rearrange("p (b h d) -> p b h d", b=2, h=NH)
        dtw = r3[:, c0 + 4864:c0 + 5376].rearrange("p (b h d) -> p b h d", b=2, h=NH)
        hst = r3[:, c0 + 5376:c0 + 5632].rearrange("p (h d) -> p h d", h=NH)
        yg = r3[:, c0 + 5632:c0 + 6144].rearrange("p (b m t) -> p b m t", b=2, m=MI)

        ps = ctx.enter_context(nc.psum_tensor("ps", [P, 8, 512], F32))
        qd_dram = nc.dram_tensor("q_split_rows", (NSPLIT, P, T), BF16, kind="Internal").ap()
        kd_dram = nc.dram_tensor("k_split_rows", (NSPLIT * KV_W, T), BF16, kind="Internal").ap()

        s_x = [sem(f"x_loaded{i}") for i in range(4)]
        s_const = sem("consts_loaded")
        s_wqkv = sem("qkv_weights_loaded")
        s_w0 = sem("summary_weights_loaded")
        s_wrest = sem("gate_router_weights_loaded")
        s_v = sem("dve_steps")
        s_a = sem("act_steps")
        s_g = sem("pool_steps")
        s_var = sem("variance_ready")
        s_sd = sem("root_ready")
        s_xn = sem("xn_ready")
        s_xnT = sem("xn_transposed")
        s_xnTc = sem("xnT_copied")
        s_wsc = sem("qkv_weights_scaled")
        s_qkvp = sem("qkv_projected")
        s_qkvc = sem("qkv_copied")
        s_rot = sem("rotated")
        s_sq = sem("squared")
        s_ssq = sem("square_sums")
        s_qksd = sem("qk_root")
        s_split = sem("splits_ready")
        s_splT = sem("splits_transposed")
        s_splTa = sem("splits_copied_by_act")
        s_splTv = sem("splits_copied_by_dve")
        s_scr = sem("splits_in_dram")
        s_qst = sem("stacks_loaded")
        s_pad = sem("stack_pads_zeroed")
        s_vp = sem("values_ready")
        s_idb = sem("bf16_identity")

        s_summ = sem("chunk_means_ready")
        s_kv = sem("summary_kv_projected")
        s_kbd = sem("summary_kv_placed")
        s_gw = sem("summary_products_ready")
        s_gc = sem("summary_products_copied")
        s_s = sem("summary_scores")
        s_sadd = sem("summary_scores_copied")
        s_sub = sem("summary_shifted")
        s_ex = sem("summary_exponentials")
        s_pr = sem("summary_probabilities")
        s_pt = sem("summary_probs_transposed")
        s_ptc = sem("summary_probs_copied")
        s_o = sem("summary_outputs")
        s_a0 = sem("summary_added")
        s_qk = sem("score_pairs")
        s_exp = sem("exponentials")
        s_msk = sem("diagonals_masked")
        s_pv = sem("value_products")
        s_vc = sem("group_values_copied")
        s_accc = sem("attention_block_copied")
        s_oT = sem("attention_token_major")
        s_att = sem("attention_normalised")
        s_aT = sem("attention_transposed")
        s_aTc = sem("attention_T_copied")
        s_gp = sem("gate_projected")
        s_gt = sem("gate_ready")
        s_og = sem("gated")
        s_wo = sem("output_projected")
        s_xm = sem("x_mid_ready")
        s_sq2 = sem("x_mid_squared")
        s_ss2 = sem("x_mid_square_sums")
        s_sd2 = sem("x_mid_root")
        s_h2 = sem("h2_ready")
        s_h2T = sem("h2_transposed")
        s_h2Tc = sem("h2T_copied")
        s_lg = sem("router_logits")
        s_oh = sem("one_hot_ready")
        s_ohT = sem("one_hot_transposed")
        s_pen = sem("penalty_ready")
        s_moew = sem("expert_weights_loaded")
        s_up = sem("expert_up_products")
        s_sg = sem("expert_sigmoids")
        s_moea = sem("expert_activations")
        s_dn = sem("expert_down_products")
        s_yc = sem("expert_sums_copied")
        s_yt = sem("expert_sums_token_major")
        s_ya = sem("expert_sums_added")
        s_l1w = sem("layer1_weights_loaded")
        s_var2 = sem("variance2_ready")
        s_sdl = sem("root2_ready")
        s_xn2 = sem("xn1_ready")
        s_xs = sem("xs_ready")
        s_xn2T = sem("xn1_transposed")
        s_xn2c = sem("xn1_T_copied")
        s_inp = sem("in_proj_scaled")
        s_pj = sem("ssm_projected")
        s_pja = sem("ssm_projections_read_by_act")
        s_pjv = sem("ssm_projections_read_by_dve")
        s_bt = sem("ssm_token_projected")
        s_btc = sem("ssm_token_copied")
        s_xcv = sem("convolved")
        s_xth = sem("convolution_tanh")
        s_dta = sem("dt_for_act")
        s_dtb = sem("dt_from_act")
        s_av = sem("decay_rates_ready")
        s_cum = sem("cumulative_decay")
        s_cumc = sem("cumulative_decay_copied")
        s_c1 = sem("chunk_products")
        s_cd = sem("chunk_decay_difference")
        s_ce = sem("chunk_exponentials")
        s_cm = sem("chunk_operands_from_pool")
        s_cx = sem("chunk_operands_from_dve")
        s_cy = sem("chunk_outputs")
        s_cg = sem("chunk_gated")
        s_ch = sem("chunk_state_ready")
        s_co = sem("chunk_projected")
        s_ca = sem("chunk_added")
        s_fu = sem("ffn_up_products")
        s_ft = sem("ffn_tanh")
        s_fs = sem("ffn_scales_ready")
        s_fm = sem("ffn_silu_products")
        s_fg = sem("ffn_gated")
        s_f2 = sem("ffn_second_products")
        s_fg2 = sem("ffn_second_gelu")
        s_f3 = sem("ffn_third_products")
        s_fg3 = sem("ffn_third_gelu")
        s_f4 = sem("ffn_down_products")
        s_fr = sem("ffn_scaled")
        s_fin = sem("result_ready")
        s_zth = sem("z_tanh")
        s_xc = sem("convolution_silu")
        s_cst = sem("chunk_state_products")
        s_out = sem("result_stored")

        BLOCKS = [(qb, kt, max(0, kt - TPB * qb) * P) for qb in range(NB) for kt in range(TPB * qb + TPB)]
        KB = len(BLOCKS)
        PAIRS = 2 * KB
        SBUFS, PBUFS = 3, 6
        DIAG = [k for k, (qb, kt, _) in enumerate(BLOCKS) if kt >= TPB * qb]

        res_flat = res.rearrange("p i d -> p (i d)")

        def last_user(n, bufs, total):
            return max(m for m in range(total) if m % bufs == n % bufs)

        block = ctx.enter_context(nc.Block())

        @block.sync
        def _(sp):
            for q in range(4):
                sp.dma_start(res[:, 4 * q:4 * q + 4, :],
                             io["x"][512 * q:512 * q + 512, :].rearrange("(i p) d -> p i d", p=P)
                             ).then_inc(s_x[q], 16)
            sp.dma_start(consts[:, :], io["consts"]).then_inc(s_const, 16)
            for c, (w, n) in enumerate((("f_Wq", 128), ("f_Wk", 32), ("f_Wv", 32))):
                sp.dma_start(wqkv[:, [0, 128, 160][c]:[0, 128, 160][c] + n], io[w]).then_inc(s_wqkv, 16)
            for c, (w, n) in enumerate((("f_bq", 128), ("f_bk", 32), ("f_bv", 32))):
                sp.dma_start(bqkv[:, [0, 128, 160][c]:[0, 128, 160][c] + n],
                             io[w].broadcast_to([P, n])).then_inc(s_wqkv, 16)
            sp.dma_start(qn_bc, io["f_qn"].broadcast_to([P, QD])).then_inc(s_wqkv, 16)
            sp.dma_start(kn_bc, io["f_kn"].broadcast_to([P, QD])).then_inc(s_wqkv, 16)
            sp.dma_start(ln1, io["f_ln1"]).then_inc(s_wqkv, 16)
            sp.dma_start(wqT, io["a_WqT"].rearrange("(j p) d -> p j d", p=P)).then_inc(s_w0, 16)
            sp.dma_start(wk0, io["a_Wk"]).then_inc(s_w0, 16)
            sp.dma_start(wv0, io["a_Wv"]).then_inc(s_w0, 16)
            sp.dma_start(wo0, io["a_Wo"].rearrange("(j p) d -> p j d", p=P)).then_inc(s_w0, 16)
            for dst, name in ((bq0, "a_bq"), (bk0, "a_bk"), (bv0, "a_bv")):
                sp.dma_start(dst, io[name]).then_inc(s_w0, 16)
            sp.dma_start(bo0_bc, io["a_bo"].broadcast_to([P, D])).then_inc(s_w0, 16)
            for s in range(NSPLIT):
                sp.wait_ge(s_splTa, s + 1)
                sp.wait_ge(s_splTv, s + 1)
                sp.dma_start(qd_dram[s], qT[:, s, :]).then_inc(s_scr, 16)
            sp.wait_ge(s_splTa, 4)
            sp.wait_ge(s_splTv, 4)
            sp.dma_start(kd_dram, kT[0:NSPLIT * KV_W, :]).then_inc(s_scr, 16)
            sp.wait_ge(s_scr, 64)
            sp.wait_ge(s_pad, 1)
            for i in range(NSPLIT):
                for j in range(NSPLIT):
                    r = 24 * i + 8 * j
                    sp.dma_start(kst[r:r + 8, :, :],
                                 kd_dram[KV_W * j:KV_W * j + KV_W, :].rearrange("(g d) t -> d g t", d=QD)
                                 ).then_inc(s_qst, 16)
            for g in range(NKV):
                for i in range(NSPLIT):
                    for j in range(NSPLIT):
                        r = 24 * i + 8 * j
                        sp.dma_start(qst[r:r + 8, REP * g:REP * g + REP, :],
                                     qd_dram[i, 32 * g:32 * g + 32, :].rearrange("(h d) t -> d h t", d=QD)
                                     ).then_inc(s_qst, 16)
            sp.wait_ge(s_pad, 2)
            for h in range(NQ):
                sp.dma_start(wg[QD * h:QD * h + QD, QD * h:QD * h + QD], io["f_Wg"]).then_inc(s_wrest, 16)
            for dst, name in ((wo, "f_Wo"), (wr, "f_Wr"), (ln2, "f_ln2"), (b2, "f_b2"), (row[:, 240:272], "f_b1c"),
                              (bgc, "f_bgc")):
                sp.dma_start(dst, io[name]).then_inc(s_wrest, 16)
            for dst, name, n in ((bo_bc, "f_bo", D), (br_bc, "f_br", E), (rank, "rank", E)):
                sp.dma_start(dst, io[name].broadcast_to([P, n])).then_inc(s_wrest, 16)
            sp.wait_ge(s_oT, 16)
            sp.dma_start(w1, io["f_W1"].rearrange("e p f -> p e f")).then_inc(s_moew, 16)
            sp.dma_start(w2, io["f_W2"].rearrange("e (c p) d -> p e c d", p=P)).then_inc(s_moew, 16)
            sp.wait_ge(s_h2Tc, NB)
            for dst, name in ((inp, "s_inT"), (f1, "g_w1T"), (f2, "g_w2T"),
                              (normw, "s_norm"), (convb, "s_convb"), (d2, "s_D"), (row[:, 284:292], "s_convw"),
                              (w1s, "g_w1s"), (w2s, "g_w2s"), (h1s, "g_h1s"), (h2s, "g_h2s")):
                sp.dma_start(dst, io[name]).then_inc(s_l1w, 16)
            sp.dma_start(owT, io["s_outT"].rearrange("(m p) d -> p m d", p=P)).then_inc(s_l1w, 16)
            for dst, name in ((fh1, "g_h1T"), (fh2, "g_h2T"), (f3, "g_w3T")):
                sp.dma_start(dst, io[name].rearrange("(k p) o -> p k o", p=P)).then_inc(s_l1w, 16)
            for dst, name, n in ((dtb, "s_dtb", NH), (alog, "s_Alog", NH), (w3s_bc, "g_w3s", D)):
                sp.dma_start(dst, io[name].broadcast_to([P, n])).then_inc(s_l1w, 16)
            for b in range(NB):
                sp.wait_ge(s_fin, b + 1)
                sp.dma_start(out[TB * b:TB * b + TB, :].rearrange("(i p) d -> p i d", p=P),
                             res[:, TPB * b:TPB * b + TPB, :]).then_inc(s_out, 16)
            sp.wait_ge(s_out, 16 * NB)

        @block.gpsimd
        def _(pool):
            step = Steps(pool, s_g)
            pool.memset(r2[64:P, :], 0.0).then_inc(s_pad, 1)
            pool.wait_ge(s_pad, 1)
            step.alone(pool.memset(vp[:, :, :, :], 0.0))
            pool.memset(vp[:, :, :, QD:QD + 1], 1.0).then_inc(s_vp, 1)
            step.alone(pool.memset(kbd[:, :, :, :], 0.0))
            step.alone(pool.memset(vbd[:, :, :, :], 0.0))
            pool.memset(wg, 0.0).then_inc(s_pad, 1)
            pool.memset(pr[:, :, :], 0.0).then_inc(s_pad, 1)
            pool.wait_ge(s_vp, 2)
            pool.sem_inc(s_pv, KB)
            vp_flat = r3[:, 0:2048].rearrange("p (i c) -> p i c", i=NT)
            with pool.Fori(0, NKV) as g:
                pool.wait_ge(s_pv, g * KB + KB)
                pool.tensor_copy(vc, vp_flat[:, :, bass.ds(g * 32, 32)]).then_inc(s_vc, 1)
                for k in DIAG:
                    off = BLOCKS[k][2]
                    for n in (2 * k, 2 * k + 1):
                        pool.wait_ge(s_exp, g * PAIRS + (PAIRS + n + 1))
                        blk = probs[:, n % PBUFS, :, off:off + P]
                        pool.tensor_tensor(blk, blk, along(tri, 2), ALU.mult).then_inc(s_msk, 1)
            pool.wait_ge(s_a0, NT)
            step.alone(pool.memset(onee, 1.0))
            pool.affine_select(out=onee, in_=onee, compare_op=ALU.is_equal, fill=0.0, base=0,
                               pattern=[[-1, E], [0, P]], channel_multiplier=1).then_inc(s_idb, 1)
            pool.wait_ge(s_ya, NB + 1)
            pool.memset(xp[:, :, 0:KW - 1], 0.0).then_inc(s_pad, 1)
            pool.wait_ge(s_pad, 4)
            pool.memset(hst, 0.0).then_inc(s_ch, 1)
            pool.wait_ge(s_pja, 3 * NB)
            for c in range(NT):
                b = c % 2
                if c >= 2:
                    pool.wait_ge(s_cy, c - 1)
                pool.wait_ge(s_ce, 2 * c + 1)
                pool.wait_ge(s_cx, 2 * c + 1)
                pool.tensor_tensor(mm[:, b], ed[:, b], along(gm[:, b, :], NH), ALU.mult).then_inc(s_cm, 1)
                pool.wait_ge(s_ce, 2 * c + 2)
                pool.tensor_tensor(cs[:, b], ec[:, b], along(CT[:, c * P:c * P + P], NH), ALU.mult
                                   ).then_inc(s_cm, 1)

        @block.scalar
        def _(act):
            step = Steps(act, s_a)
            act.wait_ge(s_var, 1)
            act.activation(sd, mv[:, :, 1], ACT.Sqrt, bias=LN_EPS).then_inc(s_sd, 1)
            act.wait_ge(s_var, 2)
            act.activation(sd2, ms, ACT.Sqrt, bias=RMS_EPS).then_inc(s_sd, 1)
            for b in range(NB):
                act.wait_ge(s_xnT, b + 1)
                act.activation(xnT[:, b * TB:b * TB + TB], ps[:, b, :], ACT.Copy).then_inc(s_xnTc, 1)
            act.wait_ge(s_rot, 1)
            act.activation(sq, rot, ACT.Square).then_inc(s_sq, 1)
            act.wait_ge(s_ssq, 1)
            act.activation(rr, ssq, ACT.Sqrt, bias=RMS_EPS, scale=1.0 / QD).then_inc(s_qksd, 1)
            for n in range(0, 8, 2):
                act.wait_ge(s_splT, n + 1)
                src = ps[:, n, :].bitcast(BF16)
                if n < 6:
                    act.activation(qT[:, n // 2, 0:1024], src, ACT.Copy).then_inc(s_splTa, 1)
                else:
                    act.activation(kT[0:96, 0:1024], src[0:96, :], ACT.Copy).then_inc(s_splTa, 1)
            act.wait_ge(s_gw, 1)
            act.activation(gmat, ps[:, 1, :].rearrange("p (h c) -> p h c", h=HEADS), ACT.Copy).then_inc(s_gc, 1)
            act.activation(g0, ps[:, 2, :].rearrange("p (h c) -> p h c", h=HEADS), ACT.Copy).then_inc(s_gc, 1)
            act.activation(vw, ps[:, 3, :].rearrange("p (q d) -> p q d", q=4), ACT.Copy).then_inc(s_gc, 1)
            for i in range(NT + 1):
                if i < NT:
                    act.wait_ge(s_sub, i + 1)
                    blk = sc[:, i % 2, :, 0:2 * i + 2]
                    act.activation(blk, blk, ACT.Exp).then_inc(s_ex, 1)
                if i >= 1:
                    act.wait_ge(s_pt, i)
                    if i >= 3:
                        act.wait_ge(s_o, i - 2)
                    act.activation(ptr[:, (i - 1) % 2, :], ps[:, 6 + (i - 1) % 2, :], ACT.Copy
                                   ).then_inc(s_ptc, 1)
            act.sem_inc(s_exp, PAIRS)
            with act.Fori(0, NKV) as g:
                for k, (qb, kt, off) in enumerate(BLOCKS):
                    for n in (2 * k, 2 * k + 1):
                        act.wait_ge(s_qk, g * PAIRS + (n + 1))
                        free = KB + (n - PBUFS) // 2 + 1 if n >= PBUFS else last_user(n, PBUFS, PAIRS) // 2 + 1
                        act.wait_ge(s_pv, g * KB + free)
                        b = 2 * (n % SBUFS)
                        act.activation(probs[:, n % PBUFS, :, off:TB], ps[:, b:b + 2, off:TB], ACT.Exp,
                                       bias=shift).then_inc(s_exp, 1)
            for b in range(NB):
                act.wait_ge(s_aT, b + 1)
                act.activation(oT[:, b * TB:b * TB + TB], ps[:, 4 + b, :], ACT.Copy).then_inc(s_aTc, 1)
            act.wait_ge(s_wrest, 16 * 25)
            for b in range(NB):
                act.wait_ge(s_gp, b + 1)
                act.activation(gate[:, b * TB:b * TB + TB], ps[:, b, :], ACT.Sigmoid, bias=bgc).then_inc(s_gt, 1)
            for b in range(NB):
                act.wait_ge(s_xm, b + 1)
                act.activation(sqm[:, TPB * b:TPB * b + TPB, :], xn[:, TPB * b:TPB * b + TPB, :], ACT.Square
                               ).then_inc(s_sq2, 1)
            act.wait_ge(s_ss2, NB)
            act.activation(sdm, ssq2, ACT.Sqrt, bias=RMS_EPS, scale=1.0 / D).then_inc(s_sd2, 1)
            for b in range(NB):
                act.wait_ge(s_h2T, b + 1)
                act.activation(h2T[:, b * TB:b * TB + TB], ps[:, b, :], ACT.Copy, scale=ln2).then_inc(s_h2Tc, 1)
            act.sem_inc(s_yc, 1)
            with act.Fori(0, NB) as tb:
                for n in range(E * FC):
                    e, c = divmod(n, FC)
                    act.wait_ge(s_up, tb * (E * FC) + (n + 1))
                    free = E * FC + n - 2 if n >= 3 else last_user(n, 3, E * FC) + 1
                    act.wait_ge(s_moea, tb * (E * FC) + free)
                    act.activation(sg[:, n % 3, :], ps[:, 2 * (n % 3) + 1, :], ACT.Sigmoid,
                                   bias=b1c[:, e, FC + c:FC + c + 1]).then_inc(s_sg, 1)
                act.wait_ge(s_dn, tb * (E * FC) + 2 * E * FC)
                act.wait_ge(s_yt, tb + 1)
                act.activation(yT, ps[:, 6, :], ACT.Copy).then_inc(s_yc, 1)
            act.wait_ge(s_var2, 1)
            act.activation(sd, mv[:, :, 1], ACT.Sqrt, bias=LN_EPS).then_inc(s_sdl, 1)
            act.wait_ge(s_var2, 2)
            act.activation(sd2, ms, ACT.Sqrt, bias=RMS_EPS).then_inc(s_sdl, 1)
            for b in range(2 * NB):
                act.wait_ge(s_xn2T, b + 1)
                dst = xnT if b < NB else xsT
                act.activation(dst[:, b % NB * TB:b % NB * TB + TB], ps[:, b, :], ACT.Copy).then_inc(s_xn2c, 1)
            for b in range(NB):
                toks = slice(b * TB, b * TB + TB)
                for k in range(5):
                    u = 6 * b + k
                    act.wait_ge(s_pj, u + 1)
                    if k < 2:
                        if b >= 1:
                            act.wait_ge(s_pjv, 3 * (b - 1) + k + 1)
                        act.activation(th[:, k, :], ps[:, u % 8, :], ACT.Tanh, scale=0.5).then_inc(s_zth, 1)
                    else:
                        dst = xp[:, k - 2, KW - 1 + b * TB:KW - 1 + b * TB + TB] if k < 4 else CT[:, toks]
                        act.activation(dst, ps[:, u % 8, :], ACT.Copy).then_inc(s_pja, 1)
            for b in range(NB):
                act.wait_ge(s_xcv, b + 1)
                if b >= 1:
                    act.wait_ge(s_xc, b)
                act.activation(thc, xc[:, :, b * TB:b * TB + TB], ACT.Tanh, scale=0.5).then_inc(s_xth, 1)
            act.wait_ge(s_dta, 1)
            act.activation(ea, alog, ACT.Exp).then_inc(s_dtb, 1)
            act.activation(dl, dl, ACT.Exp).then_inc(s_dtb, 1)
            act.wait_ge(s_dtb, 2)
            act.activation(dl, dl, ACT.Ln, bias=1.0).then_inc(s_dtb, 1)
            for c in range(NT):
                b = c % 2
                act.wait_ge(s_cd, c + 1)
                act.activation(ed[:, b], ed[:, b], ACT.Exp).then_inc(s_ce, 1)
                act.wait_ge(s_c1, c + 1)
                if c >= 2:
                    act.wait_ge(s_cm, 2 * (c - 2) + 2)
                    act.wait_ge(s_ch, c)
                act.activation(ec[:, b], ps[:, 2 + b, :].rearrange("p (h t) -> p h t", h=NH), ACT.Exp
                               ).then_inc(s_ce, 1)
            act.sem_inc(s_fg3, FO)
            with act.Fori(0, NB) as blk_i:
                for o in range(FO):
                    act.wait_ge(s_fu, blk_i * FO + (o + 1))
                    free = FO + o - 1 if o >= 2 else FO - 1 + o
                    act.wait_ge(s_fm, blk_i * FO + free)
                    act.activation(fth[:, o % 2, :], ps[:, 2 * o, :], ACT.Tanh, scale=w1sh[:, o:o + 1]
                                   ).then_inc(s_ft, 1)
                for o in range(FO):
                    act.wait_ge(s_f2, blk_i * FO + (FO + o + 1))
                    act.wait_ge(s_f3, blk_i * FO + FO)
                    act.activation(fb[:, o, :], ps[:, o, :], ACT.Gelu, scale=h1s[:, o:o + 1]).then_inc(s_fg2, 1)
                for o in range(FO):
                    act.wait_ge(s_f3, blk_i * FO + (FO + o + 1))
                    act.activation(fa[:, o, :], ps[:, FO + o, :], ACT.Gelu, scale=h2s[:, o:o + 1]
                                   ).then_inc(s_fg3, 1)

        @block.tensor
        def _(pe):
            pe.wait_ge(s_const, 16)
            for b in range(NB):
                for i in range(TPB * b, TPB * b + TPB):
                    pe.wait_ge(s_xn, i + 1)
                    m = pe.transpose(ps[:, b, (i % TPB) * P:(i % TPB) * P + P], xn[:, i, :], ident)
                m.then_inc(s_xnT, 1)
            pe.wait_ge(s_wsc, 1)
            for i in range(NT):
                pe.wait_ge(s_xnTc, i // TPB + 1)
                if i >= 8:
                    pe.wait_ge(s_qkvc, i - 8 + 2 - i % 2)
                m = pe.matmul(ps[:, 4 + (i // 2) % 4, (i % 2) * QKV_W:(i % 2) * QKV_W + QKV_W],
                              xnT[:, i * P:i * P + P], wqkv, start=True, stop=True)
                m.then_inc(s_qkvp, 1)
            pe.wait_ge(s_split, 1)
            pe.wait_ge(s_idb, 1)
            pe.wait_ge(s_qkvc, NT)
            for n in range(8):
                dst = ps[:, n, :].bitcast(BF16)
                for i in range(8 * (n % 2), 8 * (n % 2) + 8):
                    c = (i % 8) * P
                    if n < 6:
                        m = pe.transpose(dst[:, c:c + P], qs[:, i, n // 2, :], identb)
                    else:
                        m = pe.transpose(dst[0:96, c:c + P],
                                         ks[:, i, :, :].rearrange("p s c -> p (s c)"), identb)
                m.then_inc(s_splT, 1)
            pe.wait_ge(s_splTa, 4)
            pe.wait_ge(s_splTv, 4)
            pe.wait_ge(s_w0, 16 * 8)
            pe.wait_ge(s_summ, 2)
            for j in range(HC):
                pe.matmul(ps[:, 0, NC * j:NC * j + NC], wk0[:, P * j:P * j + P], summT, start=True, stop=True)
            for j in range(HC):
                m = pe.matmul(ps[:, 0, 256 + NC * j:256 + NC * j + NC], wv0[:, P * j:P * j + P], summT,
                              start=True, stop=True)
            m.then_inc(s_kv, 1)
            pe.wait_ge(s_kbd, 2)
            for j in range(HC):
                kj = kbd[:, j].rearrange("p a c -> p (a c)")
                pe.matmul(ps[:, 1, 64 * j:64 * j + 64], wqT[:, j, :], kj, start=True, stop=True)
                pe.matmul(ps[:, 2, 64 * j:64 * j + 64], bq0[:, j:j + 1].broadcast_to([P, P]), kj,
                          start=True, stop=True)
            for j in range(HC):
                m = pe.matmul(ps[64 * (j % 2):64 * (j % 2) + 64, 3, P * (j // 2):P * (j // 2) + P],
                              vbd[:, j].rearrange("p a c -> p (a c)"), wo0[:, j, :], start=True, stop=True)
            m.then_inc(s_gw, 1)
            pe.wait_ge(s_gc, 3)
            for i in range(NT + 2):
                if i < NT:
                    w = 2 * i + 2
                    if i >= 2:
                        pe.wait_ge(s_sadd, i - 1)
                    pe.matmul(ps[:, 4 + i % 2, 0:HEADS * w].rearrange("p (h c) -> p h c", h=HEADS),
                              xnT[:, i * P:i * P + P], gmat[:, :, 0:w], start=True, stop=True).then_inc(s_s, 1)
                if 1 <= i <= NT:
                    pe.wait_ge(s_pr, i)
                    if i >= 3:
                        pe.wait_ge(s_ptc, i - 2)
                    for q in range(4):
                        m = pe.transpose(ps[:, 6 + (i - 1) % 2, P * q:P * q + P],
                                         pr[:, (i - 1) % 2, P * q:P * q + P], ident)
                    m.then_inc(s_pt, 1)
                if i >= 2:
                    pe.wait_ge(s_ptc, i - 1)
                    if i >= 4:
                        pe.wait_ge(s_a0, i - 3)
                    for q in range(4):
                        m = pe.matmul(ps[:, i % 2, 0:D], ptr[:, i % 2, P * q:P * q + P], vw[:, q, :],
                                      start=(q == 0), stop=(q == 3))
                    m.then_inc(s_o, 1)
            pe.wait_ge(s_a0, NT)
            pe.wait_ge(s_qst, 16 * NSPLIT * NSPLIT * (NKV + 1))
            pe.wait_ge(s_pad, 3)
            qst_flat = r2[:, 0:16384].bitcast(BF16)
            kst_flat = r2[:, 16384:20480].bitcast(BF16)
            with pe.Fori(0, NKV) as g:
                for k in range(KB + 1):
                    if k < KB:
                        qb, kt, off = BLOCKS[k]
                        for pair in range(2):
                            n = 2 * k + pair
                            free = PAIRS + n - SBUFS + 1 if n >= SBUFS else last_user(n, SBUFS, PAIRS) + 1
                            pe.wait_ge(s_exp, g * PAIRS + free)
                            for h in range(2):
                                m = pe.matmul(ps[:, 2 * (n % SBUFS) + h, off:TB],
                                              kst_flat[:, bass.ds(g * T + kt * P, P)],
                                              qst_flat[:, bass.ds(g * (REP * T) + ((2 * pair + h) * T + qb * TB + off),
                                                                  TB - off)],
                                              start=True, stop=True)
                            m.then_inc(s_qk, 1)
                    if k >= 1:
                        qb, kt, off = BLOCKS[k - 1]
                        if k == 1:
                            pe.wait_ge(s_vc, g + 1)
                        if kt == 0:
                            pe.wait_ge(s_accc, g * NB + (qb + 1))
                        if kt >= TPB * qb:
                            pe.wait_ge(s_msk, g * (2 * len(DIAG)) + 2 * (DIAG.index(k - 1) + 1))
                        else:
                            pe.wait_ge(s_exp, g * PAIRS + (PAIRS + 2 * k))
                        for j in range(REP):
                            m = pe.matmul(ps[32 * j:32 * j + 32, 6 + qb % 2, off:TB], vc[:, kt, :],
                                          probs[:, (2 * (k - 1) + j // 2) % PBUFS, j % 2, off:TB],
                                          start=(kt == 0), stop=(kt == TPB * qb + TPB - 1))
                        m.then_inc(s_pv, 1)
            for n in range(NKV * NB):
                pe.wait_ge(s_accc, n + 3)
                if n >= 4:
                    pe.wait_ge(s_att, n - 3)
                for i in range(TPB):
                    m = pe.transpose(ps[:, n % 4, P * i:P * i + P], outT[:, n, P * i:P * i + P], ident)
                m.then_inc(s_oT, 1)
            for b in range(NB):
                pe.wait_ge(s_att, NKV * NB)
                for i in range(TPB):
                    m = pe.transpose(ps[:, 4 + b, P * i:P * i + P], att[:, TPB * b + i, :], ident)
                m.then_inc(s_aT, 1)
            pe.wait_ge(s_wrest, 16 * 25)
            for b in range(NB):
                pe.wait_ge(s_aTc, b + 1)
                pe.matmul(ps[:, b, :], wg, oT[:, b * TB:b * TB + TB], start=True, stop=True).then_inc(s_gp, 1)
            for b in range(NB):
                pe.wait_ge(s_og, b + 1)
                for i in range(TPB):
                    t = (TPB * b + i) * P
                    m = pe.matmul(ps[:, 4 + b, P * i:P * i + P], oT[:, t:t + P], wo, start=True, stop=True)
                m.then_inc(s_wo, 1)
            for b in range(NB):
                pe.wait_ge(s_h2, TPB * (b + 1))
                for i in range(TPB):
                    m = pe.transpose(ps[:, b, P * i:P * i + P], h2[:, TPB * b + i, :], ident)
                m.then_inc(s_h2T, 1)
            pe.wait_ge(s_xm, NB)
            for i in range(NT):
                pe.wait_ge(s_h2Tc, i // TPB + 1)
                m = pe.matmul(ps[:, 4, E * i:E * i + E], h2T[:, i * P:i * P + P], wr, start=True, stop=True)
            m.then_inc(s_lg, 1)
            pe.wait_ge(s_oh, 1)
            for i in range(NT):
                m = pe.transpose(ps[0:E, 4 + i // TPB, P * (i % TPB):P * (i % TPB) + P], oh[:, i, :], ident)
            m.then_inc(s_ohT, 1)
            pe.wait_ge(s_moew, 32)
            pe.wait_ge(s_pen, 1)
            pe.wait_ge(s_idb, 2)
            ES = E * FC
            pe.sem_inc(s_dn, ES)
            pe.sem_inc(s_yt, 1)
            with pe.Fori(0, NB) as tb:
                for n in range(ES + 1):
                    if n < ES:
                        e, c = divmod(n, FC)
                        free = ES + n - 2 if n >= 3 else last_user(n, 3, ES) + 1
                        pe.wait_ge(s_moea, tb * ES + free)
                        toks = bass.ds(tb * TB, TB)
                        b = 2 * (n % 3)
                        pe.matmul(ps[:, b + 1, :], w1[:, e, HID + P * c:HID + P * c + P], h2T[:, toks],
                                  start=True, stop=False)
                        pe.matmul(ps[:, b + 1, :], onee[:, e, :], pen[:, toks], start=False, stop=True)
                        pe.matmul(ps[:, b, :], w1[:, e, P * c:P * c + P], h2T[:, toks],
                                  start=True, stop=True).then_inc(s_up, 1)
                    if n == 0:
                        pe.wait_ge(s_yc, tb + 1)
                        pe.matmul(ps[:, 6, :], b2, ohT[:, toks], start=True, stop=False)
                    if n >= 1:
                        e, c = divmod(n - 1, FC)
                        pe.wait_ge(s_moea, tb * ES + (ES + n))
                        pe.matmul(ps[:, 6, :], w2[:, e, c, :], am[:, (n - 1) % 3, :],
                                  start=False, stop=(n == ES)).then_inc(s_dn, 1)
                pe.wait_ge(s_yc, tb + 2)
                pe.wait_ge(s_ya, tb + 1)
                for i in range(TPB):
                    m = pe.transpose(ps[:, 7, P * i:P * i + P], yT[:, P * i:P * i + P], ident)
                m.then_inc(s_yt, 1)
            pe.wait_ge(s_ya, NB + 1)
            for b in range(2 * NB):
                for i in range(TPB):
                    t = b % NB * TPB + i
                    if b < NB:
                        pe.wait_ge(s_xn2, t + 1)
                    else:
                        pe.wait_ge(s_xs, t + 1)
                    m = pe.transpose(ps[:, b, P * i:P * i + P], (xn if b < NB else xs)[:, t, :], ident)
                m.then_inc(s_xn2T, 1)
            def bank_read(u):
                b, k = divmod(u, 6)
                pe.wait_ge(s_pja if 2 <= k <= 4 else s_pjv, 3 * b + (k - 1 if 2 <= k <= 4 else min(k, 2) + 1))

            pe.wait_ge(s_inp, 1)
            pe.wait_ge(s_xn2c, 2 * NB)
            for u in range(6 * NB):
                b, k = divmod(u, 6)
                if u >= 8:
                    bank_read(u - 8)
                pe.matmul(ps[:, u % 8, :], inp[:, P * k:P * k + P], xsT[:, b * TB:b * TB + TB],
                          start=True, stop=True).then_inc(s_pj, 1)
            for i in range(NT):
                u = 6 * NB + i // 3
                if i % 3 == 0:
                    bank_read(u - 8)
                m = pe.matmul(ps[:, u % 8, 132 * (i % 3):132 * (i % 3) + 132], xsT[:, i * P:i * P + P],
                              inp[:, 640:772], start=True, stop=True)
                if i % 3 == 2 or i == NT - 1:
                    m.then_inc(s_bt, 1)
            pe.wait_ge(s_av, 1)
            pe.wait_ge(s_pja, 3 * NB)
            pe.wait_ge(s_pjv, 3 * NB)
            pe.matmul(ps[:, 6, 0:NT * NH], tri, av.rearrange("p i h -> p (i h)"), start=True, stop=True
                      ).then_inc(s_cum, 1)
            pe.wait_ge(s_cumc, 1)
            pe.wait_ge(s_btc, 6)
            pe.wait_ge(s_xc, NB)
            for c in range(NT + 2):
                if c < NT:
                    b = c % 2
                    toks = slice(c * P, c * P + P)
                    if c >= 2:
                        pe.wait_ge(s_cx, 2 * (c - 2) + 2)
                        pe.wait_ge(s_ce, 2 * (c - 2) + 2)
                    pe.matmul(ps[:, b, 0:P], BT[:, toks], CT[:, toks], start=True, stop=True)
                    for m_ in range(MI):
                        pe.transpose(ps[:, b, P + P * m_:2 * P + P * m_], xc[:, m_, toks], ident)
                    for h in range(NH):
                        m = pe.matmul(ps[:, 2 + b, P * h:P * h + P], av[:, c, h:h + 1].broadcast_to([P, P]), tri,
                                      start=True, stop=True)
                    m.then_inc(s_c1, 1)
                if 1 <= c <= NT:
                    k, b = c - 1, (c - 1) % 2
                    pe.wait_ge(s_cm, 2 * k + 2)
                    pe.wait_ge(s_cx, 2 * k + 2)
                    pe.wait_ge(s_ch, k + 1)
                    if k >= 2:
                        pe.wait_ge(s_cg, k - 1)
                    for h in range(NH):
                        dst = ps[PD * (h % 2):PD * (h % 2) + PD, 4 + b, P * (h // 2):P * (h // 2) + P]
                        pe.matmul(dst, dtx[:, b, h, :], mm[:, b, h, :], start=True, stop=False)
                        m = pe.matmul(dst, hst[:, h, :], cs[:, b, h, :], start=False, stop=True)
                    m.then_inc(s_cy, 1)
                    pe.matmul(ps[:, 6, 0:DI], btd[:, k, 0:P], dtw[:, b].rearrange("p h d -> p (h d)"),
                              start=True, stop=True).then_inc(s_cst, 1)
                if c >= 2:
                    k, b = c - 2, c % 2
                    pe.wait_ge(s_cg, k + 1)
                    if k >= 1:
                        pe.wait_ge(s_ca, k)
                    for m_ in range(MI):
                        m = pe.matmul(ps[:, 7, 0:D], yg[:, b, m_, :], owT[:, m_, :], start=(m_ == 0),
                                      stop=(m_ == MI - 1))
                    m.then_inc(s_co, 1)
            pe.wait_ge(s_ca, NT)
            pe.wait_ge(s_fs, 1)
            pe.sem_inc(s_f2, FO)
            pe.sem_inc(s_f3, FO)
            pe.sem_inc(s_f4, 1)
            with pe.Fori(0, NB) as blk_i:
                toks = bass.ds(blk_i * TB, TB)
                pe.wait_ge(s_fg3, blk_i * FO + FO)
                pe.wait_ge(s_fr, blk_i + 1)
                for o in range(FO):
                    pe.matmul(ps[:, 2 * o, :], f1[:, P * o:P * o + P], xnT[:, toks], start=True, stop=True)
                    pe.matmul(ps[:, 2 * o + 1, :], f2[:, P * o:P * o + P], xnT[:, toks], start=True, stop=True
                              ).then_inc(s_fu, 1)
                pe.wait_ge(s_fg, blk_i * FO + FO)
                for o in range(FO):
                    for k in range(FO):
                        m = pe.matmul(ps[:, o, :], fh1[:, k, P * o:P * o + P], fa[:, k, :],
                                      start=(k == 0), stop=(k == FO - 1))
                    m.then_inc(s_f2, 1)
                pe.wait_ge(s_fg2, blk_i * FO + FO)
                for o in range(FO):
                    for k in range(FO):
                        m = pe.matmul(ps[:, FO + o, :], fh2[:, k, P * o:P * o + P], fb[:, k, :],
                                      start=(k == 0), stop=(k == FO - 1))
                    m.then_inc(s_f3, 1)
                pe.wait_ge(s_fg3, blk_i * FO + 2 * FO)
                for i in range(TPB):
                    for k in range(FO):
                        m = pe.matmul(ps[:, 0, P * i:P * i + P], fa[:, k, P * i:P * i + P], f3[:, k, :],
                                      start=(k == 0), stop=(k == FO - 1))
                m.then_inc(s_f4, 1)

        @block.vector
        def _(dve):
            step = Steps(dve, s_v)
            for i in range(NT):
                if i % TPB == 0:
                    dve.wait_ge(s_x[i // TPB], 16)
                step.mark(dve.bn_stats(stats[:, i, :], res[:, i, :]))
            step.settle()
            for i in range(NT):
                m = dve.bn_aggr(mv[:, i, :], stats[:, i, :])
            m.then_inc(s_var, 1)
            dve.wait_ge(s_sd, 1)
            step.alone(dve.reciprocal(rstd, sd))
            for i in range(NT):
                dve.tensor_scalar(xn[:, i, :], res[:, i, :], mv[:, i, 0:1], rstd[:, i:i + 1],
                                  ALU.subtract, ALU.mult).then_inc(s_xn, 1)
            step.alone(dve.tensor_tensor(ms, mv[:, :, 1], rstd, ALU.mult))
            dve.tensor_tensor(ms, ms, rstd, ALU.mult).then_inc(s_var, 1)
            dve.wait_ge(s_wqkv, 16 * 9)
            dve.tensor_scalar(wqkv, wqkv, ln1, None, ALU.mult).then_inc(s_wsc, 1)
            dve.wait_ge(s_const, 16)
            dve.tensor_copy(identb, ident).then_inc(s_idb, 1)
            step.alone(dve.tensor_tensor(kw, qn_bc, kn_bc, ALU.mult))
            step.mark(dve.tensor_scalar(kw, kw, QD ** -0.5, None, ALU.mult))
            step.mark(dve.tensor_reduce(mx2[:, 0:1], qn_bc, X_AXIS, ALU.max, apply_absolute_value=True))
            step.mark(dve.tensor_reduce(mx2[:, 1:2], kn_bc, X_AXIS, ALU.max, apply_absolute_value=True))
            step.settle()
            step.alone(dve.tensor_tensor(shift, mx2[:, 0:1], mx2[:, 1:2], ALU.mult))
            step.alone(dve.tensor_scalar(shift, shift, -(QD ** 0.5), None, ALU.mult))
            dve.wait_ge(s_sd, 2)
            step.alone(dve.reciprocal(hs, sd2))
            for i in range(NT):
                dve.wait_ge(s_qkvp, i - i % 2 + 2)
                src = ps[:, 4 + (i // 2) % 4, (i % 2) * QKV_W:(i % 2) * QKV_W + QKV_W]
                dve.scalar_tensor_tensor(qkv[:, i, :], src, hs[:, i:i + 1], bqkv, ALU.mult, ALU.add
                                         ).then_inc(s_qkvc, 1)
            dve.wait_ge(s_qkvc, NT)
            qk = qkv[:, :, 0:160].rearrange("p i (h d) -> p i h d", d=QD)
            c_b = cosT.unsqueeze(2).broadcast_to([P, NT, 20, 4])
            s_b = sinT.unsqueeze(2).broadcast_to([P, NT, 20, 4])
            for half, (wa, wb, op) in enumerate(((c_b, s_b, ALU.subtract), (s_b, c_b, ALU.add))):
                step.mark(dve.tensor_tensor(rot_a, qk[:, :, :, 0:4], wa, ALU.mult))
                step.mark(dve.tensor_tensor(rot_b, qk[:, :, :, 4:8], wb, ALU.mult))
                step.settle()
                m = dve.tensor_tensor(rot[:, :, :, 4 * half:4 * half + 4], rot_a, rot_b, op)
                if half == 0:
                    step.alone(m)
            m.then_inc(s_rot, 1)
            dve.wait_ge(s_vp, 1)
            dve.tensor_copy(vp[:, :, :, 0:QD], qkv[:, :, 160:192].rearrange("p i (g d) -> p i g d", d=QD)
                            ).then_inc(s_vp, 1)
            dve.wait_ge(s_sq, 1)
            dve.tensor_reduce(ssq, sq, X_AXIS, ALU.add).then_inc(s_ssq, 1)
            dve.wait_ge(s_qksd, 1)
            step.alone(dve.reciprocal(ssq, rr))
            step.alone(dve.tensor_tensor(rot, rot, over(ssq.rearrange("p (i h) -> p i h", i=NT), QD), ALU.mult))
            kr = rot[:, :, 16:20, :]
            step.alone(dve.tensor_tensor(kr, kr, kw.unsqueeze(1).unsqueeze(1).broadcast_to([P, NT, NKV, QD]),
                                         ALU.mult))
            for s in range(NSPLIT):
                for spl, src in ((qs[:, :, s, :], rotf[:, :, 0:128]), (ks[:, :, s, :], rotf[:, :, 128:160])):
                    step.mark(dve.tensor_copy(spl, src))
                step.settle()
                if s < NSPLIT - 1:
                    for spl, src in ((qs[:, :, s, :], rotf[:, :, 0:128]), (ks[:, :, s, :], rotf[:, :, 128:160])):
                        step.mark(dve.tensor_tensor(src, src, spl, ALU.subtract))
                    step.settle()
            dve.sem_inc(s_split, 1)
            for n in range(1, 8, 2):
                dve.wait_ge(s_splT, n + 1)
                src = ps[:, n, :].bitcast(BF16)
                if n < 6:
                    dve.tensor_copy(qT[:, n // 2, 1024:2048], src).then_inc(s_splTv, 1)
                else:
                    dve.tensor_copy(kT[0:96, 1024:2048], src[0:96, :]).then_inc(s_splTv, 1)
            step.mark(dve.tensor_reduce(summT[:, 1:NC],
                                        xnT[:, 1:1 + CHUNK * (NC - 1)].rearrange("p (c t) -> p c t", t=CHUNK),
                                        X_AXIS, ALU.add))
            step.settle()
            step.mark(dve.tensor_scalar(summT[:, 1:NC], summT[:, 1:NC], 1.0 / CHUNK, None, ALU.mult))
            dve.tensor_copy(summT[:, 0:1], xnT[:, 0:1]).then_inc(s_summ, 1)
            step.settle()
            dve.sem_inc(s_summ, 1)
            dve.wait_ge(s_kv, 1)
            dve.wait_ge(s_pad, 3)
            for src, bias, bd, scale in ((0, bk0, kbd, HD ** -0.5), (256, bv0, vbd, 1.0)):
                step.alone(dve.tensor_tensor(kvb, ps[:, 0, src:src + 256].rearrange("p (j c) -> p j c", j=HC),
                                             over(bias, NC), ALU.add))
                for a in range(2):
                    step.mark(dve.tensor_scalar(bd[64 * a:64 * a + 64, :, a, :], kvb[64 * a:64 * a + 64], scale, None,
                                                ALU.mult))
                step.settle()
                dve.sem_inc(s_kbd, 1)
            step.alone(dve.tensor_tensor(res, res, along(bo0_bc, NT), ALU.add))
            dve.wait_ge(s_gc, 3)
            for i in range(NT + 2):
                if i < NT:
                    w = 2 * i + 2
                    b = i % 2
                    blk = sc[:, b, :, 0:w]
                    dve.wait_ge(s_s, i + 1)
                    dve.tensor_tensor(blk, ps[:, 4 + b, 0:HEADS * w].rearrange("p (h c) -> p h c", h=HEADS),
                                      g0[:, :, 0:w], ALU.add).then_inc(s_sadd, 1)
                    dve.wait_ge(s_sadd, i + 1)
                    step.alone(dve.memset(sc[0:64, b, :, w - 1:w], -BIG))
                    step.alone(dve.tensor_reduce(smx[:, b, :], blk, X_AXIS, ALU.max))
                    dve.tensor_tensor(blk, blk, over(smx[:, b, :], w), ALU.subtract).then_inc(s_sub, 1)
                if 1 <= i <= NT:
                    w = 2 * i
                    b = (i - 1) % 2
                    blk = sc[:, b, :, 0:w]
                    dve.wait_ge(s_ex, i)
                    step.alone(dve.tensor_reduce(ssm_[:, b, :], blk, X_AXIS, ALU.add))
                    step.alone(dve.reciprocal(ssm_[:, b, :], ssm_[:, b, :]))
                    if i >= 3:
                        dve.wait_ge(s_pt, i - 2)
                    dve.tensor_tensor(pr[:, b, :].rearrange("p (h c) -> p h c", h=HEADS)[:, :, 0:w], blk,
                                      over(ssm_[:, b, :], w), ALU.mult).then_inc(s_pr, 1)
                if i >= 2:
                    dve.wait_ge(s_o, i - 1)
                    dve.tensor_tensor(res[:, i - 2, :], res[:, i - 2, :], ps[:, i % 2, 0:D], ALU.add
                                      ).then_inc(s_a0, 1)
            dve.sem_inc(s_accc, 2)
            outT_flat = r1[:, 6144:14336]
            with dve.Fori(0, NKV) as g:
                for qb in range(NB):
                    last = max(k for k in range(KB) if BLOCKS[k][0] == qb)
                    dve.wait_ge(s_pv, g * KB + (KB + last + 1))
                    dve.tensor_copy(outT_flat[:, bass.ds(g * T + qb * TB, TB)], ps[:, 6 + qb % 2, :]
                                    ).then_inc(s_accc, 1)
            dve.wait_ge(s_wrest, 16 * 25)
            for n in range(NKV * NB):
                g, qb = divmod(n, NB)
                src = ps[:, n % 4, :].rearrange("p (ij m) -> p ij m", m=32)
                dve.wait_ge(s_oT, n + 1)
                step.alone(dve.reciprocal(rden[:, n % 2, :], src[:, :, QD]))
                dve.tensor_tensor(att[:, TPB * qb:TPB * qb + TPB, 32 * g:32 * g + 32].rearrange(
                    "p i (j d) -> p i j d", d=QD),
                    src[:, :, 0:QD].rearrange("p (i j) d -> p i j d", i=TPB),
                    over(rden[:, n % 2, :].rearrange("p (i j) -> p i j", i=TPB), QD), ALU.mult).then_inc(s_att, 1)
            for b in range(NB):
                dve.wait_ge(s_gt, b + 1)
                blk = oT[:, b * TB:b * TB + TB]
                dve.tensor_tensor(blk, blk, gate[:, b * TB:b * TB + TB], ALU.mult).then_inc(s_og, 1)
            step.alone(dve.tensor_tensor(xn, xn, along(bo_bc, NT), ALU.add))
            for b in range(NB):
                dve.wait_ge(s_wo, b + 1)
                blk = xn[:, TPB * b:TPB * b + TPB, :]
                dve.tensor_tensor(blk, blk, ps[:, 4 + b, :].rearrange("p (i d) -> p i d", d=D), ALU.add
                                  ).then_inc(s_xm, 1)
            for b in range(NB):
                dve.wait_ge(s_sq2, b + 1)
                dve.tensor_reduce(ssq2[:, TPB * b:TPB * b + TPB], sqm[:, TPB * b:TPB * b + TPB, :], X_AXIS, ALU.add
                                  ).then_inc(s_ss2, 1)
            dve.wait_ge(s_sd2, 1)
            step.alone(dve.reciprocal(hs2, sdm))
            for i in range(NT):
                dve.tensor_scalar(h2[:, i, :], xn[:, i, :], hs2[:, i:i + 1], None, ALU.mult).then_inc(s_h2, 1)
            dve.wait_ge(s_lg, 1)
            step.alone(dve.tensor_tensor(lg, ps[:, 4, 0:P].rearrange("p (i e) -> p i e", e=E), along(br_bc, NT),
                                         ALU.add))
            step.alone(dve.tensor_reduce(lmx, lg, X_AXIS, ALU.max))
            step.alone(dve.tensor_tensor(eq, lg, over(lmx, E), ALU.is_equal))
            step.alone(dve.tensor_tensor(rk, eq, along(rank, NT), ALU.mult))
            step.alone(dve.tensor_reduce(lmx2, rk, X_AXIS, ALU.max))
            dve.tensor_tensor(oh, rk, over(lmx2, E), ALU.is_equal).then_inc(s_oh, 1)
            dve.wait_ge(s_ohT, 1)
            ohT_ps = ps[0:E, 4:8, :].rearrange("p b t -> p (b t)")
            step.mark(dve.tensor_copy(ohT, ohT_ps))
            dve.tensor_scalar(pen, ohT_ps, 1.0, BIG, ALU.subtract, ALU.mult).then_inc(s_pen, 1)
            step.settle()
            step.alone(dve.tensor_tensor(res, res, xn, ALU.add))
            ES = E * FC
            dve.sem_inc(s_moea, ES)
            dve.sem_inc(s_ya, 1)
            with dve.Fori(0, NB) as tb:
                for n in range(ES):
                    e, c = divmod(n, FC)
                    dve.wait_ge(s_sg, tb * ES + (n + 1))
                    free = ES + n - 2 if n >= 3 else last_user(n, 3, ES) + 1
                    dve.wait_ge(s_dn, tb * ES + free)
                    dve.scalar_tensor_tensor(am[:, n % 3, :], ps[:, 2 * (n % 3), :], b1c[:, e, c:c + 1],
                                             sg[:, n % 3, :], ALU.add, ALU.mult).then_inc(s_moea, 1)
                dve.wait_ge(s_yt, tb + 2)
                blk = res_flat[:, bass.ds(tb * TB, TB)]
                dve.tensor_tensor(blk, blk, ps[:, 7, :], ALU.add).then_inc(s_ya, 1)
            dve.wait_ge(s_ya, NB + 1)
            for i in range(NT):
                step.mark(dve.bn_stats(stats[:, i, :], res[:, i, :]))
            step.settle()
            for i in range(NT):
                m = dve.bn_aggr(mv[:, i, :], stats[:, i, :])
            m.then_inc(s_var2, 1)
            dve.wait_ge(s_sdl, 1)
            step.alone(dve.reciprocal(rstd, sd))
            for i in range(NT):
                dve.tensor_scalar(xn[:, i, :], res[:, i, :], mv[:, i, 0:1], rstd[:, i:i + 1],
                                  ALU.subtract, ALU.mult).then_inc(s_xn2, 1)
            step.alone(dve.tensor_tensor(ms, mv[:, :, 1], rstd, ALU.mult))
            dve.tensor_tensor(ms, ms, rstd, ALU.mult).then_inc(s_var2, 1)
            dve.wait_ge(s_l1w, 16 * 18)
            step.mark(dve.tensor_scalar(inp, inp, normw, None, ALU.mult))
            step.mark(dve.tensor_scalar(owT, owT, 0.5, None, ALU.mult))
            step.mark(dve.tensor_scalar(d2, d2, 0.5, None, ALU.mult))
            step.mark(dve.tensor_scalar(w1sh, w1s, 0.5, None, ALU.mult))
            step.settle()
            dve.tensor_tensor(s12, w1sh, w2s, ALU.mult).then_inc(s_fs, 1)
            dve.sem_inc(s_inp, 1)
            dve.wait_ge(s_sdl, 2)
            step.alone(dve.reciprocal(hs, sd2))
            dve.wait_ge(s_xn2, NT)
            for i in range(NT):
                dve.tensor_scalar(xs[:, i, :], xn[:, i, :], hs[:, i:i + 1], None, ALU.mult).then_inc(s_xs, 1)
            step.alone(dve.tensor_tensor(res, res, xn, ALU.add))
            dve.wait_ge(s_pad, 4)
            for b in range(NB):
                toks = slice(b * TB, b * TB + TB)
                for k in (0, 1):
                    u = 6 * b + k
                    dve.wait_ge(s_zth, 2 * b + k + 1)
                    dve.scalar_tensor_tensor(z2[:, k, toks], th[:, k, :], 1.0, ps[:, u % 8, :], ALU.add, ALU.mult
                                             ).then_inc(s_pjv, 1)
                u = 6 * b + 5
                dve.wait_ge(s_pj, u + 1)
                dve.tensor_copy(BT[:, toks], ps[:, u % 8, :]).then_inc(s_pjv, 1)
                dve.wait_ge(s_pja, 3 * b + 2)
                for k in range(KW):
                    for m_ in range(MI):
                        src = xp[:, m_, b * TB + k:b * TB + k + TB]
                        if k == 0:
                            step.mark(dve.tensor_scalar(xc[:, m_, toks], src, convw[:, m_, 0:1],
                                                        convb[:, m_:m_ + 1], ALU.mult, ALU.add))
                        else:
                            step.mark(dve.scalar_tensor_tensor(xc[:, m_, toks], src, convw[:, m_, k:k + 1],
                                                               xc[:, m_, toks], ALU.mult, ALU.add))
                    step.settle()
                dve.sem_inc(s_xcv, 1)
            for b in range(NB):
                blk = xc[:, :, b * TB:b * TB + TB]
                dve.wait_ge(s_xth, b + 1)
                dve.scalar_tensor_tensor(blk, thc, 1.0, blk, ALU.add, ALU.mult).then_inc(s_xc, 1)
            for g in range(6):
                n = min(3, NT - 3 * g)
                dve.wait_ge(s_bt, g + 1)
                dve.tensor_copy(btd[:, 3 * g:3 * g + n, :],
                                ps[:, (6 * NB + g) % 8, 0:132 * n].rearrange("p (i c) -> p i c", c=132)
                                ).then_inc(s_btc, 1)
            dve.wait_ge(s_btc, 6)
            step.alone(dve.tensor_tensor(du, btd[:, :, P:P + NH], along(dtb, NT), ALU.add))
            dve.scalar_tensor_tensor(dl, du, -1.0, du, ALU.mult, ALU.min).then_inc(s_dta, 1)
            dve.wait_ge(s_dtb, 3)
            step.alone(dve.scalar_tensor_tensor(dt, du, 0.0, dl, ALU.max, ALU.add))
            dve.scalar_tensor_tensor(av, dt, -1.0, along(ea, NT), ALU.mult, ALU.mult).then_inc(s_av, 1)
            dve.wait_ge(s_av, 1)
            step.alone(dve.tensor_scalar(dt, dt, 0.5, None, ALU.mult))
            dve.wait_ge(s_cum, 1)
            dve.tensor_copy(cums, ps[:, 6, 0:NT * NH].rearrange("p (i h) -> p i h", i=NT)).then_inc(s_cumc, 1)
            dve.wait_ge(s_cumc, 1)
            for c in range(NT + 2):
                if c < NT:
                    b = c % 2
                    dve.wait_ge(s_c1, c + 1)
                    if c >= 2:
                        dve.wait_ge(s_cm, 2 * (c - 2) + 2)
                    step.alone(dve.tensor_tensor(ed[:, b], ps[:, 2 + b, :].rearrange("p (h t) -> p h t", h=NH),
                                                 over(cums[:, c, :], P), ALU.subtract))
                    dve.tensor_scalar(ed[:, b], ed[:, b], 0.0, None, ALU.min).then_inc(s_cd, 1)
                    dve.tensor_tensor(gm[:, b, :], ps[:, b, 0:P], tri, ALU.mult).then_inc(s_cx, 1)
                    if c >= 2:
                        dve.wait_ge(s_cst, c - 1)
                    step.alone(dve.tensor_tensor(dtx[:, b], ps[:, b, P:P + DI].rearrange("p (h d) -> p h d", h=NH),
                                                 over(dt[:, c, :], PD), ALU.mult))
                    dve.wait_ge(s_ce, 2 * c + 1)
                    dve.tensor_tensor(dtw[:, b], dtx[:, b], over(ed[:, b, :, P - 1], PD), ALU.mult
                                      ).then_inc(s_cx, 1)
                if 1 <= c <= NT:
                    k, b = c - 1, (c - 1) % 2
                    toks = slice(k * P, k * P + P)
                    dve.wait_ge(s_cy, k + 1)
                    dve.wait_ge(s_ce, 2 * k + 2)
                    step.alone(dve.tensor_tensor(hst, hst, over(ec[:, b, :, P - 1], PD), ALU.mult))
                    dve.wait_ge(s_cst, k + 1)
                    dve.tensor_tensor(hst, hst, ps[:, 6, 0:DI].rearrange("p (h d) -> p h d", h=NH), ALU.add
                                      ).then_inc(s_ch, 1)
                    if k >= 2:
                        dve.wait_ge(s_co, k - 1)
                    for m_ in range(MI):
                        step.mark(dve.scalar_tensor_tensor(yg[:, b, m_, :], xc[:, m_, toks], d2[:, m_:m_ + 1],
                                                           ps[:, 4 + b, P * m_:P * m_ + P], ALU.mult, ALU.add))
                    step.settle()
                    dve.tensor_tensor(yg[:, b], yg[:, b], z2[:, :, toks], ALU.mult).then_inc(s_cg, 1)
                if c >= 2:
                    dve.wait_ge(s_co, c - 1)
                    dve.tensor_tensor(res[:, c - 2, :], res[:, c - 2, :], ps[:, 7, 0:D], ALU.add
                                      ).then_inc(s_ca, 1)
            dve.sem_inc(s_fm, FO)
            dve.sem_inc(s_fr, 1)
            with dve.Fori(0, NB) as blk_i:
                dve.wait_ge(s_f4, blk_i + 1)
                for o in range(FO):
                    dve.wait_ge(s_ft, blk_i * FO + (o + 1))
                    dve.scalar_tensor_tensor(ft1[:, o % 2, :], fth[:, o % 2, :], 1.0, ps[:, 2 * o, :],
                                             ALU.add, ALU.mult).then_inc(s_fm, 1)
                    dve.wait_ge(s_fm, blk_i * FO + (FO + o + 1))
                    dve.scalar_tensor_tensor(fa[:, o, :], ft1[:, o % 2, :], s12[:, o:o + 1], ps[:, 2 * o + 1, :],
                                             ALU.mult, ALU.mult).then_inc(s_fg, 1)
                dve.wait_ge(s_f4, blk_i + 2)
                dve.tensor_tensor(fst, ps[:, 0, :].rearrange("p (i d) -> p i d", i=TPB), along(w3s_bc, TPB),
                                  ALU.mult).then_inc(s_fr, 1)
                dve.wait_ge(s_fr, blk_i + 2)
                blk = res_flat[:, bass.ds(blk_i * TB, TB)]
                dve.tensor_tensor(blk, blk, fst.rearrange("p i d -> p (i d)"), ALU.add).then_inc(s_fin, 1)


def kernel(**inputs):
    import concourse.bacc as bacc
    from concourse.bass_utils import run_bass_kernel_spmd

    f = {k: np.asarray(v) for k, v in inputs.items()}
    row_ = lambda a: a.reshape(1, -1)
    cols = lambda a, n: a.reshape(n, P).T
    inT = f["L1_attn_in_proj_w"].T
    arrays = {
        "x": f["L0_attn_x"][0],
        "a_WqT": f["L0_attn_Wq"].T, "a_Wk": f["L0_attn_Wk"], "a_Wv": f["L0_attn_Wv"], "a_Wo": f["L0_attn_Wo"],
        "a_bq": cols(f["L0_attn_bq"], HC), "a_bk": cols(f["L0_attn_bk"], HC), "a_bv": cols(f["L0_attn_bv"], HC),
        "a_bo": row_(f["L0_attn_bo"]),
        "f_ln1": f["L0_ffn_ln1_w"].reshape(P, 1), "f_ln2": f["L0_ffn_ln2_w"].reshape(P, 1),
        "f_Wq": f["L0_ffn_Wq"], "f_Wk": f["L0_ffn_Wk"], "f_Wv": f["L0_ffn_Wv"],
        "f_bq": row_(f["L0_ffn_bq"]), "f_bk": row_(f["L0_ffn_bk"]), "f_bv": row_(f["L0_ffn_bv"]),
        "f_qn": row_(f["L0_ffn_qn_w"]), "f_kn": row_(f["L0_ffn_kn_w"]),
        "f_Wg": f["L0_ffn_Wg"], "f_bgc": np.tile(f["L0_ffn_bg"], NQ).reshape(P, 1),
        "f_Wo": f["L0_ffn_Wo"], "f_bo": row_(f["L0_ffn_bo"]),
        "f_Wr": f["L0_ffn_Wr"], "f_br": row_(f["L0_ffn_br"]),
        "f_W1": f["L0_ffn_W1"], "f_b1c": f["L0_ffn_b1"].reshape(E, 2 * FC, P).transpose(2, 0, 1).reshape(P, -1),
        "f_W2": f["L0_ffn_W2"], "f_b2": f["L0_ffn_b2"],
        "s_norm": f["L1_attn_norm_w"].reshape(P, 1),
        "s_inT": np.concatenate([inT[:, 0:2 * DI], inT[:, 2 * DI + P:2 * DI + 2 * P],
                                 inT[:, 2 * DI:2 * DI + P], inT[:, 2 * DI + 2 * P:]], axis=1),
        "s_convw": f["L1_attn_conv_w"].reshape(MI, P, KW).transpose(1, 0, 2).reshape(P, -1),
        "s_convb": cols(f["L1_attn_conv_b"], MI),
        "s_D": np.repeat(f["L1_attn_D"], PD).reshape(MI, P).T,
        "s_dtb": row_(f["L1_attn_dt_bias"]), "s_Alog": row_(f["L1_attn_A_log"]),
        "s_outT": f["L1_attn_out_proj_w"].T,
        "g_w1T": f["L1_ffn_w1_w"].T, "g_w2T": f["L1_ffn_w2_w"].T,
        "g_h1T": f["L1_ffn_h1_w"].T, "g_h2T": f["L1_ffn_h2_w"].T, "g_w3T": f["L1_ffn_w3_w"].T,
        "g_w1s": cols(f["L1_ffn_w1_s"], FO), "g_w2s": cols(f["L1_ffn_w2_s"], FO),
        "g_h1s": cols(f["L1_ffn_h1_s"], FO), "g_h2s": cols(f["L1_ffn_h2_s"], FO),
        "g_w3s": row_(f["L1_ffn_w3_s"]),
    }
    inv = (np.float32(1.0) / np.float32(10000.0) ** (np.arange(0, QD, 2, dtype=np.float32) / np.float32(QD))
           ).astype(np.float32)
    ang = np.arange(T, dtype=np.float32)[:, None] * inv[None, :]
    table = lambda a: a.astype(np.float32).reshape(NT, P, 4).transpose(1, 0, 2).reshape(P, -1)
    arrays["consts"] = np.concatenate([np.eye(P, dtype=np.float32), np.triu(np.ones((P, P), np.float32)),
                                       table(np.cos(ang)), table(np.sin(ang))], axis=1)
    arrays["rank"] = np.arange(E, 0, -1, dtype=np.float32).reshape(1, E)

    nc = bacc.Bacc("TRN2", target_bir_lowering=False, num_devices=1)
    arrays = {k: np.ascontiguousarray(v) for k, v in arrays.items()}
    io = {k: nc.dram_tensor(f"in_{k}", a.shape, mybir.dt.from_np(a.dtype), kind="ExternalInput").ap()
          for k, a in arrays.items()}
    out = nc.dram_tensor("out", (T, D), F32, kind="ExternalOutput").ap()
    build(nc, io, out)
    r = run_bass_kernel_spmd(nc, [{f"in_{k}": a for k, a in arrays.items()}], core_ids=[0])
    return r.results[0]["out"].reshape(1, T, D)
```

```python
from contextlib import ExitStack

import numpy as np

import concourse.bass as bass
import concourse.mybir as mybir

F32 = mybir.dt.float32
F32R = mybir.dt.float32r
BF16 = mybir.dt.bfloat16
ALU = mybir.AluOpType
ACT = mybir.ActivationFunctionType
X_AXIS = mybir.AxisListType.X

P = 128
T = 2048
D = 128
NT = T // P
TB = 512
NB = T // TB
TPB = TB // P

HEADS, HD = 16, 64
NC = 32
CHUNK = 64
HC = HEADS * HD // P

NQ, NKV, QD = 16, 4, 8
REP = NQ // NKV
QKV_W = NQ * QD + 2 * NKV * QD
NSPLIT = 3
KV_W = NKV * QD

E, HID = 8, 256
FC = HID // P

DI, NH, PD = 256, 4, 64
KW = 4
MI = DI // P

FH = 512
FO = FH // P

LN_EPS, RMS_EPS = 1e-5, 1e-6
BIG = 1e30


class Steps:

    def __init__(self, eng, sem):
        self.eng, self.sem, self.n = eng, sem, 0

    def mark(self, instruction):
        instruction.then_inc(self.sem, 1)
        self.n += 1
        return self.n

    def settle(self):
        self.eng.wait_ge(self.sem, self.n)

    def alone(self, instruction):
        self.mark(instruction)
        self.settle()


def over(ap, n):
    return ap.unsqueeze(len(ap.shape)).broadcast_to(list(ap.shape) + [n])


def product(pe, dst, w, x, start, stop):
    (wh, wl), (xh, xl) = w, x
    pe.matmul(dst, wh, xh, start=start, stop=False)
    pe.matmul(dst, wh, xl, start=False, stop=False)
    return pe.matmul(dst, wl, xh, start=False, stop=stop)


def along(ap, n):
    return ap.unsqueeze(1).broadcast_to([ap.shape[0], n] + list(ap.shape[1:]))


def build(nc, io, out):
    ctx = ExitStack()
    with ctx:
        def sb(name, cols, dt=F32, rows=P):
            return ctx.enter_context(nc.sbuf_tensor(name, [rows, cols], dt))

        def sem(name):
            return ctx.enter_context(nc.semaphore(name))

        res = sb("res", NT * D)[:, :].rearrange("p (i d) -> p i d", i=NT)
        xn = sb("xn", NT * D)[:, :].rearrange("p (i d) -> p i d", i=NT)
        xnT = sb("xnT", T)[:, :]
        consts = sb("consts", 2 * P + 2 * NT * 4)
        ident = consts[:, 0:P]
        tri = consts[:, P:2 * P]
        cosT = consts[:, 2 * P:2 * P + 4 * NT].rearrange("p (i f) -> p i f", i=NT)
        sinT = consts[:, 2 * P + 4 * NT:2 * P + 8 * NT].rearrange("p (i f) -> p i f", i=NT)
        identb = sb("identb", P, BF16)[:, :]
        small = sb("small", 512)
        stats = sb("stats", NT * 6)[:, :].rearrange("p (i s) -> p i s", i=NT)
        mv = small[:, 0:32].rearrange("p (i s) -> p i s", i=NT)
        sd, rstd, ms, sd2, hs = (small[:, 32 + 16 * k:48 + 16 * k] for k in range(5))
        bo_bc = small[:, 128:256]
        bo0_bc = small[:, 256:384]
        w3s_bc = small[:, 384:512]
        row = sb("row", 1024)
        bqkv = row[:, 0:QKV_W]
        qn_bc, kn_bc = row[:, 192:200], row[:, 200:208]
        kw = row[:, 208:216]
        shift = row[:, 216:217]
        mx2 = row[:, 217:219]
        ln1 = row[:, 220:221]
        ln2 = row[:, 221:222]
        bgc = row[:, 222:223]
        br_bc = row[:, 224:232]
        rank = row[:, 232:240]
        b1c = row[:, 240:272].rearrange("p (e k) -> p e k", e=E)
        wr = row[:, 272:280]
        normw = row[:, 280:281]
        convw = row[:, 284:292].rearrange("p (m k) -> p m k", m=MI)
        convb = row[:, 292:294]
        d2 = row[:, 294:296]
        dtb = row[:, 296:300]
        alog = row[:, 300:304]
        w1s, w2s = row[:, 304:308], row[:, 308:312]
        h1s, h2s = row[:, 312:316], row[:, 316:320]
        zero = row[:, 320:321]
        wg = row[:, 384:512]
        wo = row[:, 512:640]
        b2 = row[0:E, 640:768]
        oneEf = row[0:E, 768:896]
        w1sh = row[:, 896:900]
        s12 = row[:, 900:904]

        cmask = row[:, 904:936]

        r3 = sb("r3", 10080)
        with nc.sbuf_tensor("r1", [P, 14400], F32) as r1, nc.sbuf_tensor("r2", [P, 20480], F32) as r2:
            pass
        r1r, r2r = sb("r1r", 14400, F32R), sb("r2r", 20480, F32R)

        qkv = r1[:, 0:3072].rearrange("p (i c) -> p i c", i=NT)
        rot = r1[:, 3072:5632].rearrange("p (i d h) -> p i d h", i=NT, d=QD)
        rot_a = r1[:, 5632:6912].rearrange("p (i d h) -> p i d h", i=NT, d=4)
        rot_b = r1[:, 6912:8192].rearrange("p (i d h) -> p i d h", i=NT, d=4)
        sq = r1[:, 5632:8192].rearrange("p (i d h) -> p i d h", i=NT, d=QD)
        qs = r1[:, 5632:8704].bitcast(BF16).rearrange("p (i s c) -> p i s c", i=NT, s=NSPLIT)
        ks = r1[:, 8704:9472].bitcast(BF16).rearrange("p (i s c) -> p i s c", i=NT, s=NSPLIT)
        qT = r1[:, 0:3072].bitcast(BF16).rearrange("p (s t) -> p s t", s=NSPLIT)
        kT = r1[:, 9472:10496].bitcast(BF16)
        ssq = r1[:, 10496:10816]
        rr = r1[:, 10816:11136]
        wqkv = r1[:, 11136:11328]
        probs = r1[:, 0:8192].rearrange("p (b h t) -> p b h t", b=8, h=2)
        att = r1[:, 8192:10240].rearrange("p (i c) -> p i c", i=NT)
        accT = r1[:, 10240:11264].rearrange("p (b t) -> p b t", b=2)
        xti = r1[:, 11264:11776].rearrange("p (m t) -> p m t", m=NB)
        rden = r1[:, 11776:11808].rearrange("p (b n) -> p b n", b=2)
        pr = r1[:, 11808:13856].rearrange("p (m n) -> p m n", m=NB)
        qst = r2[:, 0:16384].bitcast(BF16).rearrange("p (h t) -> p h t", h=NQ)
        kst = r2[:, 16384:20480].bitcast(BF16).rearrange("p (g t) -> p g t", g=NKV)
        vp = r3[:, 0:2048].rearrange("p (i g m) -> p i g m", i=NT, g=NKV)
        wqT = r1[:, 12416:13440].rearrange("p (j d) -> p j d", j=HC)
        kbd = r1[:, 13440:13952].rearrange("p (j a c) -> p j a c", j=HC, a=2)
        kvb = r1[:, 13952:14208].rearrange("p (j c) -> p j c", j=HC)
        s0 = 2048
        wk0 = r3[:, s0:s0 + 1024]
        wv0 = r3[:, s0 + 1024:s0 + 2048]
        wo0 = r3[:, s0 + 2048:s0 + 3072].rearrange("p (j d) -> p j d", j=HC)
        vbd = r3[:, s0 + 3072:s0 + 3584].rearrange("p (j a c) -> p j a c", j=HC, a=2)
        gmat = r3[:, s0 + 3584:s0 + 4096].rearrange("p (h c) -> p h c", h=HEADS)
        g0 = r3[:, s0 + 4096:s0 + 4608].rearrange("p (h c) -> p h c", h=HEADS)
        vw = r3[:, s0 + 4608:s0 + 5120].rearrange("p (q d) -> p q d", q=4)
        sc = r3[:, s0 + 5120:s0 + 6144].rearrange("p (b h c) -> p b h c", b=2, h=HEADS)
        ptr = r3[:, s0 + 6144:s0 + 6656]
        s1 = s0 + 7168
        summT = r3[:, s1:s1 + NC]
        bq0 = r3[:, s1 + 32:s1 + 40]
        bk0 = r3[:, s1 + 40:s1 + 48]
        bv0 = r3[:, s1 + 48:s1 + 56]
        smx = r3[:, s1 + 64:s1 + 96].rearrange("p (b h) -> p b h", b=2)
        ssm_ = r3[:, s1 + 96:s1 + 128].rearrange("p (b h) -> p b h", b=2)

        vc = r3[:, 9344:9856].rearrange("p (i m) -> p i m", i=NT)

        oT = r2[:, 2048:4096]
        gate = r2[:, 4096:6144]
        sqm = r2[:, 6144:8192].rearrange("p (i d) -> p i d", i=NT)
        h2 = r2[:, 8192:10240].rearrange("p (i d) -> p i d", i=NT)
        w1 = r1[:, 0:4096].rearrange("p (e f) -> p e f", e=E)
        w2 = r1[:, 4096:6144].rearrange("p (e c d) -> p e c d", e=E, c=FC)
        w1f, w2f = r1[:, 0:4096], r1[:, 4096:6144]
        w1hf, w2hf = (r2r[:, a:b] for a, b in ((14336, 18432), (18432, 20480)))
        w1lf, w2lf = r1r[:, 0:4096], r1r[:, 4096:6144]
        w1h, w1l = (a.rearrange("p (e f) -> p e f", e=E) for a in (w1hf, w1lf))
        w2h, w2l = (a.rearrange("p (e c d) -> p e c d", e=E, c=FC) for a in (w2hf, w2lf))
        h2T = r3[:, 2048:4096]
        h2h, h2l = r1r[:, 8192:10240], r1r[:, 10240:12288]
        m0 = 4096
        ssq2, sdm, hs2 = (r3[:, m0 + 32 + 16 * k:m0 + 48 + 16 * k] for k in range(3))
        lg, eq, rk, oh = (r3[:, m0 + 128 + 128 * k:m0 + 256 + 128 * k].rearrange("p (i e) -> p i e", e=E)
                          for k in range(4))
        lmx = r3[:, m0 + 96:m0 + 112]
        lmx2 = r3[:, m0 + 112:m0 + 128]
        ohT = r3[0:E, m0 + 640:m0 + 640 + T]
        pen = r3[0:E, m0 + 640 + T:m0 + 640 + T + T // 2].bitcast(BF16)
        onee = r3[0:E, m0 + 640 + T + T // 2:m0 + 640 + T + T // 2 + 512].bitcast(BF16).rearrange(
            "p (e m) -> p e m", e=E)
        sg = r2[:, 10240:11776].rearrange("p (b t) -> p b t", b=3)
        am = r2[:, 11776:13312].rearrange("p (b t) -> p b t", b=3)
        amh = r2r[:, 6664:8200].rearrange("p (b t) -> p b t", b=3)
        aml = r2r[:, 11776:13312].rearrange("p (b t) -> p b t", b=3)
        yT = r2[:, 13312:13824]

        inp = r2[:, 0:772]
        owT = r2[:, 772:1028].rearrange("p (m d) -> p m d", m=MI)
        f1 = r2[:, 1028:1540]
        f2 = r2[:, 1540:2052]
        fh1 = r2[:, 2052:4100].rearrange("p (k o) -> p k o", k=FO)
        fh2 = r2[:, 4100:6148].rearrange("p (k o) -> p k o", k=FO)
        f3 = r2[:, 6148:6660].rearrange("p (k d) -> p k d", k=FO)
        fa = r2[:, 6660:8708].rearrange("p (k t) -> p k t", k=FO)
        fb = r2[:, 8708:10756].rearrange("p (k t) -> p k t", k=FO)
        fth = r2[:, 10756:11780].rearrange("p (b t) -> p b t", b=2)
        fst = r2[:, 11780:12292].rearrange("p (i d) -> p i d", i=TPB)
        xsT = r2[:, 12292:14340]
        xs = r2[:, 14340:16388].rearrange("p (i d) -> p i d", i=NT)
        btd = r2[:, 16388:18500].rearrange("p (i c) -> p i c", i=NT)
        z2 = r1[:, 0:4096].rearrange("p (m t) -> p m t", m=MI)
        xp = r1[:, 4096:8200].rearrange("p (m t) -> p m t", m=MI)
        xc = r1[:, 8200:12296].rearrange("p (m t) -> p m t", m=MI)
        CT = r1[:, 12296:14344]
        BT = r3[:, 0:2048]
        k0 = 2048
        dt, av, cums, du, dl = (r3[:, k0 + 64 * k:k0 + 64 * k + 64].rearrange("p (i h) -> p i h", i=NT)
                                for k in range(5))
        ea = r3[:, k0 + 320:k0 + 324]
        th = r3[:, k0 + 512:k0 + 1536].rearrange("p (b t) -> p b t", b=2)
        c0 = k0 + 1536
        thc = r3[:, c0 + 256:c0 + 1280].rearrange("p (m t) -> p m t", m=MI)
        ft1 = r2[:, 18500:19524].rearrange("p (b t) -> p b t", b=2)
        xcs = r3[:, k0 + 512:k0 + 1536].rearrange("p (m t) -> p m t", m=MI)
        BTs = r2[:, 14340:14852]
        btds = r2[:, 14852:15364].rearrange("p (i n) -> p i n", i=TPB)
        avs = r2[:, 15364:15380].rearrange("p (i h) -> p i h", i=TPB)
        gm = r3[:, c0:c0 + 256].rearrange("p (b t) -> p b t", b=2)
        ed = r3[:, c0 + 256:c0 + 1280].rearrange("p (b h t) -> p b h t", b=2, h=NH)
        ec = r3[:, c0 + 1280:c0 + 2304].rearrange("p (b h t) -> p b h t", b=2, h=NH)
        mm = r3[:, c0 + 2304:c0 + 3328].rearrange("p (b h t) -> p b h t", b=2, h=NH)
        cs = r3[:, c0 + 3328:c0 + 4352].rearrange("p (b h t) -> p b h t", b=2, h=NH)
        dtx = r3[:, c0 + 4352:c0 + 4864].rearrange("p (b h d) -> p b h d", b=2, h=NH)
        dtw = r3[:, c0 + 4864:c0 + 5376].rearrange("p (b h d) -> p b h d", b=2, h=NH)
        hst = r3[:, c0 + 5376:c0 + 5632].rearrange("p (h d) -> p h d", h=NH)
        yg = r3[:, c0 + 5632:c0 + 6144].rearrange("p (b m t) -> p b m t", b=2, m=MI)

        ps = ctx.enter_context(nc.psum_tensor("ps", [P, 8, 512], F32))
        qd_dram = nc.dram_tensor("q_split_rows", (NSPLIT, P, T), BF16, kind="Internal").ap()
        kd_dram = nc.dram_tensor("k_split_rows", (NSPLIT * KV_W, T), BF16, kind="Internal").ap()

        s_x = [sem(f"x_loaded{i}") for i in range(4)]
        s_const = sem("consts_loaded")
        s_wqkv = sem("qkv_weights_loaded")
        s_w0 = sem("summary_weights_loaded")
        s_wrest = sem("gate_router_weights_loaded")
        s_v = sem("dve_steps")
        s_a = sem("act_steps")
        s_g = sem("pool_steps")
        s_var = sem("variance_ready")
        s_sd = sem("root_ready")
        s_xn = sem("xn_ready")
        s_xnT = sem("xn_transposed")
        s_xnTc = sem("xnT_copied")
        s_wsc = sem("qkv_weights_scaled")
        s_qkvp = sem("qkv_projected")
        s_qkvc = sem("qkv_copied")
        s_rot = sem("rotated")
        s_sq = sem("squared")
        s_ssq = sem("square_sums")
        s_qksd = sem("qk_root")
        s_split = sem("splits_ready")
        s_splT = sem("splits_transposed")
        s_splTa = sem("splits_copied_by_act")
        s_splTv = sem("splits_copied_by_dve")
        s_scr = sem("splits_in_dram")
        s_qst = sem("stacks_loaded")
        s_pad = sem("stack_pads_zeroed")
        s_vp = sem("values_ready")
        s_sm = sem("summary_softmax_steps")
        s_rden = sem("sums_inverted")
        s_shift = sem("score_bound_ready")
        s_xti = sem("round_tiles_copied")
        s_mf = sem("shared_bank_filled")
        s_mr = sem("shared_bank_read")
        s_idb = sem("bf16_identity")

        s_summ = sem("chunk_means_ready")
        s_kv = sem("summary_kv_projected")
        s_kbd = sem("summary_kv_placed")
        s_gw = sem("summary_products_ready")
        s_gc = sem("summary_products_copied")
        s_sub = sem("summary_shifted")
        s_ex = sem("summary_exponentials")
        s_pr = sem("summary_probabilities")
        s_qk = sem("score_pairs")
        s_exp = sem("exponentials")
        s_msk = sem("diagonals_masked")
        s_pv = sem("value_products")
        s_vc = sem("group_values_copied")
        s_accc = sem("attention_block_copied")
        s_aT = sem("attention_transposed")
        s_aTc = sem("attention_T_copied")
        s_gp = sem("gate_projected")
        s_gt = sem("gate_ready")
        s_og = sem("gated")
        s_wo = sem("output_projected")
        s_xm = sem("x_mid_ready")
        s_sq2 = sem("x_mid_squared")
        s_ss2 = sem("x_mid_square_sums")
        s_sd2 = sem("x_mid_root")
        s_h2 = sem("h2_ready")
        s_h2T = sem("h2_transposed")
        s_h2Tc = sem("h2T_copied")
        s_lg = sem("router_logits")
        s_oh = sem("one_hot_ready")
        s_ohT = sem("one_hot_transposed")
        s_pen = sem("penalty_ready")
        s_moew = sem("expert_weights_loaded")
        s_up = sem("expert_up_products")
        s_sg = sem("expert_sigmoids")
        s_moea = sem("expert_activations")
        s_dn = sem("expert_down_products")
        s_yc = sem("expert_sums_copied")
        s_yt = sem("expert_sums_token_major")
        s_ohTc = sem("one_hot_rows_copied")
        s_whi = sem("expert_weights_high")
        s_wsp = sem("expert_weights_split")
        s_h2s = sem("h2_high_parts")
        s_h2l = sem("h2_low_parts")
        s_amh = sem("expert_products_high_parts")
        s_aml = sem("expert_products_split")
        s_ya = sem("expert_sums_added")
        s_l1w = sem("layer1_weights_loaded")
        s_var2 = sem("variance2_ready")
        s_sdl = sem("root2_ready")
        s_xn2 = sem("xn1_ready")
        s_xs = sem("xs_ready")
        s_xn2T = sem("xn1_transposed")
        s_xn2c = sem("xn1_T_copied")
        s_inp = sem("in_proj_scaled")
        s_pj = sem("ssm_projected")
        s_pja = sem("ssm_projections_read_by_act")
        s_pjv = sem("ssm_projections_read_by_dve")
        s_bt = sem("ssm_token_projected")
        s_btc = sem("ssm_token_copied")
        s_xcv = sem("convolved")
        s_xth = sem("convolution_tanh")
        s_dta = sem("dt_for_act")
        s_dtb = sem("dt_from_act")
        s_av = sem("decay_rates_ready")
        s_cum = sem("cumulative_decay")
        s_cumc = sem("cumulative_decay_copied")
        s_cstep = sem("chunk_dve_steps")
        s_stage = sem("block_operands_staged")
        s_c1 = sem("chunk_products")
        s_cd = sem("chunk_decay_difference")
        s_ce = sem("chunk_exponentials")
        s_cm = sem("chunk_operands_from_pool")
        s_cx = sem("chunk_operands_from_dve")
        s_cy = sem("chunk_outputs")
        s_cg = sem("chunk_gated")
        s_ch = sem("chunk_state_ready")
        s_co = sem("chunk_projected")
        s_ca = sem("chunk_added")
        s_fu = sem("ffn_up_products")
        s_ft = sem("ffn_tanh")
        s_fs = sem("ffn_scales_ready")
        s_fm = sem("ffn_silu_products")
        s_fg = sem("ffn_gated")
        s_f2 = sem("ffn_second_products")
        s_fg2 = sem("ffn_second_gelu")
        s_f3 = sem("ffn_third_products")
        s_fg3 = sem("ffn_third_gelu")
        s_f4 = sem("ffn_down_products")
        s_fr = sem("ffn_scaled")
        s_fin = sem("result_ready")
        s_zth = sem("z_tanh")
        s_xc = sem("convolution_silu")
        s_cst = sem("chunk_state_products")
        s_out = sem("result_stored")

        def key_tiles(qb):
            diag, full = list(range(TPB * qb + 1, TPB * qb + TPB)), list(range(TPB * qb))
            head = [TPB * qb]
            while diag:
                head += full[:1] + diag[:1]
                full, diag = full[1:], diag[1:]
            return head + full

        BLOCKS = [(qb, kt, max(0, kt - TPB * qb) * P) for qb in range(NB) for kt in key_tiles(qb)]
        FIRST = [min(k for k, blk in enumerate(BLOCKS) if blk[0] == qb) for qb in range(NB)]
        LAST = [max(k for k, blk in enumerate(BLOCKS) if blk[0] == qb) for qb in range(NB)]
        LAG = 2
        KB = len(BLOCKS)
        PAIRS = 2 * KB
        SBUFS, PBUFS = 3, 8
        DIAG = [k for k, (qb, kt, _) in enumerate(BLOCKS) if kt >= TPB * qb]

        SHARED = 7
        AUX = sorted([(8 * m + s, what, m) for m in range(NB) for s, what in
                      ((1, "SCORE"), (6, "TRANSPOSE"), (8, "OUTPUT"))]
                     + [(LAST[qb] + LAG + 2 if qb < NB - 1 else KB + LAG - 1, "ATT", qb) for qb in range(NB)])
        NAUX = len(AUX)
        SUMM_EXP = {8 * m + 3: m for m in range(NB)}

        WSPLIT = [(w1f[:, 0:2048], w1hf[:, 0:2048], w1lf[:, 0:2048]), (w2f, w2hf, w2lf),
                  (w1f[:, 2048:4096], w1hf[:, 2048:4096], w1lf[:, 2048:4096])]

        def summ_chunks(m):
            return (m + 1) * NC // NB

        LAYER1 = [("UP", 0), ("CHUNK", 0), ("UP", 1), ("UP", 2), ("UP", 3), ("CHUNK", 1), ("MID1", 0),
                  ("STATE", 0), ("MID1", 1), ("PROJECT", 0), ("CHUNK", 2), ("MID1", 2), ("STATE", 1),
                  ("MID1", 3), ("PROJECT", 1), ("CHUNK", 3), ("MID2", 0), ("STATE", 2), ("MID2", 1),
                  ("PROJECT", 2), ("MID2", 2), ("STATE", 3), ("MID2", 3), ("PROJECT", 3), ("DOWN", 0)]

        def ffn_bank(n):
            return 4 if n == 16 else 4 + (n + 1) % 4

        res_flat = res.rearrange("p i d -> p (i d)")

        def last_user(n, bufs, total):
            return max(m for m in range(total) if m % bufs == n % bufs)

        block = ctx.enter_context(nc.Block())

        @block.sync
        def _(sp):
            for q in range(4):
                sp.dma_start(res[:, 4 * q:4 * q + 4, :],
                             io["x"][512 * q:512 * q + 512, :].rearrange("(i p) d -> p i d", p=P)
                             ).then_inc(s_x[q], 16)
            sp.dma_start(consts[:, :], io["consts"]).then_inc(s_const, 16)
            sp.dma_start(wqkv, io["f_Wqkv"]).then_inc(s_wqkv, 16)
            sp.dma_start(bqkv, io["f_bqkv"].broadcast_to([P, QKV_W])).then_inc(s_wqkv, 16)
            sp.dma_start(qn_bc, io["f_qn"].broadcast_to([P, QD])).then_inc(s_wqkv, 16)
            sp.dma_start(kn_bc, io["f_kn"].broadcast_to([P, QD])).then_inc(s_wqkv, 16)
            sp.dma_start(ln1, io["f_ln1"]).then_inc(s_wqkv, 16)
            sp.dma_start(wqT, io["a_WqT"].rearrange("(j p) d -> p j d", p=P)).then_inc(s_w0, 16)
            sp.dma_start(wk0, io["a_Wk"]).then_inc(s_w0, 16)
            sp.dma_start(wv0, io["a_Wv"]).then_inc(s_w0, 16)
            sp.dma_start(wo0, io["a_Wo"].rearrange("(j p) d -> p j d", p=P)).then_inc(s_w0, 16)
            for dst, name in ((bq0, "a_bq"), (bk0, "a_bk"), (bv0, "a_bv")):
                sp.dma_start(dst, io[name]).then_inc(s_w0, 16)
            sp.dma_start(cmask, io["cmask"]).then_inc(s_w0, 16)
            sp.dma_start(bo0_bc, io["a_bo"].broadcast_to([P, D])).then_inc(s_w0, 16)
            for s in range(NSPLIT):
                sp.wait_ge(s_splTa, s + 1)
                sp.wait_ge(s_splTv, s + 1)
                sp.dma_start(qd_dram[s], qT[:, s, :]).then_inc(s_scr, 16)
            sp.wait_ge(s_splTa, 4)
            sp.wait_ge(s_splTv, 4)
            sp.dma_start(kd_dram, kT[0:NSPLIT * KV_W, :]).then_inc(s_scr, 16)
            sp.wait_ge(s_scr, 64)
            sp.wait_ge(s_pad, 1)
            for i in range(NSPLIT):
                sp.dma_start(kst[24 * i:24 * i + 24, :, :].rearrange("p g t -> p (g t)"),
                             kd_dram.rearrange("(r g) t -> r (g t)", g=NKV)).then_inc(s_qst, 16)
            for i in range(NSPLIT):
                sp.dma_start(qst[24 * i:24 * i + 24, :, :].rearrange("p h t -> p (h t)"),
                             qd_dram[i].rearrange("(d h) t -> d (h t)", h=NQ).unsqueeze(0).broadcast_to(
                                 [NSPLIT, QD, NQ * T])).then_inc(s_qst, 16)
            sp.wait_ge(s_pad, 2)
            for h in range(NQ):
                sp.dma_start(wg[QD * h:QD * h + QD, QD * h:QD * h + QD], io["f_Wg"]).then_inc(s_wrest, 16)
            for dst, name in ((wo, "f_Wo"), (wr, "f_Wr"), (ln2, "f_ln2"), (b2, "f_b2"), (row[:, 240:272], "f_b1c"),
                              (bgc, "f_bgc")):
                sp.dma_start(dst, io[name]).then_inc(s_wrest, 16)
            for dst, name, n in ((bo_bc, "f_bo", D), (br_bc, "f_br", E), (rank, "rank", E)):
                sp.dma_start(dst, io[name].broadcast_to([P, n])).then_inc(s_wrest, 16)
            sp.wait_ge(s_pv, KB * (NKV + 1))
            sp.dma_start(w1, io["f_W1"].rearrange("e p f -> p e f")).then_inc(s_moew, 16)
            sp.dma_start(w2, io["f_W2"].rearrange("e (c p) d -> p e c d", p=P)).then_inc(s_moew, 16)
            sp.wait_ge(s_h2Tc, NB)
            for dst, name in ((inp, "s_inT"), (f1, "g_w1T"), (f2, "g_w2T"),
                              (normw, "s_norm"), (convb, "s_convb"), (d2, "s_D"), (row[:, 284:292], "s_convw"),
                              (w1s, "g_w1s"), (w2s, "g_w2s"), (h1s, "g_h1s"), (h2s, "g_h2s")):
                sp.dma_start(dst, io[name]).then_inc(s_l1w, 16)
            sp.dma_start(owT, io["s_outT"].rearrange("(m p) d -> p m d", p=P)).then_inc(s_l1w, 16)
            for dst, name in ((fh1, "g_h1T"), (fh2, "g_h2T"), (f3, "g_w3T")):
                sp.dma_start(dst, io[name].rearrange("(k p) o -> p k o", p=P)).then_inc(s_l1w, 16)
            for dst, name, n in ((dtb, "s_dtb", NH), (alog, "s_Alog", NH), (w3s_bc, "g_w3s", D)):
                sp.dma_start(dst, io[name].broadcast_to([P, n])).then_inc(s_l1w, 16)
            for b in range(NB):
                sp.wait_ge(s_fin, b + 1)
                sp.dma_start(out[TB * b:TB * b + TB, :].rearrange("(i p) d -> p i d", p=P),
                             res[:, TPB * b:TPB * b + TPB, :]).then_inc(s_out, 16)
            sp.wait_ge(s_out, 16 * NB)

        @block.gpsimd
        def _(pool):
            step = Steps(pool, s_g)
            pool.memset(r2[64:P, :], 0.0).then_inc(s_pad, 1)
            pool.wait_ge(s_pad, 1)
            step.alone(pool.memset(vp[:, :, :, :], 0.0))
            pool.memset(vp[:, :, :, QD:QD + 1], 1.0).then_inc(s_vp, 1)
            step.alone(pool.memset(kbd[:, :, :, :], 0.0))
            step.alone(pool.memset(vbd[:, :, :, :], 0.0))
            pool.memset(wg, 0.0).then_inc(s_pad, 1)
            pool.wait_ge(s_pad, 2)
            pool.memset(qst[96:97, :, :], 1.0).then_inc(s_pad, 1)
            pool.wait_ge(s_pad, 3)
            pool.wait_ge(s_shift, 1)
            pool.tensor_scalar(kst[96:97, :, :], qst[96:97, 0:NKV, :], shift[96:97, :], None, ALU.mult
                               ).then_inc(s_pad, 1)
            pool.wait_ge(s_qst, 16 * 2 * NSPLIT)
            pool.wait_ge(s_pad, 4)
            pool.wait_ge(s_gw, 1)
            pool.memset(pr[:, :, :], 0.0).then_inc(s_pad, 1)
            pool.sem_inc(s_pv, KB)
            xnT_blocks = xnT.rearrange("p (m c) -> p m c", m=NB)
            pool.wait_ge(s_pad, 5)
            with pool.Fori(0, NKV) as g:
                pool.wait_ge(s_pv, g * KB + KB)
                pool.tensor_copy(xti, xnT_blocks[:, :, bass.ds(g * P, P)]).then_inc(s_xti, 1)
                for k in DIAG:
                    off = BLOCKS[k][2]
                    for n in (2 * k, 2 * k + 1):
                        pool.wait_ge(s_exp, g * PAIRS + (PAIRS + n + 1))
                        blk = probs[:, n % PBUFS, :, off:off + P]
                        pool.tensor_tensor(blk, blk, along(tri, 2), ALU.mult).then_inc(s_msk, 1)
            pool.wait_ge(s_mr, NKV * NAUX + 1)
            step.alone(pool.memset(onee, 1.0))
            pool.affine_select(out=onee, in_=onee, compare_op=ALU.is_equal, fill=0.0, base=0,
                               pattern=[[-1, E], [0, P]], channel_multiplier=1).then_inc(s_idb, 1)
            for n, (w, hi, lo) in enumerate(WSPLIT):
                pool.wait_ge(s_whi, n + 1)
                pool.tensor_tensor(lo, w, hi, ALU.subtract).then_inc(s_wsp, 1)
                pool.wait_ge(s_wsp, n + 1)
            pool.wait_ge(s_ya, NB + 1)
            pool.memset(xp[:, :, 0:KW - 1], 0.0).then_inc(s_pad, 1)
            pool.wait_ge(s_pad, 6)
            pool.memset(hst, 0.0).then_inc(s_ch, 1)
            pool.wait_ge(s_pja, 3 * NB)
            pool.wait_ge(s_pjv, 3 * NB)
            pool.wait_ge(s_xc, NB)
            pool.wait_ge(s_av, 1)
            pool.wait_ge(s_btc, 6)
            pool.sem_inc(s_cm, 4)
            with pool.Fori(0, NB) as blk_i:
                toks = bass.ds(blk_i * TB, TB)
                pool.wait_ge(s_cg, blk_i * TPB + 1)
                pool.tensor_copy(xcs, xc[:, :, toks]).then_inc(s_stage, 1)
                pool.tensor_copy(BTs, BT[:, toks]).then_inc(s_stage, 1)
                pool.tensor_copy(avs, av[:, bass.ds(blk_i * TPB, TPB), :]).then_inc(s_stage, 1)
                pool.tensor_copy(btds, btd[:, bass.ds(blk_i * TPB, TPB), 0:P]).then_inc(s_stage, 1)
                for j in range(TPB):
                    b = j % 2
                    pool.wait_ge(s_cy, blk_i * TPB + (j + 1))
                    pool.wait_ge(s_ce, blk_i * (2 * TPB) + (2 * j + 3))
                    pool.wait_ge(s_cx, blk_i * (2 * TPB) + (2 * j + 3))
                    pool.tensor_tensor(mm[:, b], ed[:, b], along(gm[:, b, :], NH), ALU.mult).then_inc(s_cm, 1)
                    pool.wait_ge(s_ce, blk_i * (2 * TPB) + (2 * j + 4))
                    pool.tensor_tensor(cs[:, b], ec[:, b], along(CT[:, bass.ds(blk_i * TB + j * P, P)], NH),
                                       ALU.mult).then_inc(s_cm, 1)

        @block.scalar
        def _(act):
            step = Steps(act, s_a)
            act.wait_ge(s_var, 1)
            act.activation(sd, mv[:, :, 1], ACT.Sqrt, bias=LN_EPS).then_inc(s_sd, 1)
            act.wait_ge(s_var, 2)
            act.activation(sd2, ms, ACT.Sqrt, bias=RMS_EPS).then_inc(s_sd, 1)
            for b in range(NB):
                act.wait_ge(s_xnT, b + 1)
                act.activation(xnT[:, b * TB:b * TB + TB], ps[:, b, :], ACT.Copy).then_inc(s_xnTc, 1)
            act.wait_ge(s_rot, 1)
            act.activation(sq, rot, ACT.Square).then_inc(s_sq, 1)
            act.wait_ge(s_ssq, 1)
            act.activation(rr, ssq, ACT.Sqrt, bias=RMS_EPS, scale=1.0 / QD).then_inc(s_qksd, 1)
            for n in range(0, 8, 2):
                act.wait_ge(s_splT, n + 1)
                src = ps[:, n, :].bitcast(BF16)
                if n < 6:
                    act.activation(qT[:, n // 2, 0:1024], src, ACT.Copy).then_inc(s_splTa, 1)
                else:
                    act.activation(kT[0:96, 0:1024], src[0:96, :], ACT.Copy).then_inc(s_splTa, 1)
            act.wait_ge(s_gw, 1)
            act.activation(gmat, ps[:, 1, :].rearrange("p (h c) -> p h c", h=HEADS), ACT.Copy).then_inc(s_gc, 1)
            act.activation(g0, ps[:, 2, :].rearrange("p (h c) -> p h c", h=HEADS), ACT.Copy).then_inc(s_gc, 1)
            act.activation(vw, ps[:, 3, :].rearrange("p (q d) -> p q d", q=4), ACT.Copy).then_inc(s_gc, 1)
            act.sem_inc(s_exp, PAIRS)
            with act.Fori(0, NKV) as g:
                for k, (qb, kt, off) in enumerate(BLOCKS):
                    for n in (2 * k, 2 * k + 1):
                        act.wait_ge(s_qk, g * PAIRS + (n + 1))
                        free = KB + (n - PBUFS) // 2 + 1 if n >= PBUFS else last_user(n, PBUFS, PAIRS) // 2 + 1
                        act.wait_ge(s_pv, g * KB + free)
                        b = 2 * (n % SBUFS)
                        act.activation(probs[:, n % PBUFS, :, off:TB], ps[:, b:b + 2, off:TB], ACT.Exp
                                       ).then_inc(s_exp, 1)
                    if k in SUMM_EXP:
                        m = SUMM_EXP[k]
                        act.wait_ge(s_sub, g * NB + (m + 1))
                        blk = sc[:, m % 2, :, 0:summ_chunks(m)]
                        act.activation(blk, blk, ACT.Exp).then_inc(s_ex, 1)
            for b in range(NB):
                act.wait_ge(s_aT, b + 1)
                act.activation(oT[:, b * TB:b * TB + TB], ps[:, 4 + b, :], ACT.Copy).then_inc(s_aTc, 1)
            act.wait_ge(s_wrest, 16 * 25)
            for b in range(NB):
                act.wait_ge(s_gp, b + 1)
                act.activation(gate[:, b * TB:b * TB + TB], ps[:, b, :], ACT.Sigmoid, bias=bgc).then_inc(s_gt, 1)
            for b in range(NB):
                act.wait_ge(s_xm, b + 1)
                act.activation(sqm[:, TPB * b:TPB * b + TPB, :], xn[:, TPB * b:TPB * b + TPB, :], ACT.Square
                               ).then_inc(s_sq2, 1)
            act.wait_ge(s_moew, 32)
            for w, hi, _ in WSPLIT:
                act.activation(hi, w, ACT.Copy).then_inc(s_whi, 1)
            act.wait_ge(s_ss2, NB)
            act.activation(sdm, ssq2, ACT.Sqrt, bias=RMS_EPS, scale=1.0 / D).then_inc(s_sd2, 1)
            for b in range(NB):
                act.wait_ge(s_h2T, b + 1)
                act.activation(h2T[:, b * TB:b * TB + TB], ps[:, b, :], ACT.Copy, scale=ln2).then_inc(s_h2Tc, 1)
            for b in range(NB):
                act.wait_ge(s_h2Tc, b + 1)
                act.activation(h2h[:, b * TB:b * TB + TB], h2T[:, b * TB:b * TB + TB], ACT.Copy).then_inc(s_h2s, 1)
            act.wait_ge(s_pen, 1)
            act.activation(ohT, ps[0:E, 4:8, :].rearrange("p b t -> p (b t)"), ACT.Copy).then_inc(s_ohTc, 1)
            act.sem_inc(s_yc, 1)
            with act.Fori(0, NB) as tb:
                for n in range(E * FC):
                    e, c = divmod(n, FC)
                    act.wait_ge(s_up, tb * (E * FC) + (n + 1))
                    free = E * FC + n - 2 if n >= 3 else last_user(n, 3, E * FC) + 1
                    act.wait_ge(s_moea, tb * (E * FC) + free)
                    act.activation(sg[:, n % 3, :], ps[:, 2 * (n % 3) + 1, :], ACT.Sigmoid,
                                   bias=b1c[:, e, FC + c:FC + c + 1]).then_inc(s_sg, 1)
                act.wait_ge(s_dn, tb * (E * FC) + 2 * E * FC)
                act.wait_ge(s_yt, tb + 1)
                act.activation(yT, ps[:, 6, :], ACT.Copy).then_inc(s_yc, 1)
            act.wait_ge(s_var2, 1)
            act.activation(sd, mv[:, :, 1], ACT.Sqrt, bias=LN_EPS).then_inc(s_sdl, 1)
            act.wait_ge(s_var2, 2)
            act.activation(sd2, ms, ACT.Sqrt, bias=RMS_EPS).then_inc(s_sdl, 1)
            for b in range(2 * NB):
                act.wait_ge(s_xn2T, b + 1)
                dst = xnT if b < NB else xsT
                act.activation(dst[:, b % NB * TB:b % NB * TB + TB], ps[:, b, :], ACT.Copy).then_inc(s_xn2c, 1)
            for b in range(NB):
                toks = slice(b * TB, b * TB + TB)
                for k in range(5):
                    u = 6 * b + k
                    act.wait_ge(s_pj, u + 1)
                    if k < 2:
                        if b >= 1:
                            act.wait_ge(s_pjv, 3 * (b - 1) + k + 1)
                        act.activation(th[:, k, :], ps[:, u % 8, :], ACT.Tanh, scale=0.5).then_inc(s_zth, 1)
                    else:
                        dst = xp[:, k - 2, KW - 1 + b * TB:KW - 1 + b * TB + TB] if k < 4 else CT[:, toks]
                        act.activation(dst, ps[:, u % 8, :], ACT.Copy).then_inc(s_pja, 1)
            for b in range(NB):
                act.wait_ge(s_xcv, b + 1)
                if b >= 1:
                    act.wait_ge(s_xc, b)
                act.activation(thc, xc[:, :, b * TB:b * TB + TB], ACT.Tanh, scale=0.5).then_inc(s_xth, 1)
            act.wait_ge(s_dta, 1)
            act.activation(ea, alog, ACT.Exp).then_inc(s_dtb, 1)
            act.activation(dl, dl, ACT.Exp).then_inc(s_dtb, 1)
            act.wait_ge(s_dtb, 2)
            act.activation(dl, dl, ACT.Ln, bias=1.0).then_inc(s_dtb, 1)
            act.sem_inc(s_fg3, FO)
            act.sem_inc(s_ce, 2)
            with act.Fori(0, NB) as blk_i:
                for what, o in LAYER1:
                    if what == "UP":
                        act.wait_ge(s_fu, blk_i * FO + (o + 1))
                        free = FO + o - 1 if o >= 2 else FO - 1 + o
                        act.wait_ge(s_fm, blk_i * FO + free)
                        act.activation(fth[:, o % 2, :], ps[:, ffn_bank(2 * o), :], ACT.Tanh,
                                       scale=w1sh[:, o:o + 1]).then_inc(s_ft, 1)
                    elif what == "MID1":
                        act.wait_ge(s_f2, blk_i * FO + (FO + o + 1))
                        act.wait_ge(s_f3, blk_i * FO + FO)
                        act.activation(fb[:, o, :], ps[:, ffn_bank(8 + o), :], ACT.Gelu, scale=h1s[:, o:o + 1]
                                       ).then_inc(s_fg2, 1)
                    elif what == "MID2":
                        act.wait_ge(s_f3, blk_i * FO + (FO + o + 1))
                        act.activation(fa[:, o, :], ps[:, ffn_bank(12 + o), :], ACT.Gelu, scale=h2s[:, o:o + 1]
                                       ).then_inc(s_fg3, 1)
                    elif what == "CHUNK":
                        b = o % 2
                        act.wait_ge(s_cd, blk_i * TPB + (o + 1))
                        act.activation(ed[:, b], ed[:, b], ACT.Exp).then_inc(s_ce, 1)
                        act.wait_ge(s_c1, blk_i * TPB + (o + 1))
                        act.wait_ge(s_cm, blk_i * (2 * TPB) + (2 * o + 2))
                        act.wait_ge(s_ch, blk_i * TPB + (o + 1))
                        act.activation(ec[:, b], ps[:, 1, :].rearrange("p (h t) -> p h t", h=NH), ACT.Exp
                                       ).then_inc(s_ce, 1)

        @block.tensor
        def _(pe):
            pe.wait_ge(s_const, 16)
            for b in range(NB):
                for i in range(TPB * b, TPB * b + TPB):
                    pe.wait_ge(s_xn, i + 1)
                    m = pe.transpose(ps[:, b, (i % TPB) * P:(i % TPB) * P + P], xn[:, i, :], ident)
                m.then_inc(s_xnT, 1)
            pe.wait_ge(s_wsc, 1)
            for i in range(NT):
                pe.wait_ge(s_xnTc, i // TPB + 1)
                if i >= 8:
                    pe.wait_ge(s_qkvc, i - 8 + 2 - i % 2)
                m = pe.matmul(ps[:, 4 + (i // 2) % 4, (i % 2) * QKV_W:(i % 2) * QKV_W + QKV_W],
                              xnT[:, i * P:i * P + P], wqkv, start=True, stop=True)
                m.then_inc(s_qkvp, 1)
            pe.wait_ge(s_split, 1)
            pe.wait_ge(s_idb, 1)
            pe.wait_ge(s_qkvc, NT)
            for n in range(8):
                dst = ps[:, n, :].bitcast(BF16)
                for i in range(8 * (n % 2), 8 * (n % 2) + 8):
                    c = (i % 8) * P
                    if n < 6:
                        m = pe.transpose(dst[:, c:c + P], qs[:, i, n // 2, :], identb)
                    else:
                        m = pe.transpose(dst[0:96, c:c + P],
                                         ks[:, i, :, :].rearrange("p s c -> p (s c)"), identb)
                m.then_inc(s_splT, 1)
            pe.wait_ge(s_splTa, 4)
            pe.wait_ge(s_splTv, 4)
            pe.wait_ge(s_w0, 16 * 9)
            pe.wait_ge(s_summ, 2)
            for j in range(HC):
                pe.matmul(ps[:, 0, NC * j:NC * j + NC], wk0[:, P * j:P * j + P], summT, start=True, stop=True)
            for j in range(HC):
                m = pe.matmul(ps[:, 0, 256 + NC * j:256 + NC * j + NC], wv0[:, P * j:P * j + P], summT,
                              start=True, stop=True)
            m.then_inc(s_kv, 1)
            pe.wait_ge(s_kbd, 2)
            for j in range(HC):
                kj = kbd[:, j].rearrange("p a c -> p (a c)")
                pe.matmul(ps[:, 1, 64 * j:64 * j + 64], wqT[:, j, :], kj, start=True, stop=True)
                pe.matmul(ps[:, 2, 64 * j:64 * j + 64], bq0[:, j:j + 1].broadcast_to([P, P]), kj,
                          start=True, stop=True)
            for j in range(HC):
                m = pe.matmul(ps[64 * (j % 2):64 * (j % 2) + 64, 3, P * (j // 2):P * (j // 2) + P],
                              vbd[:, j].rearrange("p a c -> p (a c)"), wo0[:, j, :], start=True, stop=True)
            m.then_inc(s_gw, 1)
            pe.wait_ge(s_gc, 3)
            pe.wait_ge(s_qst, 16 * 2 * NSPLIT)
            pe.wait_ge(s_pad, 5)
            qst_flat = r2[:, 0:16384].bitcast(BF16)
            kst_flat = r2[:, 16384:20480].bitcast(BF16)
            with pe.Fori(0, NKV) as g:
                for k in range(KB + LAG):
                    if k < KB:
                        qb, kt, off = BLOCKS[k]
                        for pair in range(2):
                            n = 2 * k + pair
                            free = PAIRS + n - SBUFS + 1 if n >= SBUFS else last_user(n, SBUFS, PAIRS) + 1
                            pe.wait_ge(s_exp, g * PAIRS + free)
                            for h in range(2):
                                m = pe.matmul(ps[:, 2 * (n % SBUFS) + h, off:TB],
                                              kst_flat[:, bass.ds(g * T + kt * P, P)],
                                              qst_flat[:, bass.ds(g * (REP * T) + ((2 * pair + h) * T + qb * TB + off),
                                                                  TB - off)],
                                              start=True, stop=True)
                            m.then_inc(s_qk, 1)
                    if k >= LAG:
                        v = k - LAG
                        qb, kt, off = BLOCKS[v]
                        if v == 0:
                            pe.wait_ge(s_vc, g + 1)
                        if v == FIRST[qb]:
                            pe.wait_ge(s_accc, g * NB + (qb + 1))
                        if kt >= TPB * qb:
                            pe.wait_ge(s_msk, g * (2 * len(DIAG)) + 2 * (DIAG.index(v) + 1))
                        else:
                            pe.wait_ge(s_exp, g * PAIRS + (PAIRS + 2 * v + 2))
                        for j in range(REP):
                            m = pe.matmul(ps[32 * j:32 * j + 32, 6, off:TB], vc[:, kt, :],
                                          probs[:, (2 * v + j // 2) % PBUFS, j % 2, off:TB],
                                          start=(v == FIRST[qb]), stop=(v == LAST[qb]))
                        m.then_inc(s_pv, 1)
                    for n, (_, what, m) in enumerate(AUX):
                        if AUX[n][0] != k:
                            continue
                        pe.wait_ge(s_mr, g * NAUX + (n + 1))
                        if what == "SCORE":
                            pe.wait_ge(s_xti, g + 1)
                            w = summ_chunks(m)
                            a = pe.matmul(ps[:, SHARED, 0:HEADS * w].rearrange("p (h c) -> p h c", h=HEADS),
                                          xti[:, m, :], gmat[:, :, 0:w], start=True, stop=True)
                        elif what == "TRANSPOSE":
                            pe.wait_ge(s_pr, g * NB + (m + 1))
                            for q in range(4):
                                a = pe.transpose(ps[:, SHARED, P * q:P * q + P], pr[:, m, P * q:P * q + P], ident)
                        elif what == "OUTPUT":
                            for q in range(4):
                                a = pe.matmul(ps[:, SHARED, 0:D], ptr[:, P * q:P * q + P], vw[:, q, :],
                                              start=(q == 0), stop=(q == 3))
                        else:
                            pe.wait_ge(s_accc, g * NB + (m + 2))
                            for i in range(TPB):
                                a = pe.transpose(ps[:, SHARED, P * i:P * i + P], accT[:, m % 2, P * i:P * i + P],
                                                 ident)
                        a.then_inc(s_mf, 1)
            for b in range(NB):
                pe.wait_ge(s_mr, NKV * NAUX + 1)
                for i in range(TPB):
                    m = pe.transpose(ps[:, 4 + b, P * i:P * i + P], att[:, TPB * b + i, :], ident)
                m.then_inc(s_aT, 1)
            pe.wait_ge(s_wrest, 16 * 25)
            for b in range(NB):
                pe.wait_ge(s_aTc, b + 1)
                pe.matmul(ps[:, b, :], wg, oT[:, b * TB:b * TB + TB], start=True, stop=True).then_inc(s_gp, 1)
            for b in range(NB):
                pe.wait_ge(s_og, b + 1)
                for i in range(TPB):
                    t = (TPB * b + i) * P
                    m = pe.matmul(ps[:, 4 + b, P * i:P * i + P], oT[:, t:t + P], wo, start=True, stop=True)
                m.then_inc(s_wo, 1)
            for b in range(NB):
                pe.wait_ge(s_h2, TPB * (b + 1))
                for i in range(TPB):
                    m = pe.transpose(ps[:, b, P * i:P * i + P], h2[:, TPB * b + i, :], ident)
                m.then_inc(s_h2T, 1)
            pe.wait_ge(s_xm, NB)
            for i in range(NT):
                pe.wait_ge(s_h2Tc, i // TPB + 1)
                m = pe.matmul(ps[:, 4, E * i:E * i + E], h2T[:, i * P:i * P + P], wr, start=True, stop=True)
            m.then_inc(s_lg, 1)
            pe.wait_ge(s_oh, 1)
            for i in range(NT):
                m = pe.transpose(ps[0:E, 4 + i // TPB, P * (i % TPB):P * (i % TPB) + P], oh[:, i, :], ident)
            m.then_inc(s_ohT, 1)
            pe.wait_ge(s_wsp, 2)
            pe.wait_ge(s_h2l, NB)
            pe.wait_ge(s_pen, 1)
            pe.wait_ge(s_idb, 2)
            ES = E * FC
            pe.sem_inc(s_dn, ES)
            pe.sem_inc(s_yt, 1)
            with pe.Fori(0, NB) as tb:
                for n in range(ES + 2):
                    if n < ES:
                        e, c = divmod(n, FC)
                        free = ES + n - 2 if n >= 3 else last_user(n, 3, ES) + 1
                        if n == 2:
                            pe.wait_ge(s_ohTc, 1)
                        if n == ES // 2:
                            pe.wait_ge(s_wsp, 3)
                        pe.wait_ge(s_moea, tb * ES + free)
                        toks = bass.ds(tb * TB, TB)
                        b = 2 * (n % 3)
                        halves = [(w1h[:, e, a:a + P], w1l[:, e, a:a + P]) for a in (P * c, HID + P * c)]
                        x = (h2h[:, toks], h2l[:, toks])
                        product(pe, ps[:, b + 1, :], halves[1], x, start=True, stop=False)
                        pe.matmul(ps[:, b + 1, :], onee[:, e, :], pen[:, toks], start=False, stop=True)
                        product(pe, ps[:, b, :], halves[0], x, start=True, stop=True).then_inc(s_up, 1)
                    if n == 0:
                        pe.wait_ge(s_ohTc, 1)
                        pe.wait_ge(s_yc, tb + 1)
                        pe.matmul(ps[:, 6, :], b2, ohT[:, toks], start=True, stop=False)
                    if n >= 2:
                        e, c = divmod(n - 2, FC)
                        pe.wait_ge(s_aml, tb * ES + (n - 1))
                        product(pe, ps[:, 6, :], (w2h[:, e, c, :], w2l[:, e, c, :]),
                                (amh[:, (n - 2) % 3, :], aml[:, (n - 2) % 3, :]),
                                start=False, stop=(n == ES + 1)).then_inc(s_dn, 1)
                pe.wait_ge(s_yc, tb + 2)
                pe.wait_ge(s_ya, tb + 1)
                for i in range(TPB):
                    m = pe.transpose(ps[:, 7, P * i:P * i + P], yT[:, P * i:P * i + P], ident)
                m.then_inc(s_yt, 1)
            pe.wait_ge(s_ya, NB + 1)
            for b in range(2 * NB):
                for i in range(TPB):
                    t = b % NB * TPB + i
                    if b < NB:
                        pe.wait_ge(s_xn2, t + 1)
                    else:
                        pe.wait_ge(s_xs, t + 1)
                    m = pe.transpose(ps[:, b, P * i:P * i + P], (xn if b < NB else xs)[:, t, :], ident)
                m.then_inc(s_xn2T, 1)
            def bank_read(u):
                b, k = divmod(u, 6)
                pe.wait_ge(s_pja if 2 <= k <= 4 else s_pjv, 3 * b + (k - 1 if 2 <= k <= 4 else min(k, 2) + 1))

            pe.wait_ge(s_inp, 1)
            pe.wait_ge(s_xn2c, 2 * NB)
            for u in range(6 * NB):
                b, k = divmod(u, 6)
                if u >= 8:
                    bank_read(u - 8)
                pe.matmul(ps[:, u % 8, :], inp[:, P * k:P * k + P], xsT[:, b * TB:b * TB + TB],
                          start=True, stop=True).then_inc(s_pj, 1)
            for i in range(NT):
                u = 6 * NB + i // 3
                if i % 3 == 0:
                    bank_read(u - 8)
                m = pe.matmul(ps[:, u % 8, 132 * (i % 3):132 * (i % 3) + 132], xsT[:, i * P:i * P + P],
                              inp[:, 640:772], start=True, stop=True)
                if i % 3 == 2 or i == NT - 1:
                    m.then_inc(s_bt, 1)
            pe.wait_ge(s_av, 1)
            pe.wait_ge(s_pja, 3 * NB)
            pe.wait_ge(s_pjv, 3 * NB)
            pe.matmul(ps[:, 6, 0:NT * NH], tri, av.rearrange("p i h -> p (i h)"), start=True, stop=True
                      ).then_inc(s_cum, 1)
            pe.wait_ge(s_cumc, 1)
            pe.wait_ge(s_btc, 6)
            pe.wait_ge(s_fs, 1)
            for credit, n in ((s_f2, FO), (s_f3, FO), (s_f4, 1), (s_cy, 2), (s_cst, 2), (s_co, 2)):
                pe.sem_inc(credit, n)
            with pe.Fori(0, NB) as blk_i:
                toks = bass.ds(blk_i * TB, TB)
                for what, o in LAYER1:
                    if what == "UP":
                        if o >= 2:
                            pe.wait_ge(s_fg, blk_i * FO + (o - 1))
                        if o == 1:
                            pe.wait_ge(s_fr, blk_i + 1)
                        pe.matmul(ps[:, ffn_bank(2 * o), :], f1[:, P * o:P * o + P], xnT[:, toks],
                                  start=True, stop=True)
                        pe.matmul(ps[:, ffn_bank(2 * o + 1), :], f2[:, P * o:P * o + P], xnT[:, toks],
                                  start=True, stop=True).then_inc(s_fu, 1)
                    elif what == "MID1":
                        pe.wait_ge(s_fg, blk_i * FO + FO)
                        for k in range(FO):
                            m = pe.matmul(ps[:, ffn_bank(8 + o), :], fh1[:, k, P * o:P * o + P], fa[:, k, :],
                                          start=(k == 0), stop=(k == FO - 1))
                        m.then_inc(s_f2, 1)
                    elif what == "MID2":
                        pe.wait_ge(s_fg2, blk_i * FO + FO)
                        for k in range(FO):
                            m = pe.matmul(ps[:, ffn_bank(12 + o), :], fh2[:, k, P * o:P * o + P], fb[:, k, :],
                                          start=(k == 0), stop=(k == FO - 1))
                        m.then_inc(s_f3, 1)
                    elif what == "DOWN":
                        pe.wait_ge(s_fg3, blk_i * FO + 2 * FO)
                        for i in range(TPB):
                            for k in range(FO):
                                m = pe.matmul(ps[:, ffn_bank(16), P * i:P * i + P], fa[:, k, P * i:P * i + P],
                                              f3[:, k, :], start=(k == 0), stop=(k == FO - 1))
                        m.then_inc(s_f4, 1)
                    elif what == "CHUNK":
                        pe.wait_ge(s_stage, blk_i * 4 + 3)
                        pe.wait_ge(s_cx, blk_i * (2 * TPB) + (2 * o + 2))
                        pe.wait_ge(s_ce, blk_i * (2 * TPB) + (2 * o + 2))
                        pe.matmul(ps[:, 0, 0:P], BTs[:, P * o:P * o + P], CT[:, bass.ds(blk_i * TB + o * P, P)],
                                  start=True, stop=True)
                        for m_ in range(MI):
                            pe.transpose(ps[:, 0, P + P * m_:2 * P + P * m_], xcs[:, m_, P * o:P * o + P], ident)
                        for h in range(NH):
                            m = pe.matmul(ps[:, 1, P * h:P * h + P], avs[:, o, h:h + 1].broadcast_to([P, P]), tri,
                                          start=True, stop=True)
                        m.then_inc(s_c1, 1)
                    elif what == "STATE":
                        b = o % 2
                        pe.wait_ge(s_stage, blk_i * 4 + 4)
                        pe.wait_ge(s_cm, blk_i * (2 * TPB) + (2 * o + 6))
                        pe.wait_ge(s_cx, blk_i * (2 * TPB) + (2 * o + 4))
                        pe.wait_ge(s_ch, blk_i * TPB + (o + 2))
                        pe.wait_ge(s_ca, blk_i * TPB + (o + 1))
                        for h in range(NH):
                            dst = ps[PD * (h % 2):PD * (h % 2) + PD, 2, P * (h // 2):P * (h // 2) + P]
                            pe.matmul(dst, dtx[:, b, h, :], mm[:, b, h, :], start=True, stop=False)
                            m = pe.matmul(dst, hst[:, h, :], cs[:, b, h, :], start=False, stop=True)
                        m.then_inc(s_cy, 1)
                        pe.matmul(ps[:, 3, 0:DI], btds[:, o, :], dtw[:, b].rearrange("p h d -> p (h d)"),
                                  start=True, stop=True).then_inc(s_cst, 1)
                    else:
                        pe.wait_ge(s_cg, blk_i * TPB + (o + 2))
                        for m_ in range(MI):
                            m = pe.matmul(ps[:, 2, 2 * P:2 * P + D], yg[:, o % 2, m_, :], owT[:, m_, :],
                                          start=(m_ == 0), stop=(m_ == MI - 1))
                        m.then_inc(s_co, 1)

        @block.vector
        def _(dve):
            step = Steps(dve, s_v)
            for i in range(NT):
                if i % TPB == 0:
                    dve.wait_ge(s_x[i // TPB], 16)
                step.mark(dve.bn_stats(stats[:, i, :], res[:, i, :]))
            step.settle()
            for i in range(NT):
                m = dve.bn_aggr(mv[:, i, :], stats[:, i, :])
            m.then_inc(s_var, 1)
            dve.wait_ge(s_sd, 1)
            step.alone(dve.reciprocal(rstd, sd))
            for i in range(NT):
                dve.tensor_scalar(xn[:, i, :], res[:, i, :], mv[:, i, 0:1], rstd[:, i:i + 1],
                                  ALU.subtract, ALU.mult).then_inc(s_xn, 1)
            step.alone(dve.tensor_tensor(ms, mv[:, :, 1], rstd, ALU.mult))
            dve.tensor_tensor(ms, ms, rstd, ALU.mult).then_inc(s_var, 1)
            dve.wait_ge(s_wqkv, 16 * 5)
            dve.tensor_scalar(wqkv, wqkv, ln1, None, ALU.mult).then_inc(s_wsc, 1)
            dve.wait_ge(s_const, 16)
            dve.tensor_copy(identb, ident).then_inc(s_idb, 1)
            step.alone(dve.tensor_tensor(kw, qn_bc, kn_bc, ALU.mult))
            step.mark(dve.tensor_scalar(kw, kw, QD ** -0.5, None, ALU.mult))
            step.mark(dve.tensor_reduce(mx2[:, 0:1], qn_bc, X_AXIS, ALU.max, apply_absolute_value=True))
            step.mark(dve.tensor_reduce(mx2[:, 1:2], kn_bc, X_AXIS, ALU.max, apply_absolute_value=True))
            step.settle()
            step.alone(dve.tensor_tensor(shift, mx2[:, 0:1], mx2[:, 1:2], ALU.mult))
            dve.tensor_scalar(shift, shift, -(QD ** 0.5), None, ALU.mult).then_inc(s_shift, 1)
            dve.wait_ge(s_sd, 2)
            step.alone(dve.reciprocal(hs, sd2))
            for i in range(NT):
                dve.wait_ge(s_qkvp, i - i % 2 + 2)
                src = ps[:, 4 + (i // 2) % 4, (i % 2) * QKV_W:(i % 2) * QKV_W + QKV_W]
                dve.scalar_tensor_tensor(qkv[:, i, :], src, hs[:, i:i + 1], bqkv, ALU.mult, ALU.add
                                         ).then_inc(s_qkvc, 1)
            dve.wait_ge(s_qkvc, NT)
            qk = qkv[:, :, 0:160].rearrange("p i (d h) -> p i d h", d=QD)
            c_b = cosT.unsqueeze(3).broadcast_to([P, NT, 4, 20])
            s_b = sinT.unsqueeze(3).broadcast_to([P, NT, 4, 20])
            for half, (wa, wb, op) in enumerate(((c_b, s_b, ALU.subtract), (s_b, c_b, ALU.add))):
                step.mark(dve.tensor_tensor(rot_a, qk[:, :, 0:4, :], wa, ALU.mult))
                step.mark(dve.tensor_tensor(rot_b, qk[:, :, 4:8, :], wb, ALU.mult))
                step.settle()
                m = dve.tensor_tensor(rot[:, :, 4 * half:4 * half + 4, :], rot_a, rot_b, op)
                if half == 0:
                    step.alone(m)
            m.then_inc(s_rot, 1)
            dve.wait_ge(s_vp, 1)
            dve.tensor_copy(vp[:, :, :, 0:QD], qkv[:, :, 160:192].rearrange("p i (g d) -> p i g d", d=QD)
                            ).then_inc(s_vp, 1)
            dve.wait_ge(s_sq, 1)
            dve.tensor_reduce(ssq, sq.rearrange("p i d h -> p i h d"), X_AXIS, ALU.add).then_inc(s_ssq, 1)
            dve.wait_ge(s_qksd, 1)
            step.alone(dve.reciprocal(ssq, rr))
            step.alone(dve.tensor_tensor(rot, rot, ssq.rearrange("p (i h) -> p i h", i=NT).unsqueeze(2).broadcast_to(
                [P, NT, QD, 20]), ALU.mult))
            kr = rot[:, :, :, NQ:20]
            step.alone(dve.tensor_tensor(kr, kr, over(along(kw, NT), NKV),
                                         ALU.mult))
            by_head = lambda split: split.rearrange("p i (d h) -> p i d h", d=QD)
            for s in range(NSPLIT):
                parts = ((by_head(qs[:, :, s, :]), rot[:, :, :, 0:NQ]), (by_head(ks[:, :, s, :]), kr))
                for spl, src in parts:
                    step.mark(dve.tensor_copy(spl, src))
                step.settle()
                if s < NSPLIT - 1:
                    for spl, src in parts:
                        step.mark(dve.tensor_tensor(src, src, spl, ALU.subtract))
                    step.settle()
            dve.sem_inc(s_split, 1)
            for n in range(1, 8, 2):
                dve.wait_ge(s_splT, n + 1)
                src = ps[:, n, :].bitcast(BF16)
                if n < 6:
                    dve.tensor_copy(qT[:, n // 2, 1024:2048], src).then_inc(s_splTv, 1)
                else:
                    dve.tensor_copy(kT[0:96, 1024:2048], src[0:96, :]).then_inc(s_splTv, 1)
            step.mark(dve.tensor_reduce(summT[:, 1:NC],
                                        xnT[:, 1:1 + CHUNK * (NC - 1)].rearrange("p (c t) -> p c t", t=CHUNK),
                                        X_AXIS, ALU.add))
            step.settle()
            step.mark(dve.tensor_scalar(summT[:, 1:NC], summT[:, 1:NC], 1.0 / CHUNK, None, ALU.mult))
            dve.tensor_copy(summT[:, 0:1], xnT[:, 0:1]).then_inc(s_summ, 1)
            step.settle()
            dve.sem_inc(s_summ, 1)
            dve.wait_ge(s_kv, 1)
            dve.wait_ge(s_pad, 2)
            for src, bias, bd, scale in ((0, bk0, kbd, HD ** -0.5), (256, bv0, vbd, 1.0)):
                step.alone(dve.tensor_tensor(kvb, ps[:, 0, src:src + 256].rearrange("p (j c) -> p j c", j=HC),
                                             over(bias, NC), ALU.add))
                for a in range(2):
                    step.mark(dve.tensor_scalar(bd[64 * a:64 * a + 64, :, a, :], kvb[64 * a:64 * a + 64], scale, None,
                                                ALU.mult))
                step.settle()
                dve.sem_inc(s_kbd, 1)
            step.alone(dve.tensor_tensor(res, res, along(bo0_bc, NT), ALU.add))
            dve.wait_ge(s_gc, 3)
            dve.wait_ge(s_wrest, 16 * 25)
            dve.wait_ge(s_xnT, NB)
            step.alone(dve.tensor_tensor(xn, xn, along(bo_bc, NT), ALU.add))
            dve.wait_ge(s_pad, 5)
            dve.wait_ge(s_vp, 2)
            dve.sem_inc(s_accc, 1)
            dve.sem_inc(s_mr, 1)
            vp_flat = r3[:, 0:2048].rearrange("p (i c) -> p i c", i=NT)
            att_blocks = att
            events = sorted([(k, 3, n) for n, (k, _, _) in enumerate(AUX)]
                            + [(LAST[qb] + LAG, 1, qb) for qb in range(NB)]
                            + [(k + 1, 2, m) for k, m in SUMM_EXP.items()])
            with dve.Fori(0, NKV) as g:
                dve.wait_ge(s_pv, g * KB + KB)
                dve.tensor_copy(vc, vp_flat[:, :, bass.ds(g * 32, 32)]).then_inc(s_vc, 1)
                for k, kind, n in events:
                    if kind == 1:
                        dve.wait_ge(s_pv, g * KB + (KB + LAST[n] + 1))
                        dve.tensor_copy(accT[:, n % 2, :], ps[:, 6, :]).then_inc(s_accc, 1)
                        continue
                    if kind == 2:
                        m, w = n, summ_chunks(n)
                        blk = sc[:, m % 2, :, 0:w]
                        dve.wait_ge(s_ex, g * NB + (m + 1))
                        dve.tensor_reduce(ssm_[:, m % 2, :], blk, X_AXIS, ALU.add).then_inc(s_sm, 1)
                        dve.wait_ge(s_sm, g * 4 * NB + (4 * m + 3))
                        dve.reciprocal(ssm_[:, m % 2, :], ssm_[:, m % 2, :]).then_inc(s_sm, 1)
                        dve.wait_ge(s_sm, g * 4 * NB + (4 * m + 4))
                        dve.tensor_tensor(pr[:, m, :].rearrange("p (h c) -> p h c", h=HEADS)[:, :, 0:w], blk,
                                          over(ssm_[:, m % 2, :], w), ALU.mult).then_inc(s_pr, 1)
                        continue
                    _, what, m = AUX[n]
                    dve.wait_ge(s_mf, g * NAUX + (n + 1))
                    w = summ_chunks(m)
                    if what == "SCORE":
                        blk = sc[:, m % 2, :, 0:w]
                        ended = sc[:, m % 2, :, w - NC // NB:w]
                        dve.tensor_tensor(blk, ps[:, SHARED, 0:HEADS * w].rearrange("p (h c) -> p h c", h=HEADS),
                                          g0[:, :, 0:w], ALU.add).then_inc(s_mr, 1)
                        dve.wait_ge(s_mr, g * NAUX + (n + 2))
                        dve.tensor_tensor(ended, ended, along(cmask[:, bass.ds(g * 8, 8)], HEADS), ALU.add
                                          ).then_inc(s_sm, 1)
                        dve.wait_ge(s_sm, g * 4 * NB + (4 * m + 1))
                        dve.tensor_reduce(smx[:, m % 2, :], blk, X_AXIS, ALU.max).then_inc(s_sm, 1)
                        dve.wait_ge(s_sm, g * 4 * NB + (4 * m + 2))
                        dve.tensor_tensor(blk, blk, over(smx[:, m % 2, :], w), ALU.subtract).then_inc(s_sub, 1)
                    elif what == "TRANSPOSE":
                        dve.tensor_copy(ptr, ps[:, SHARED, :]).then_inc(s_mr, 1)
                    elif what == "OUTPUT":
                        tile = res_flat[:, bass.ds(g * D + m * (TPB * D), D)]
                        dve.tensor_tensor(tile, tile, ps[:, SHARED, 0:D], ALU.add).then_inc(s_mr, 1)
                    else:
                        src = ps[:, SHARED, :].rearrange("p (ij m) -> p ij m", m=32)
                        dve.reciprocal(rden[:, m % 2, :], src[:, :, QD]).then_inc(s_rden, 1)
                        dve.wait_ge(s_rden, g * NB + (m + 1))
                        dve.tensor_tensor(
                            att_blocks[:, TPB * m:TPB * m + TPB, bass.ds(g * 32, 32)].rearrange(
                                "p i (j d) -> p i j d", d=QD),
                            src[:, :, 0:QD].rearrange("p (i j) d -> p i j d", i=TPB),
                            over(rden[:, m % 2, :].rearrange("p (i j) -> p i j", i=TPB), QD), ALU.mult
                            ).then_inc(s_mr, 1)
            for b in range(NB):
                dve.wait_ge(s_gt, b + 1)
                blk = oT[:, b * TB:b * TB + TB]
                dve.tensor_tensor(blk, blk, gate[:, b * TB:b * TB + TB], ALU.mult).then_inc(s_og, 1)
            for b in range(NB):
                dve.wait_ge(s_wo, b + 1)
                blk = xn[:, TPB * b:TPB * b + TPB, :]
                dve.tensor_tensor(blk, blk, ps[:, 4 + b, :].rearrange("p (i d) -> p i d", d=D), ALU.add
                                  ).then_inc(s_xm, 1)
            for b in range(NB):
                dve.wait_ge(s_sq2, b + 1)
                dve.tensor_reduce(ssq2[:, TPB * b:TPB * b + TPB], sqm[:, TPB * b:TPB * b + TPB, :], X_AXIS, ALU.add
                                  ).then_inc(s_ss2, 1)
            dve.wait_ge(s_sd2, 1)
            step.alone(dve.reciprocal(hs2, sdm))
            for i in range(NT):
                dve.tensor_scalar(h2[:, i, :], xn[:, i, :], hs2[:, i:i + 1], None, ALU.mult).then_inc(s_h2, 1)
            step.alone(dve.tensor_tensor(res, res, xn, ALU.add))
            for b in range(NB):
                blk = slice(b * TB, b * TB + TB)
                dve.wait_ge(s_h2s, b + 1)
                dve.tensor_tensor(h2l[:, blk], h2T[:, blk], h2h[:, blk], ALU.subtract).then_inc(s_h2l, 1)
            dve.wait_ge(s_lg, 1)
            step.alone(dve.tensor_tensor(lg, ps[:, 4, 0:P].rearrange("p (i e) -> p i e", e=E), along(br_bc, NT),
                                         ALU.add))
            step.alone(dve.tensor_reduce(lmx, lg, X_AXIS, ALU.max))
            step.alone(dve.tensor_tensor(eq, lg, over(lmx, E), ALU.is_equal))
            step.alone(dve.tensor_tensor(rk, eq, along(rank, NT), ALU.mult))
            step.alone(dve.tensor_reduce(lmx2, rk, X_AXIS, ALU.max))
            dve.tensor_tensor(oh, rk, over(lmx2, E), ALU.is_equal).then_inc(s_oh, 1)
            dve.wait_ge(s_ohT, 1)
            ohT_ps = ps[0:E, 4:8, :].rearrange("p b t -> p (b t)")
            dve.tensor_scalar(pen, ohT_ps, 1.0, BIG, ALU.subtract, ALU.mult).then_inc(s_pen, 1)
            ES = E * FC
            dve.sem_inc(s_moea, ES)
            dve.sem_inc(s_ya, 1)
            with dve.Fori(0, NB) as tb:
                for n in range(ES):
                    e, c = divmod(n, FC)
                    dve.wait_ge(s_sg, tb * ES + (n + 1))
                    free = ES + n - 2 if n >= 3 else last_user(n, 3, ES) + 1
                    dve.wait_ge(s_dn, tb * ES + free)
                    dve.scalar_tensor_tensor(am[:, n % 3, :], ps[:, 2 * (n % 3), :], b1c[:, e, c:c + 1],
                                             sg[:, n % 3, :], ALU.add, ALU.mult).then_inc(s_moea, 1)
                    dve.wait_ge(s_moea, tb * ES + (ES + n + 1))
                    dve.tensor_copy(amh[:, n % 3, :], am[:, n % 3, :]).then_inc(s_amh, 1)
                    dve.wait_ge(s_amh, tb * ES + (n + 1))
                    dve.tensor_tensor(aml[:, n % 3, :], am[:, n % 3, :], amh[:, n % 3, :], ALU.subtract
                                      ).then_inc(s_aml, 1)
                dve.wait_ge(s_yt, tb + 2)
                blk = res_flat[:, bass.ds(tb * TB, TB)]
                dve.tensor_tensor(blk, blk, ps[:, 7, :], ALU.add).then_inc(s_ya, 1)
            dve.wait_ge(s_ya, NB + 1)
            for i in range(NT):
                step.mark(dve.bn_stats(stats[:, i, :], res[:, i, :]))
            step.settle()
            for i in range(NT):
                m = dve.bn_aggr(mv[:, i, :], stats[:, i, :])
            m.then_inc(s_var2, 1)
            dve.wait_ge(s_sdl, 1)
            step.alone(dve.reciprocal(rstd, sd))
            for i in range(NT):
                dve.tensor_scalar(xn[:, i, :], res[:, i, :], mv[:, i, 0:1], rstd[:, i:i + 1],
                                  ALU.subtract, ALU.mult).then_inc(s_xn2, 1)
            step.alone(dve.tensor_tensor(ms, mv[:, :, 1], rstd, ALU.mult))
            dve.tensor_tensor(ms, ms, rstd, ALU.mult).then_inc(s_var2, 1)
            dve.wait_ge(s_l1w, 16 * 18)
            step.mark(dve.tensor_scalar(inp, inp, normw, None, ALU.mult))
            step.mark(dve.tensor_scalar(owT, owT, 0.5, None, ALU.mult))
            step.mark(dve.tensor_scalar(d2, d2, 0.5, None, ALU.mult))
            step.mark(dve.tensor_scalar(w1sh, w1s, 0.5, None, ALU.mult))
            step.settle()
            dve.tensor_tensor(s12, w1sh, w2s, ALU.mult).then_inc(s_fs, 1)
            dve.sem_inc(s_inp, 1)
            dve.wait_ge(s_sdl, 2)
            step.alone(dve.reciprocal(hs, sd2))
            dve.wait_ge(s_xn2, NT)
            for i in range(NT):
                dve.tensor_scalar(xs[:, i, :], xn[:, i, :], hs[:, i:i + 1], None, ALU.mult).then_inc(s_xs, 1)
            step.alone(dve.tensor_tensor(res, res, xn, ALU.add))
            dve.wait_ge(s_pad, 6)
            for b in range(NB):
                toks = slice(b * TB, b * TB + TB)
                for k in (0, 1):
                    u = 6 * b + k
                    dve.wait_ge(s_zth, 2 * b + k + 1)
                    dve.scalar_tensor_tensor(z2[:, k, toks], th[:, k, :], 1.0, ps[:, u % 8, :], ALU.add, ALU.mult
                                             ).then_inc(s_pjv, 1)
                u = 6 * b + 5
                dve.wait_ge(s_pj, u + 1)
                dve.tensor_copy(BT[:, toks], ps[:, u % 8, :]).then_inc(s_pjv, 1)
                dve.wait_ge(s_pja, 3 * b + 2)
                for k in range(KW):
                    for m_ in range(MI):
                        src = xp[:, m_, b * TB + k:b * TB + k + TB]
                        if k == 0:
                            step.mark(dve.tensor_scalar(xc[:, m_, toks], src, convw[:, m_, 0:1],
                                                        convb[:, m_:m_ + 1], ALU.mult, ALU.add))
                        else:
                            step.mark(dve.scalar_tensor_tensor(xc[:, m_, toks], src, convw[:, m_, k:k + 1],
                                                               xc[:, m_, toks], ALU.mult, ALU.add))
                    step.settle()
                dve.sem_inc(s_xcv, 1)
            for b in range(NB):
                blk = xc[:, :, b * TB:b * TB + TB]
                dve.wait_ge(s_xth, b + 1)
                dve.scalar_tensor_tensor(blk, thc, 1.0, blk, ALU.add, ALU.mult).then_inc(s_xc, 1)
            for g in range(6):
                n = min(3, NT - 3 * g)
                dve.wait_ge(s_bt, g + 1)
                dve.tensor_copy(btd[:, 3 * g:3 * g + n, :],
                                ps[:, (6 * NB + g) % 8, 0:132 * n].rearrange("p (i c) -> p i c", c=132)
                                ).then_inc(s_btc, 1)
            dve.wait_ge(s_btc, 6)
            step.alone(dve.tensor_tensor(du, btd[:, :, P:P + NH], along(dtb, NT), ALU.add))
            dve.scalar_tensor_tensor(dl, du, -1.0, du, ALU.mult, ALU.min).then_inc(s_dta, 1)
            dve.wait_ge(s_dtb, 3)
            step.alone(dve.scalar_tensor_tensor(dt, du, 0.0, dl, ALU.max, ALU.add))
            dve.scalar_tensor_tensor(av, dt, -1.0, along(ea, NT), ALU.mult, ALU.mult).then_inc(s_av, 1)
            dve.wait_ge(s_av, 1)
            step.alone(dve.tensor_scalar(dt, dt, 0.5, None, ALU.mult))
            dve.wait_ge(s_cum, 1)
            dve.tensor_copy(cums, ps[:, 6, 0:NT * NH].rearrange("p (i h) -> p i h", i=NT)).then_inc(s_cumc, 1)
            dve.wait_ge(s_cumc, 1)
            for credit, n in ((s_fm, FO), (s_fr, 1), (s_cx, 2), (s_cg, 1), (s_ca, 1), (s_ch, 1)):
                dve.sem_inc(credit, n)
            cums_f, dt_f = (a.rearrange("p i h -> p (i h)") for a in (cums, dt))
            dve_order = []
            for what, o in LAYER1:
                dve_order.append((what, o))
                if what == "CHUNK":
                    dve_order.append(("WEIGHT", o))
            first = dve_order.index(("WEIGHT", 0))
            dve_order[first], dve_order[first + 1] = dve_order[first + 1], dve_order[first]
            CSTEPS = 4 * TPB
            with dve.Fori(0, NB) as blk_i:
                steps = 0
                for what, o in dve_order:
                    b = o % 2
                    chunk4 = bass.ds(blk_i * (TPB * NH) + o * NH, NH)
                    if what == "UP":
                        if o == 0:
                            dve.wait_ge(s_f4, blk_i + 1)
                        dve.wait_ge(s_ft, blk_i * FO + (o + 1))
                        dve.scalar_tensor_tensor(ft1[:, o % 2, :], fth[:, o % 2, :], 1.0, ps[:, ffn_bank(2 * o), :],
                                                 ALU.add, ALU.mult).then_inc(s_fm, 1)
                        dve.wait_ge(s_fm, blk_i * FO + (FO + o + 1))
                        dve.scalar_tensor_tensor(fa[:, o, :], ft1[:, o % 2, :], s12[:, o:o + 1],
                                                 ps[:, ffn_bank(2 * o + 1), :], ALU.mult, ALU.mult
                                                 ).then_inc(s_fg, 1)
                    elif what == "CHUNK":
                        dve.wait_ge(s_c1, blk_i * TPB + (o + 1))
                        dve.wait_ge(s_cm, blk_i * (2 * TPB) + (2 * o + 2))
                        dve.tensor_tensor(ed[:, b], ps[:, 1, :].rearrange("p (h t) -> p h t", h=NH),
                                          over(cums_f[:, chunk4], P), ALU.subtract).then_inc(s_cstep, 1)
                        steps += 1
                        dve.wait_ge(s_cstep, blk_i * CSTEPS + steps)
                        dve.tensor_scalar(ed[:, b], ed[:, b], 0.0, None, ALU.min).then_inc(s_cd, 1)
                        dve.tensor_tensor(gm[:, b, :], ps[:, 0, 0:P], tri, ALU.mult).then_inc(s_cx, 1)
                    elif what == "WEIGHT":
                        dve.wait_ge(s_cst, blk_i * TPB + (o + 1))
                        dve.tensor_tensor(dtx[:, b], ps[:, 0, P:P + DI].rearrange("p (h d) -> p h d", h=NH),
                                          over(dt_f[:, chunk4], PD), ALU.mult).then_inc(s_cstep, 1)
                        steps += 1
                        dve.wait_ge(s_cstep, blk_i * CSTEPS + steps)
                        dve.wait_ge(s_ce, blk_i * (2 * TPB) + (2 * o + 3))
                        dve.tensor_tensor(dtw[:, b], dtx[:, b], over(ed[:, b, :, P - 1], PD), ALU.mult
                                          ).then_inc(s_cx, 1)
                    elif what == "STATE":
                        dve.wait_ge(s_cy, blk_i * TPB + (o + 3))
                        dve.wait_ge(s_ce, blk_i * (2 * TPB) + (2 * o + 4))
                        dve.tensor_tensor(hst, hst, over(ec[:, b, :, P - 1], PD), ALU.mult).then_inc(s_cstep, 1)
                        steps += 1
                        dve.wait_ge(s_co, blk_i * TPB + (o + 1))
                        for m_ in range(MI):
                            m = dve.scalar_tensor_tensor(yg[:, b, m_, :], xcs[:, m_, P * o:P * o + P],
                                                         d2[:, m_:m_ + 1], ps[:, 2, P * m_:P * m_ + P],
                                                         ALU.mult, ALU.add)
                        m.then_inc(s_cstep, 1)
                        steps += 1
                        dve.wait_ge(s_cstep, blk_i * CSTEPS + steps)
                        dve.wait_ge(s_cst, blk_i * TPB + (o + 3))
                        dve.tensor_tensor(hst, hst, ps[:, 3, 0:DI].rearrange("p (h d) -> p h d", h=NH), ALU.add
                                          ).then_inc(s_ch, 1)
                        dve.tensor_tensor(yg[:, b], yg[:, b], z2[:, :, bass.ds(blk_i * TB + o * P, P)], ALU.mult
                                          ).then_inc(s_cg, 1)
                    elif what == "PROJECT":
                        dve.wait_ge(s_co, blk_i * TPB + (o + 3))
                        tile = res_flat[:, bass.ds(blk_i * TB + o * D, D)]
                        dve.tensor_tensor(tile, tile, ps[:, 2, 2 * P:2 * P + D], ALU.add).then_inc(s_ca, 1)
                    elif what == "DOWN":
                        dve.wait_ge(s_f4, blk_i + 2)
                        dve.tensor_tensor(fst, ps[:, ffn_bank(16), :].rearrange("p (i d) -> p i d", i=TPB),
                                          along(w3s_bc, TPB), ALU.mult).then_inc(s_fr, 1)
                        dve.wait_ge(s_fr, blk_i + 2)
                        dve.wait_ge(s_ca, blk_i * TPB + (TPB + 1))
                        blk = res_flat[:, bass.ds(blk_i * TB, TB)]
                        dve.tensor_tensor(blk, blk, fst.rearrange("p i d -> p (i d)"), ALU.add).then_inc(s_fin, 1)


def kernel(**inputs):
    import concourse.bacc as bacc
    from concourse.bass_utils import run_bass_kernel_spmd

    f = {k: np.asarray(v) for k, v in inputs.items()}
    row_ = lambda a: a.reshape(1, -1)
    cols = lambda a, n: a.reshape(n, P).T
    inT = f["L1_attn_in_proj_w"].T

    def heads_inner(q, k, v):
        qk = np.concatenate([q.reshape(-1, NQ, QD), k.reshape(-1, NKV, QD)], axis=1)
        return np.concatenate([qk.transpose(0, 2, 1).reshape(len(q), -1), v], axis=1)

    arrays = {
        "x": f["L0_attn_x"][0],
        "a_WqT": f["L0_attn_Wq"].T, "a_Wk": f["L0_attn_Wk"], "a_Wv": f["L0_attn_Wv"], "a_Wo": f["L0_attn_Wo"],
        "a_bq": cols(f["L0_attn_bq"], HC), "a_bk": cols(f["L0_attn_bk"], HC), "a_bv": cols(f["L0_attn_bv"], HC),
        "a_bo": row_(f["L0_attn_bo"]),
        "f_ln1": f["L0_ffn_ln1_w"].reshape(P, 1), "f_ln2": f["L0_ffn_ln2_w"].reshape(P, 1),
        "f_Wqkv": heads_inner(f["L0_ffn_Wq"], f["L0_ffn_Wk"], f["L0_ffn_Wv"]),
        "f_bqkv": heads_inner(row_(f["L0_ffn_bq"]), row_(f["L0_ffn_bk"]), row_(f["L0_ffn_bv"])),
        "f_qn": row_(f["L0_ffn_qn_w"]), "f_kn": row_(f["L0_ffn_kn_w"]),
        "f_Wg": f["L0_ffn_Wg"], "f_bgc": np.tile(f["L0_ffn_bg"], NQ).reshape(P, 1),
        "f_Wo": f["L0_ffn_Wo"], "f_bo": row_(f["L0_ffn_bo"]),
        "f_Wr": f["L0_ffn_Wr"], "f_br": row_(f["L0_ffn_br"]),
        "f_W1": f["L0_ffn_W1"], "f_b1c": f["L0_ffn_b1"].reshape(E, 2 * FC, P).transpose(2, 0, 1).reshape(P, -1),
        "f_W2": f["L0_ffn_W2"], "f_b2": f["L0_ffn_b2"],
        "s_norm": f["L1_attn_norm_w"].reshape(P, 1),
        "s_inT": np.concatenate([inT[:, 0:2 * DI], inT[:, 2 * DI + P:2 * DI + 2 * P],
                                 inT[:, 2 * DI:2 * DI + P], inT[:, 2 * DI + 2 * P:]], axis=1),
        "s_convw": f["L1_attn_conv_w"].reshape(MI, P, KW).transpose(1, 0, 2).reshape(P, -1),
        "s_convb": cols(f["L1_attn_conv_b"], MI),
        "s_D": np.repeat(f["L1_attn_D"], PD).reshape(MI, P).T,
        "s_dtb": row_(f["L1_attn_dt_bias"]), "s_Alog": row_(f["L1_attn_A_log"]),
        "s_outT": f["L1_attn_out_proj_w"].T,
        "g_w1T": f["L1_ffn_w1_w"].T, "g_w2T": f["L1_ffn_w2_w"].T,
        "g_h1T": f["L1_ffn_h1_w"].T, "g_h2T": f["L1_ffn_h2_w"].T, "g_w3T": f["L1_ffn_w3_w"].T,
        "g_w1s": cols(f["L1_ffn_w1_s"], FO), "g_w2s": cols(f["L1_ffn_w2_s"], FO),
        "g_h1s": cols(f["L1_ffn_h1_s"], FO), "g_h2s": cols(f["L1_ffn_h2_s"], FO),
        "g_w3s": row_(f["L1_ffn_w3_s"]),
    }
    inv = (np.float32(1.0) / np.float32(10000.0) ** (np.arange(0, QD, 2, dtype=np.float32) / np.float32(QD))
           ).astype(np.float32)
    ang = np.arange(T, dtype=np.float32)[:, None] * inv[None, :]
    table = lambda a: a.astype(np.float32).reshape(NT, P, 4).transpose(1, 0, 2).reshape(P, -1)
    p_, r_, c_ = np.ogrid[0:P, 0:TPB, 0:NC // NB]
    cmask = np.where(CHUNK * c_ <= P * r_ + p_, 0.0, -BIG).astype(np.float32).reshape(P, -1)
    arrays["consts"] = np.concatenate([np.eye(P, dtype=np.float32), np.triu(np.ones((P, P), np.float32)),
                                       table(np.cos(ang)), table(np.sin(ang))], axis=1)
    arrays["cmask"] = cmask
    arrays["rank"] = np.arange(E, 0, -1, dtype=np.float32).reshape(1, E)

    nc = bacc.Bacc("TRN2", target_bir_lowering=False, num_devices=1)
    arrays = {k: np.ascontiguousarray(v) for k, v in arrays.items()}
    io = {k: nc.dram_tensor(f"in_{k}", a.shape, mybir.dt.from_np(a.dtype), kind="ExternalInput").ap()
          for k, a in arrays.items()}
    out = nc.dram_tensor("out", (T, D), F32, kind="ExternalOutput").ap()
    build(nc, io, out)
    r = run_bass_kernel_spmd(nc, [{f"in_{k}": a for k, a in arrays.items()}], core_ids=[0])
    return r.results[0]["out"].reshape(1, T, D)
```

```python
from contextlib import ExitStack

import numpy as np

import concourse.bass as bass
import concourse.mybir as mybir

F32 = mybir.dt.float32
F32R = mybir.dt.float32r
BF16 = mybir.dt.bfloat16
ALU = mybir.AluOpType
ACT = mybir.ActivationFunctionType
X_AXIS = mybir.AxisListType.X

P = 128
T = 2048
D = 128
NT = T // P
TB = 512
NB = T // TB
TPB = TB // P

HEADS, HD = 16, 64
NC = 32
CHUNK = 64
HC = HEADS * HD // P

NQ, NKV, QD = 16, 4, 8
REP = NQ // NKV
QKV_W = NQ * QD + 2 * NKV * QD
NSPLIT = 3
KV_W = NKV * QD

E, HID = 8, 256
FC = HID // P

DI, NH, PD = 256, 4, 64
KW = 4
MI = DI // P

FH = 512
FO = FH // P

LN_EPS, RMS_EPS = 1e-5, 1e-6
BIG = 1e30
TWO_ONES = float(np.array([1.0, 1.0], np.float32).view(np.uint16)[1::2].copy().view(np.float32)[0])


class Steps:

    def __init__(self, eng, sem):
        self.eng, self.sem, self.n = eng, sem, 0

    def mark(self, instruction):
        instruction.then_inc(self.sem, 1)
        self.n += 1
        return self.n

    def settle(self):
        self.eng.wait_ge(self.sem, self.n)

    def alone(self, instruction):
        self.mark(instruction)
        self.settle()


def over(ap, n):
    return ap.unsqueeze(len(ap.shape)).broadcast_to(list(ap.shape) + [n])


def product(pe, dst, w, x, start, stop):
    (wh, wl), (xh, xl) = w, x
    pe.matmul(dst, wh, xh, start=start, stop=False)
    pe.matmul(dst, wh, xl, start=False, stop=False)
    return pe.matmul(dst, wl, xh, start=False, stop=stop)


def along(ap, n):
    return ap.unsqueeze(1).broadcast_to([ap.shape[0], n] + list(ap.shape[1:]))


def build(nc, io, out):
    ctx = ExitStack()
    with ctx:
        def sb(name, cols, dt=F32, rows=P):
            return ctx.enter_context(nc.sbuf_tensor(name, [rows, cols], dt))

        def sem(name):
            return ctx.enter_context(nc.semaphore(name))

        res = sb("res", NT * D)[:, :].rearrange("p (i d) -> p i d", i=NT)
        r3 = sb("r3", 10080)
        sizes = (("xn", NT * D), ("xnT", T), ("row", 1024), ("r1", 14400), ("r2", 20480))
        smalls = [("consts", 2 * P + 2 * NT * 4, F32), ("identb", P, BF16), ("small", 512, F32),
                  ("stats", NT * 6, F32)]
        consts, identb, small, stats = (sb(*a) for a in smalls)
        with ExitStack() as first_names:
            xn, xnT, row, r1, r2 = (first_names.enter_context(nc.sbuf_tensor(name, [P, cols], F32))
                                    for name, cols in sizes)
        xnr, xnTr, rowr, r1r, r2r = (sb(name + "r", cols, F32R) for name, cols in sizes)
        xn = xn[:, :].rearrange("p (i d) -> p i d", i=NT)
        xnT = xnT[:, :]
        ident = consts[:, 0:P]
        tri = consts[:, P:2 * P]
        cosT = consts[:, 2 * P:2 * P + 4 * NT].rearrange("p (i f) -> p i f", i=NT)
        sinT = consts[:, 2 * P + 4 * NT:2 * P + 8 * NT].rearrange("p (i f) -> p i f", i=NT)
        identb = identb[:, :]
        stats = stats[:, :].rearrange("p (i s) -> p i s", i=NT)
        mv = small[:, 0:32].rearrange("p (i s) -> p i s", i=NT)
        sd, rstd, ms, sd2, hs = (small[:, 32 + 16 * k:48 + 16 * k] for k in range(5))
        bo_bc = small[:, 128:256]
        bo0_bc = small[:, 256:384]
        w3s_bc = small[:, 384:512]
        bqkv = row[:, 0:QKV_W]
        qn_bc, kn_bc = row[:, 192:200], row[:, 200:208]
        kw = row[:, 208:216]
        shift = row[:, 216:217]
        mx2 = row[:, 217:219]
        ln1 = row[:, 220:221]
        ln2 = row[:, 221:222]
        bgc = row[:, 222:223]
        br_bc = row[:, 224:232]
        rank = row[:, 232:240]
        b1c = row[:, 240:272].rearrange("p (e k) -> p e k", e=E)
        wr = row[:, 272:280]
        normw = row[:, 280:281]
        convw = row[:, 284:292].rearrange("p (m k) -> p m k", m=MI)
        convb = row[:, 292:294]
        d2 = row[:, 294:296]
        dtb = row[:, 296:300]
        alog = row[:, 300:304]
        w1s, w2s = row[:, 304:308], row[:, 308:312]
        h1s, h2s = row[:, 312:316], row[:, 316:320]
        warm = row[:, 321:323]
        wg = row[:, 384:512]
        wo = row[:, 512:640]
        b2 = row[0:E, 640:768]
        oneEf = row[0:E, 768:896]
        w1sh = row[:, 896:900]
        s12 = row[:, 900:904]

        cmask = row[:, 904:936]

        qkv = r1[:, 0:3072].rearrange("p (i c) -> p i c", i=NT)
        rot = r1[:, 3072:5632].rearrange("p (i d h) -> p i d h", i=NT, d=QD)
        rot_a = r1[:, 5632:6912].rearrange("p (i d h) -> p i d h", i=NT, d=4)
        rot_b = r1[:, 6912:8192].rearrange("p (i d h) -> p i d h", i=NT, d=4)
        sq = r1[:, 5632:8192].rearrange("p (i d h) -> p i d h", i=NT, d=QD)
        qs = r1[:, 5632:8704].bitcast(BF16).rearrange("p (i s c) -> p i s c", i=NT, s=NSPLIT)
        ks = r1[:, 8704:9472].bitcast(BF16).rearrange("p (i s c) -> p i s c", i=NT, s=NSPLIT)
        qT = r1[:, 0:3072].bitcast(BF16).rearrange("p (s t) -> p s t", s=NSPLIT)
        kT = r1[:, 9472:10496].bitcast(BF16)
        ssq = r1[:, 10496:10816]
        rr = r1[:, 10816:11136]
        wqkv = r1[:, 11136:11328]
        probs = r1[:, 0:8192].rearrange("p (b h t) -> p b h t", b=8, h=2)
        att = r1[:, 8192:10240].rearrange("p (i c) -> p i c", i=NT)
        accT = r1[:, 10240:11264].rearrange("p (b t) -> p b t", b=2)
        xti = r1[:, 11264:11776].rearrange("p (m t) -> p m t", m=NB)
        rden = r1[:, 11776:11808].rearrange("p (b n) -> p b n", b=2)
        pr = r1[:, 11808:13856].rearrange("p (m n) -> p m n", m=NB)
        qst = r2[:, 0:16384].bitcast(BF16).rearrange("p (h t) -> p h t", h=NQ)
        kst = r2[:, 16384:20480].bitcast(BF16).rearrange("p (g t) -> p g t", g=NKV)
        vp = r3[:, 0:2048].rearrange("p (i g m) -> p i g m", i=NT, g=NKV)
        wqT = r1[:, 12416:13440].rearrange("p (j d) -> p j d", j=HC)
        kbd = r1[:, 13440:13952].rearrange("p (j a c) -> p j a c", j=HC, a=2)
        kvb = r1[:, 13952:14208].rearrange("p (j c) -> p j c", j=HC)
        s0 = 2048
        wk0 = r3[:, s0:s0 + 1024]
        wv0 = r3[:, s0 + 1024:s0 + 2048]
        wo0 = r3[:, s0 + 2048:s0 + 3072].rearrange("p (j d) -> p j d", j=HC)
        vbd = r3[:, s0 + 3072:s0 + 3584].rearrange("p (j a c) -> p j a c", j=HC, a=2)
        gmat = r3[:, s0 + 3584:s0 + 4096].rearrange("p (h c) -> p h c", h=HEADS)
        g0 = r3[:, s0 + 4096:s0 + 4608].rearrange("p (h c) -> p h c", h=HEADS)
        vw = r3[:, s0 + 4608:s0 + 5120].rearrange("p (q d) -> p q d", q=4)
        sc = r3[:, s0 + 5120:s0 + 6144].rearrange("p (b h c) -> p b h c", b=2, h=HEADS)
        ptr = r3[:, s0 + 6144:s0 + 6656]
        s1 = s0 + 7168
        summT = r3[:, s1:s1 + NC]
        bq0 = r3[:, s1 + 32:s1 + 40]
        bk0 = r3[:, s1 + 40:s1 + 48]
        bv0 = r3[:, s1 + 48:s1 + 56]
        smx = r3[:, s1 + 64:s1 + 96].rearrange("p (b h) -> p b h", b=2)
        ssm_ = r3[:, s1 + 96:s1 + 128].rearrange("p (b h) -> p b h", b=2)

        vc = r3[:, 9344:9856].rearrange("p (i m) -> p i m", i=NT)

        oT = r2[:, 2048:4096]
        gate = r2[:, 4096:6144]
        sqm = r2[:, 6144:8192].rearrange("p (i d) -> p i d", i=NT)
        h2 = r2[:, 8192:10240].rearrange("p (i d) -> p i d", i=NT)
        w1 = r1[:, 0:4096].rearrange("p (e f) -> p e f", e=E)
        w2 = r1[:, 4096:6144].rearrange("p (e c d) -> p e c d", e=E, c=FC)
        w1f, w2f = r1[:, 0:4096], r1[:, 4096:6144]
        w1hf, w2hf = (r2r[:, a:b] for a, b in ((14336, 18432), (18432, 20480)))
        w1lf, w2lf = r1r[:, 0:4096], r1r[:, 4096:6144]
        w1h, w1l = (a.rearrange("p (e f) -> p e f", e=E) for a in (w1hf, w1lf))
        w2h, w2l = (a.rearrange("p (e c d) -> p e c d", e=E, c=FC) for a in (w2hf, w2lf))
        h2T = r3[:, 2048:4096]
        h2h, h2l = r1r[:, 8192:10240], r1r[:, 10240:12288]
        m0 = 4096
        ssq2, sdm, hs2 = (r3[:, m0 + 32 + 16 * k:m0 + 48 + 16 * k] for k in range(3))
        lg, eq, rk, oh = (r3[:, m0 + 128 + 128 * k:m0 + 256 + 128 * k].rearrange("p (i e) -> p i e", e=E)
                          for k in range(4))
        lmx = r3[:, m0 + 96:m0 + 112]
        lmx2 = r3[:, m0 + 112:m0 + 128]
        ohT = r3[0:E, m0 + 640:m0 + 640 + T]
        pen = r3[0:E, m0 + 640 + T:m0 + 640 + T + T // 2].bitcast(BF16)
        onee = r3[0:E, m0 + 640 + T + T // 2:m0 + 640 + T + T // 2 + 512].bitcast(BF16).rearrange(
            "p (e m) -> p e m", e=E)
        sg = r2[:, 10240:11776].rearrange("p (b t) -> p b t", b=3)
        am = r2[:, 11776:13312].rearrange("p (b t) -> p b t", b=3)
        amh = r2r[:, 6664:8200].rearrange("p (b t) -> p b t", b=3)
        aml = r2r[:, 11776:13312].rearrange("p (b t) -> p b t", b=3)
        yT = r2[:, 13312:13824]

        inp = r2[:, 0:772]
        owT = r2[:, 772:1028].rearrange("p (m d) -> p m d", m=MI)
        f1 = r2[:, 1028:1540]
        f2 = r2[:, 1540:2052]
        fh1 = r2[:, 2052:4100].rearrange("p (k o) -> p k o", k=FO)
        fh2 = r2[:, 4100:6148].rearrange("p (k o) -> p k o", k=FO)
        f3 = r2[:, 6148:6660].rearrange("p (k d) -> p k d", k=FO)
        f12f, f12hf, f12lf = r2[:, 1028:2052], r2r[:, 18500:19524], r2r[:, 1028:2052]
        fh1h = r1r[:, 4096:6144].rearrange("p (k o) -> p k o", k=FO)
        fh1l = r2r[:, 2052:4100].rearrange("p (k o) -> p k o", k=FO)
        fh2h = [r2r[:, 15364:15876], r2r[:, 15876:16388], r2r[:, 19524:20036], rowr[:, 384:896]]
        fh2l = r2r[:, 4100:6148].rearrange("p (k o) -> p k o", k=FO)
        fah = r1r[:, 6144:8192].rearrange("p (k t) -> p k t", k=FO)
        fal = r2r[:, 6660:8708].rearrange("p (k t) -> p k t", k=FO)
        fbh = r2r[:, 12292:14340].rearrange("p (k t) -> p k t", k=FO)
        fbl = r2r[:, 8708:10756].rearrange("p (k t) -> p k t", k=FO)
        xnTh, xnTl = xnr[:, :], xnTr[:, :]
        FSPLIT = [(f12f, f12hf, f12lf), (xnT, xnTh, xnTl)] + [(fh2[:, k, :], fh2h[k], fh2l[:, k, :])
                                                             for k in range(FO)] + [(fh1, fh1h, fh1l)]
        fa = r2[:, 6660:8708].rearrange("p (k t) -> p k t", k=FO)
        fb = r2[:, 8708:10756].rearrange("p (k t) -> p k t", k=FO)
        fth = r2[:, 10756:11780].rearrange("p (b t) -> p b t", b=2)
        fst = r2[:, 11780:12292].rearrange("p (i d) -> p i d", i=TPB)
        cdiag = r2[:, 11780:12292].rearrange("p (k j) -> p k j", k=KW)
        xsT = r2[:, 12292:14340]
        xs = r2[:, 14340:16388].rearrange("p (i d) -> p i d", i=NT)
        btd = r2[:, 16388:18500].rearrange("p (i c) -> p i c", i=NT)
        z2 = r1[:, 0:4096].rearrange("p (m t) -> p m t", m=MI)
        xp = r1[:, 4096:8200].rearrange("p (m t) -> p m t", m=MI)
        xc = r1[:, 8200:12296].rearrange("p (m t) -> p m t", m=MI)
        CT = r1[:, 12296:14344]
        BT = r3[:, 0:2048]
        k0 = 2048
        dt, av, cums, du, dl = (r3[:, k0 + 64 * k:k0 + 64 * k + 64].rearrange("p (i h) -> p i h", i=NT)
                                for k in range(5))
        ea = r3[:, k0 + 320:k0 + 324]
        th = r3[:, k0 + 512:k0 + 1536].rearrange("p (b t) -> p b t", b=2)
        c0 = k0 + 1536
        thc = r3[:, c0 + 256:c0 + 1280].rearrange("p (m t) -> p m t", m=MI)
        xcs = r3[:, k0 + 512:k0 + 1536].rearrange("p (m t) -> p m t", m=MI)
        BTs = r2[:, 14340:14852]
        btds = r2[:, 14852:15364].rearrange("p (i n) -> p i n", i=TPB)
        avs = r3[:, k0 + 324:k0 + 340].rearrange("p (i h) -> p i h", i=TPB)
        gm = r3[:, c0:c0 + 256].rearrange("p (b t) -> p b t", b=2)
        ed = r3[:, c0 + 256:c0 + 1280].rearrange("p (b h t) -> p b h t", b=2, h=NH)
        ec = r3[:, c0 + 1280:c0 + 2304].rearrange("p (b h t) -> p b h t", b=2, h=NH)
        mm = r3[:, c0 + 2304:c0 + 3328].rearrange("p (b h t) -> p b h t", b=2, h=NH)
        cs = r3[:, c0 + 3328:c0 + 4352].rearrange("p (b h t) -> p b h t", b=2, h=NH)
        dtx = r3[:, c0 + 4352:c0 + 4864].rearrange("p (b h d) -> p b h d", b=2, h=NH)
        dtw = r3[:, c0 + 4864:c0 + 5376].rearrange("p (b h d) -> p b h d", b=2, h=NH)
        hst = r3[:, c0 + 5376:c0 + 5632].rearrange("p (h d) -> p h d", h=NH)
        yg = r3[:, c0 + 5632:c0 + 6144].rearrange("p (b m t) -> p b m t", b=2, m=MI)

        ps = ctx.enter_context(nc.psum_tensor("ps", [P, 8, 512], F32))
        qd_dram = nc.dram_tensor("q_split_rows", (NSPLIT, P, T), BF16, kind="Internal").ap()
        kd_dram = nc.dram_tensor("k_split_rows", (NSPLIT * KV_W, T), BF16, kind="Internal").ap()

        s_x = [sem(f"x_loaded{i}") for i in range(4)]
        s_const = sem("consts_loaded")
        s_wqkv = sem("qkv_weights_loaded")
        s_w0 = sem("summary_weights_loaded")
        s_wrest = sem("gate_router_weights_loaded")
        s_v = sem("dve_steps")
        s_a = sem("act_steps")
        s_g = sem("pool_steps")
        s_var = sem("variance_ready")
        s_sd = sem("root_ready")
        s_xn = sem("xn_ready")
        s_xnT = sem("xn_transposed")
        s_xnTc = sem("xnT_copied")
        s_wsc = sem("qkv_weights_scaled")
        s_qkvp = sem("qkv_projected")
        s_qkvc = sem("qkv_copied")
        s_rot = sem("rotated")
        s_sq = sem("squared")
        s_ssq = sem("square_sums")
        s_qksd = sem("qk_root")
        s_split = sem("splits_ready")
        s_splT = sem("splits_transposed")
        s_splTa = sem("splits_copied_by_act")
        s_splTh = sem("first_halves_copied_by_act")
        s_splTv = sem("splits_copied_by_dve")
        s_qscr = [sem(f"q_split{i}_in_dram") for i in range(NSPLIT)]
        s_kscr = sem("k_splits_in_dram")
        s_qst = sem("stacks_loaded")
        s_qst2 = sem("other_groups_loaded")
        s_qgrp = sem("groups_loaded")
        s_pad = sem("stack_pads_zeroed")
        s_vp = sem("values_ready")
        s_sm = sem("summary_softmax_steps")
        s_rden = sem("sums_inverted")
        s_krow = sem("bound_row_ready")
        s_shift = sem("score_bound_ready")
        s_xti = sem("round_tiles_copied")
        s_mf = sem("shared_bank_filled")
        s_mr = sem("shared_bank_read")
        s_idb = sem("bf16_identity")

        s_summ = sem("chunk_means_ready")
        s_kv = sem("summary_kv_projected")
        s_kbd = sem("summary_kv_placed")
        s_gw = sem("summary_products_ready")
        s_gc = sem("summary_products_copied")
        s_sub = sem("summary_shifted")
        s_ex = sem("summary_exponentials")
        s_pr = sem("summary_probabilities")
        s_qk = sem("score_pairs")
        s_exp = sem("exponentials")
        s_msk = sem("diagonals_masked")
        s_pv = sem("value_products")
        s_vc = sem("group_values_copied")
        s_accc = sem("attention_block_copied")
        s_aT = sem("attention_transposed")
        s_aTc = sem("attention_T_copied")
        s_gp = sem("gate_projected")
        s_gt = sem("gate_ready")
        s_og = sem("gated")
        s_wo = sem("output_projected")
        s_xm = sem("x_mid_ready")
        s_sq2 = sem("x_mid_squared")
        s_ss2 = sem("x_mid_square_sums")
        s_sd2 = sem("x_mid_root")
        s_h2 = sem("h2_ready")
        s_h2T = sem("h2_transposed")
        s_h2Tc = sem("h2T_copied")
        s_lg = sem("router_logits")
        s_oh = sem("one_hot_ready")
        s_ohT = sem("one_hot_transposed")
        s_pen = sem("penalty_ready")
        s_moew = sem("expert_weights_loaded")
        s_up = sem("expert_up_products")
        s_sg = sem("expert_sigmoids")
        s_moea = sem("expert_activations")
        s_dn = sem("expert_down_products")
        s_yc = sem("expert_sums_copied")
        s_yt = sem("expert_sums_token_major")
        s_ohTc = sem("one_hot_rows_copied")
        s_whi = sem("expert_weights_high")
        s_wsp = sem("expert_weights_split")
        s_h2s = sem("h2_high_parts")
        s_h2l = sem("h2_low_parts")
        s_amh = sem("expert_products_high_parts")
        s_aml = sem("expert_products_split")
        s_ya = sem("expert_sums_added")
        s_l1w = sem("layer1_weights_loaded")
        s_var2 = sem("variance2_ready")
        s_sdl = sem("root2_ready")
        s_xn2 = sem("xn1_ready")
        s_xs = sem("xs_ready")
        s_xn2T = sem("xn1_transposed")
        s_xn2c = sem("xn1_T_copied")
        s_inp = sem("in_proj_scaled")
        s_pj = sem("ssm_projected")
        s_pja = sem("ssm_projections_read_by_act")
        s_pjv = sem("ssm_projections_read_by_dve")
        s_bt = sem("ssm_token_projected")
        s_btc = sem("ssm_token_copied")
        s_xcv = sem("convolved")
        s_xth = sem("convolution_tanh")
        s_dta = sem("dt_for_act")
        s_dtb = sem("dt_from_act")
        s_av = sem("decay_rates_ready")
        s_cstep = sem("chunk_dve_steps")
        s_stage = sem("block_operands_staged")
        s_c1 = sem("chunk_products")
        s_cd = sem("chunk_decay_difference")
        s_ce = sem("chunk_exponentials")
        s_cm = sem("chunk_operands_from_pool")
        s_cx = sem("chunk_operands_from_dve")
        s_cy = sem("chunk_outputs")
        s_cg = sem("chunk_gated")
        s_ch = sem("chunk_state_ready")
        s_co = sem("chunk_projected")
        s_ca = sem("chunk_added")
        s_fu = sem("ffn_up_products")
        s_ft = sem("ffn_tanh")
        s_fs = sem("ffn_scales_ready")
        s_fm = sem("ffn_silu_products")
        s_fg = sem("ffn_gated")
        s_f2 = sem("ffn_second_products")
        s_fg2 = sem("ffn_second_gelu")
        s_f3 = sem("ffn_third_products")
        s_fg3 = sem("ffn_third_gelu")
        s_f4 = sem("ffn_down_products")
        s_fr = sem("ffn_scaled")
        s_fh1 = sem("first_middle_weights_split")
        s_bn = sem("statistics_of_x1")
        s_diag = sem("taps_as_diagonals")
        s_xnd = sem("xn1_used")
        s_fhi = sem("ffn_weights_high")
        s_flo = sem("ffn_weights_split")
        s_fah = sem("ffn_gated_high")
        s_fal = sem("ffn_gated_split")
        s_fbh = sem("ffn_middle_high")
        s_fbl = sem("ffn_middle_split")
        s_fin = sem("result_ready")
        s_zth = sem("z_tanh")
        s_xc = sem("convolution_silu")
        s_cst = sem("chunk_state_products")
        s_out = sem("result_stored")

        def key_tiles(qb):
            diag, full = list(range(TPB * qb + 1, TPB * qb + TPB)), list(range(TPB * qb))
            head = [TPB * qb]
            while diag:
                head += full[:1] + diag[:1]
                full, diag = full[1:], diag[1:]
            return head + full

        BLOCKS = [(qb, kt, max(0, kt - TPB * qb) * P) for qb in range(NB) for kt in key_tiles(qb)]
        FIRST = [min(k for k, blk in enumerate(BLOCKS) if blk[0] == qb) for qb in range(NB)]
        LAST = [max(k for k, blk in enumerate(BLOCKS) if blk[0] == qb) for qb in range(NB)]
        LAG = 2
        KB = len(BLOCKS)
        PAIRS = 2 * KB
        SBUFS, PBUFS = 3, 8
        DIAG = [k for k, (qb, kt, _) in enumerate(BLOCKS) if kt >= TPB * qb]

        SHARED = 7
        AUX = sorted([(8 * m + s, what, m) for m in range(NB) for s, what in
                      ((1, "SCORE"), (6, "TRANSPOSE"), (8, "OUTPUT"))]
                     + [(LAST[qb] + LAG + 2 if qb < NB - 1 else KB + LAG - 1, "ATT", qb) for qb in range(NB)])
        NAUX = len(AUX)
        SUMM_EXP = {8 * m + 3: m for m in range(NB)}

        WSPLIT = [(w1f[:, 0:2048], w1hf[:, 0:2048], w1lf[:, 0:2048]), (w2f, w2hf, w2lf),
                  (w1f[:, 2048:4096], w1hf[:, 2048:4096], w1lf[:, 2048:4096])]

        def conv(dve, step, m, b):
            dst = xc[:, m, b * TB:b * TB + TB]
            for k in range(KW):
                src = xp[:, m, b * TB + k:b * TB + k + TB]
                if k == 0:
                    step.alone(dve.tensor_scalar(dst, src, convw[:, m, 0:1], convb[:, m:m + 1], ALU.mult, ALU.add))
                else:
                    step.alone(dve.scalar_tensor_tensor(dst, src, convw[:, m, k:k + 1], dst, ALU.mult, ALU.add))

        CONV_ON_PE = (1, 3)
        PROJ = []
        for b in range(NB):
            PROJ += [("T", 2 * b - 2), ("T", 2 * b - 1)] if b in (1, 2) else []
            PROJ += [(what, b) for what in ("z0", "z1", "x0", "x1", "C", "B")] + ([("K", b - 1)] if b - 1 in CONV_ON_PE else [])
            PROJ += [("A", 0)] if b == 2 else []
        PROJ += [("K", NB - 1)] if NB - 1 in CONV_ON_PE else []
        PROJ_ACT = [u for u in PROJ if u[0] in ("x0", "x1", "C", "T")]
        PROJ_DVE = [u for u in PROJ if u not in PROJ_ACT]

        def proj_bank(what, b):
            return PROJ.index((what, b)) % 8

        def summ_chunks(m):
            return (m + 1) * NC // NB

        LAYER1 = [("UP", 0), ("UP", 1), ("CHUNK", 0), ("UP", 2), ("UP", 3), ("CHUNK", 1), ("STATE", 0),
                  ("MID1", 0), ("MID1", 1), ("PROJECT", 0), ("CHUNK", 2), ("MID1", 2), ("STATE", 1),
                  ("MID1", 3), ("PROJECT", 1), ("CHUNK", 3), ("MID2", 0), ("STATE", 2), ("MID2", 1),
                  ("PROJECT", 2), ("MID2", 2), ("STATE", 3), ("MID2", 3), ("PROJECT", 3), ("DOWN", 0)]
        def placed(order, *extra):
            order = list(order)
            for new, after in extra:
                order.insert(order.index(after) + 1, new)
            return order

        ACT_ORDER = placed(LAYER1, *((("GATED", o), ("UP", min(o + 1, 3))) for o in (0, 1, 3, 2)))
        DVE_ORDER = placed(LAYER1, *((("GATED", o), ("UP", min(o + 1, 3))) for o in (0, 1, 3, 2)),
                           *((("WEIGHT", j), ("CHUNK", j)) for j in range(TPB)),
                           *((("MIDDLE", o), ("MID1", o + 1) if o < 3 else ("MID1", 3)) for o in (0, 1, 3, 2)))

        def ffn_bank(n):
            return 4 if n == 16 else 4 + (n + 1) % 4

        res_flat = res.rearrange("p i d -> p (i d)")

        def last_user(n, bufs, total):
            return max(m for m in range(total) if m % bufs == n % bufs)

        block = ctx.enter_context(nc.Block())

        @block.sync
        def _(sp):
            for q in range(4):
                sp.dma_start(res[:, 4 * q:4 * q + 4, :],
                             io["x"][512 * q:512 * q + 512, :].rearrange("(i p) d -> p i d", p=P)
                             ).then_inc(s_x[q], 16)
            sp.dma_start(consts[:, :], io["consts"]).then_inc(s_const, 16)
            sp.dma_start(wqkv, io["f_Wqkv"]).then_inc(s_wqkv, 16)
            sp.dma_start(bqkv, io["f_bqkv"].broadcast_to([P, QKV_W])).then_inc(s_wqkv, 16)
            sp.dma_start(qn_bc, io["f_qn"].broadcast_to([P, QD])).then_inc(s_wqkv, 16)
            sp.dma_start(kn_bc, io["f_kn"].broadcast_to([P, QD])).then_inc(s_wqkv, 16)
            sp.dma_start(ln1, io["f_ln1"]).then_inc(s_wqkv, 16)
            sp.dma_start(wqT, io["a_WqT"].rearrange("(j p) d -> p j d", p=P)).then_inc(s_w0, 16)
            sp.dma_start(wk0, io["a_Wk"]).then_inc(s_w0, 16)
            sp.dma_start(wv0, io["a_Wv"]).then_inc(s_w0, 16)
            sp.dma_start(wo0, io["a_Wo"].rearrange("(j p) d -> p j d", p=P)).then_inc(s_w0, 16)
            for dst, name in ((bq0, "a_bq"), (bk0, "a_bk"), (bv0, "a_bv")):
                sp.dma_start(dst, io[name]).then_inc(s_w0, 16)
            sp.dma_start(cmask, io["cmask"]).then_inc(s_w0, 16)
            sp.dma_start(bo0_bc, io["a_bo"].broadcast_to([P, D])).then_inc(s_w0, 16)
            sp.wait_ge(s_pad, 2)
            for h in range(NQ):
                sp.dma_start(wg[QD * h:QD * h + QD, QD * h:QD * h + QD], io["f_Wg"]).then_inc(s_wrest, 16)
            for dst, name in ((wo, "f_Wo"), (wr, "f_Wr"), (ln2, "f_ln2"), (b2, "f_b2"), (row[:, 240:272], "f_b1c"),
                              (bgc, "f_bgc")):
                sp.dma_start(dst, io[name]).then_inc(s_wrest, 16)
            for dst, name, n in ((bo_bc, "f_bo", D), (br_bc, "f_br", E), (rank, "rank", E)):
                sp.dma_start(dst, io[name].broadcast_to([P, n])).then_inc(s_wrest, 16)
            def load_q(i, heads, loaded):
                sp.dma_start(qst[24 * i:24 * i + 24, heads, :].rearrange("p h t -> p (h t)"),
                             qd_dram[i].rearrange("(d h) t -> d h t", h=NQ)[:, heads, :].rearrange(
                                 "d h t -> d (h t)").unsqueeze(0).broadcast_to(
                                 [NSPLIT, QD, (heads.stop - heads.start) * T])).then_inc(loaded, 16)

            sp.wait_ge(s_pad, 1)
            for i in range(NSPLIT):
                if i == NSPLIT - 1:
                    sp.wait_ge(s_splTa, 3)
                    sp.wait_ge(s_splTh, 3)
                    sp.dma_start(kd_dram, kT[0:NSPLIT * KV_W, :]).then_inc(s_kscr, 16)
                if i == NSPLIT - 1:
                    sp.wait_ge(s_splTa, 4)
                    sp.wait_ge(s_splTv, 1)
                else:
                    sp.wait_ge(s_splTa, i + 1)
                    sp.wait_ge(s_splTh, i + 1)
                sp.dma_start(qd_dram[i], qT[:, i, :]).then_inc(s_qscr[i], 16)
                if i == NSPLIT - 1:
                    sp.wait_ge(s_kscr, 16)
                    for k in range(NSPLIT):
                        sp.dma_start(kst[24 * k:24 * k + 24, :, :].rearrange("p g t -> p (g t)"),
                                     kd_dram.rearrange("(r g) t -> r (g t)", g=NKV)).then_inc(s_qst, 16)
                sp.wait_ge(s_qscr[i], 16)
                load_q(i, slice(0, REP), s_qst)
                for n in {0: (0,), 2: (1, 2)}.get(i, ()):
                    load_q(n, slice(REP, NQ), s_qst2)
            sp.wait_ge(s_qst, 16 * 2 * NSPLIT)
            sp.sem_inc(s_qgrp, 1)
            sp.wait_ge(s_qst2, 16 * NSPLIT)
            sp.sem_inc(s_qgrp, NKV - 1)
            sp.wait_ge(s_pv, KB * (NKV + 1))
            sp.dma_start(w1, io["f_W1"].rearrange("e p f -> p e f")).then_inc(s_moew, 16)
            sp.dma_start(w2, io["f_W2"].rearrange("e (c p) d -> p e c d", p=P)).then_inc(s_moew, 16)
            sp.wait_ge(s_h2Tc, NB)
            for dst, name in ((inp, "s_inT"), (f1, "g_w1T"), (f2, "g_w2T"),
                              (normw, "s_norm"), (convb, "s_convb"), (d2, "s_D"), (row[:, 284:292], "s_convw"),
                              (w1s, "g_w1s"), (w2s, "g_w2s"), (h1s, "g_h1s"), (h2s, "g_h2s")):
                sp.dma_start(dst, io[name]).then_inc(s_l1w, 16)
            sp.dma_start(owT, io["s_outT"].rearrange("(m p) d -> p m d", p=P)).then_inc(s_l1w, 16)
            for dst, name in ((fh1, "g_h1T"), (fh2, "g_h2T"), (f3, "g_w3T")):
                sp.dma_start(dst, io[name].rearrange("(k p) o -> p k o", p=P)).then_inc(s_l1w, 16)
            for dst, name, n in ((dtb, "s_dtb", NH), (alog, "s_Alog", NH), (w3s_bc, "g_w3s", D)):
                sp.dma_start(dst, io[name].broadcast_to([P, n])).then_inc(s_l1w, 16)
            for b in range(NB):
                sp.wait_ge(s_fin, b + 1)
                sp.dma_start(out[TB * b:TB * b + TB, :].rearrange("(i p) d -> p i d", p=P),
                             res[:, TPB * b:TPB * b + TPB, :]).then_inc(s_out, 16)
            sp.wait_ge(s_out, 16 * NB)

        @block.gpsimd
        def _(pool):
            step = Steps(pool, s_g)
            pool.memset(r2[64:P, :], 0.0).then_inc(s_pad, 1)
            pool.wait_ge(s_pad, 1)
            step.alone(pool.memset(vp[:, :, :, :], 0.0))
            pool.memset(vp[:, :, :, QD:QD + 1], 1.0).then_inc(s_vp, 1)
            step.alone(pool.memset(kbd[:, :, :, :], 0.0))
            step.alone(pool.memset(vbd[:, :, :, :], 0.0))
            pool.memset(wg, 0.0).then_inc(s_pad, 1)
            pool.wait_ge(s_pad, 2)
            pool.memset(r2[96:97, 0:NQ * T // 2], TWO_ONES).then_inc(s_pad, 1)
            pool.wait_ge(s_pad, 3)
            pool.wait_ge(s_gw, 1)
            pool.memset(pr[:, :, :], 0.0).then_inc(s_pad, 1)
            pool.sem_inc(s_pv, KB)
            xnT_blocks = xnT.rearrange("p (m c) -> p m c", m=NB)
            pool.wait_ge(s_pad, 4)
            pool.wait_ge(s_qst, 16 * 2 * NSPLIT)
            with pool.Fori(0, NKV) as g:
                pool.wait_ge(s_pv, g * KB + KB)
                pool.tensor_copy(xti, xnT_blocks[:, :, bass.ds(g * P, P)]).then_inc(s_xti, 1)
                for k in DIAG:
                    off = BLOCKS[k][2]
                    for n in (2 * k, 2 * k + 1):
                        pool.wait_ge(s_exp, g * PAIRS + (PAIRS + n + 1))
                        blk = probs[:, n % PBUFS, :, off:off + P]
                        pool.tensor_tensor(blk, blk, along(tri, 2), ALU.mult).then_inc(s_msk, 1)
            pool.wait_ge(s_mr, NKV * NAUX + 1)
            step.alone(pool.memset(onee, 1.0))
            pool.affine_select(out=onee, in_=onee, compare_op=ALU.is_equal, fill=0.0, base=0,
                               pattern=[[-1, E], [0, P]], channel_multiplier=1).then_inc(s_idb, 1)
            for n, (w, hi, lo) in enumerate(WSPLIT):
                pool.wait_ge(s_whi, n + 1)
                pool.tensor_tensor(lo, w, hi, ALU.subtract).then_inc(s_wsp, 1)
                pool.wait_ge(s_wsp, n + 1)
            pool.wait_ge(s_l1w, 16 * 18)
            step.mark(pool.tensor_scalar(inp, inp, normw, None, ALU.mult))
            step.mark(pool.tensor_scalar(owT, owT, 0.5, None, ALU.mult))
            step.mark(pool.tensor_scalar(d2, d2, 0.5, None, ALU.mult))
            step.mark(pool.tensor_scalar(w1sh, w1s, 0.5, None, ALU.mult))
            step.settle()
            pool.tensor_tensor(s12, w1sh, w2s, ALU.mult).then_inc(s_fs, 1)
            pool.sem_inc(s_inp, 1)
            pool.wait_ge(s_ya, NB + 1)
            pool.memset(xp[:, :, 0:KW - 1], 0.0).then_inc(s_pad, 1)
            pool.wait_ge(s_pad, 5)
            pool.memset(hst, 0.0).then_inc(s_ch, 1)
            for k in range(KW):
                step.alone(pool.tensor_scalar(cdiag[:, k, :], ident, convw[:, 1, k:k + 1], None, ALU.mult))
            pool.sem_inc(s_diag, 1)
            pool.wait_ge(s_xn2, NT)
            pool.tensor_tensor(res, res, xn, ALU.add).then_inc(s_xnd, 1)
            pool.wait_ge(s_xnd, 1)
            for n, (whole, hi, lo) in enumerate(FSPLIT[:-1]):
                pool.wait_ge(s_fhi, n + 1)
                pool.tensor_tensor(lo, whole, hi, ALU.subtract).then_inc(s_flo, 1)
                pool.wait_ge(s_flo, n + 1)
            pool.wait_ge(s_pja, PROJ_ACT.index(("C", NB - 1)) + 1)
            pool.wait_ge(s_pjv, PROJ_DVE.index(("B", NB - 1)) + 1)
            pool.wait_ge(s_av, 1)
            pool.wait_ge(s_btc, 6)
            pool.sem_inc(s_cm, 4)
            with pool.Fori(0, NB) as blk_i:
                toks = bass.ds(blk_i * TB, TB)
                pool.wait_ge(s_cg, blk_i * TPB + 1)
                pool.wait_ge(s_xc, blk_i + 1)
                pool.tensor_copy(xcs, xc[:, :, toks]).then_inc(s_stage, 1)
                pool.tensor_copy(BTs, BT[:, toks]).then_inc(s_stage, 1)
                pool.tensor_copy(avs, av[:, bass.ds(blk_i * TPB, TPB), :]).then_inc(s_stage, 1)
                pool.tensor_copy(btds, btd[:, bass.ds(blk_i * TPB, TPB), 0:P]).then_inc(s_stage, 1)
                for j in range(TPB):
                    b = j % 2
                    pool.wait_ge(s_cy, blk_i * TPB + (j + 1))
                    pool.wait_ge(s_ce, blk_i * (2 * TPB) + (2 * j + 3))
                    pool.wait_ge(s_cx, blk_i * (2 * TPB) + (2 * j + 3))
                    pool.tensor_tensor(mm[:, b], ed[:, b], along(gm[:, b, :], NH), ALU.mult).then_inc(s_cm, 1)
                    pool.wait_ge(s_ce, blk_i * (2 * TPB) + (2 * j + 4))
                    pool.tensor_tensor(cs[:, b], ec[:, b], along(CT[:, bass.ds(blk_i * TB + j * P, P)], NH),
                                       ALU.mult).then_inc(s_cm, 1)

        @block.scalar
        def _(act):
            step = Steps(act, s_a)
            act.wait_ge(s_var, 1)
            act.activation(sd, mv[:, :, 1], ACT.Sqrt, bias=LN_EPS).then_inc(s_sd, 1)
            act.wait_ge(s_var, 2)
            act.activation(sd2, ms, ACT.Sqrt, bias=RMS_EPS).then_inc(s_sd, 1)
            for b in range(NB):
                act.wait_ge(s_xnT, b + 1)
                act.activation(xnT[:, b * TB:b * TB + TB], ps[:, b, :], ACT.Copy).then_inc(s_xnTc, 1)
            act.wait_ge(s_rot, 1)
            act.activation(sq, rot, ACT.Square).then_inc(s_sq, 1)
            act.wait_ge(s_ssq, 1)
            act.activation(rr, ssq, ACT.Sqrt, bias=RMS_EPS, scale=1.0 / QD).then_inc(s_qksd, 1)
            act.wait_ge(s_gw, 1)
            act.activation(gmat, ps[:, 1, :].rearrange("p (h c) -> p h c", h=HEADS), ACT.Copy).then_inc(s_gc, 1)
            act.activation(g0, ps[:, 2, :].rearrange("p (h c) -> p h c", h=HEADS), ACT.Copy).then_inc(s_gc, 1)
            act.activation(vw, ps[:, 3, :].rearrange("p (q d) -> p q d", q=4), ACT.Copy).then_inc(s_gc, 1)
            for t, n in enumerate((0, 1, 2, 3, 6, 7, 4)):
                act.wait_ge(s_splT, t + 1)
                src = ps[:, n, :].bitcast(BF16)
                half = slice(1024 * (n % 2), 1024 * (n % 2) + 1024)
                if n < 6:
                    m = act.activation(qT[:, n // 2, half], src, ACT.Copy)
                else:
                    m = act.activation(kT[0:96, half], src[0:96, :], ACT.Copy)
                if n % 2 == 1 or n == 4:
                    m.then_inc(s_splTa, 1)
                else:
                    m.then_inc(s_splTh, 1)
            act.wait_ge(s_pad, 3)
            act.wait_ge(s_shift, 1)
            act.activation(kst[96:97, :, :], qst[96:97, 0:NKV, :], ACT.Copy, scale=shift[96:97, :]
                           ).then_inc(s_krow, 1)
            act.sem_inc(s_exp, PAIRS)
            step.alone(act.activation(warm[:, 0:1], sd[:, 0:1], ACT.Copy))
            with act.Fori(0, NKV) as g:
                act.activation(warm[:, 1:2], warm[:, 0:1], ACT.Exp)
                for k, (qb, kt, off) in enumerate(BLOCKS):
                    for n in (2 * k, 2 * k + 1):
                        act.wait_ge(s_qk, g * PAIRS + (n + 1))
                        free = KB + (n - PBUFS) // 2 + 1 if n >= PBUFS else last_user(n, PBUFS, PAIRS) // 2 + 1
                        act.wait_ge(s_pv, g * KB + free)
                        b = 2 * (n % SBUFS)
                        act.activation(probs[:, n % PBUFS, :, off:TB], ps[:, b:b + 2, off:TB], ACT.Exp
                                       ).then_inc(s_exp, 1)
                    if k in SUMM_EXP:
                        m = SUMM_EXP[k]
                        act.wait_ge(s_sub, g * NB + (m + 1))
                        blk = sc[:, m % 2, :, 0:summ_chunks(m)]
                        act.activation(blk, blk, ACT.Exp).then_inc(s_ex, 1)
            for b in range(NB):
                act.wait_ge(s_aT, b + 1)
                act.activation(oT[:, b * TB:b * TB + TB], ps[:, 4 + b, :], ACT.Copy).then_inc(s_aTc, 1)
            act.wait_ge(s_wrest, 16 * 25)
            for b in range(NB):
                act.wait_ge(s_gp, b + 1)
                act.activation(gate[:, b * TB:b * TB + TB], ps[:, b, :], ACT.Sigmoid, bias=bgc).then_inc(s_gt, 1)
            for b in range(NB):
                act.wait_ge(s_xm, b + 1)
                act.activation(sqm[:, TPB * b:TPB * b + TPB, :], xn[:, TPB * b:TPB * b + TPB, :], ACT.Square
                               ).then_inc(s_sq2, 1)

            def weights_high(n):
                w, hi, _ = WSPLIT[n]
                act.wait_ge(s_moew, 32)
                act.activation(hi, w, ACT.Copy).then_inc(s_whi, 1)

            act.wait_ge(s_ss2, NB)
            act.activation(sdm, ssq2, ACT.Sqrt, bias=RMS_EPS, scale=1.0 / D).then_inc(s_sd2, 1)
            weights_high(0)
            for b in range(NB):
                act.wait_ge(s_h2T, b + 1)
                act.activation(h2T[:, b * TB:b * TB + TB], ps[:, b, :], ACT.Copy, scale=ln2).then_inc(s_h2Tc, 1)
            weights_high(1)
            for b in range(NB):
                act.wait_ge(s_h2Tc, b + 1)
                act.activation(h2h[:, b * TB:b * TB + TB], h2T[:, b * TB:b * TB + TB], ACT.Copy).then_inc(s_h2s, 1)
            weights_high(2)
            act.wait_ge(s_pen, 1)
            act.activation(ohT, ps[0:E, 4:8, :].rearrange("p b t -> p (b t)"), ACT.Copy).then_inc(s_ohTc, 1)
            act.sem_inc(s_yc, 1)
            with act.Fori(0, NB) as tb:
                act.activation(warm[:, 1:2], warm[:, 0:1], ACT.Sigmoid)
                for n in range(E * FC):
                    e, c = divmod(n, FC)
                    act.wait_ge(s_up, tb * (E * FC) + (n + 1))
                    free = E * FC + n - 2 if n >= 3 else last_user(n, 3, E * FC) + 1
                    act.wait_ge(s_moea, tb * (E * FC) + free)
                    act.activation(sg[:, n % 3, :], ps[:, 2 * (n % 3) + 1, :], ACT.Sigmoid,
                                   bias=b1c[:, e, FC + c:FC + c + 1]).then_inc(s_sg, 1)
                act.wait_ge(s_dn, tb * (E * FC) + 2 * E * FC)
                act.wait_ge(s_yt, tb + 1)
                act.activation(yT, ps[:, 6, :], ACT.Copy).then_inc(s_yc, 1)
            act.wait_ge(s_var2, 1)
            act.activation(sd, mv[:, :, 1], ACT.Sqrt, bias=LN_EPS).then_inc(s_sdl, 1)
            act.wait_ge(s_var2, 2)
            act.activation(sd2, ms, ACT.Sqrt, bias=RMS_EPS).then_inc(s_sdl, 1)
            for b in range(NB):
                act.wait_ge(s_xn2T, b + 1)
                act.activation(xsT[:, b * TB:b * TB + TB], ps[:, b, :], ACT.Copy).then_inc(s_xn2c, 1)
            act.wait_ge(s_dta, 1)
            act.activation(ea, alog, ACT.Exp).then_inc(s_dtb, 1)
            act.activation(dl, dl, ACT.Exp).then_inc(s_dtb, 1)
            act.wait_ge(s_dtb, 2)
            act.activation(dl, dl, ACT.Ln, bias=1.0).then_inc(s_dtb, 1)
            act.sem_inc(s_fg3, FO)
            act.sem_inc(s_ce, 2)
            for b in range(NB):
                toks = slice(b * TB, b * TB + TB)
                for k, what in enumerate(("z0", "z1", "x0", "x1", "C")):
                    act.wait_ge(s_pj, PROJ.index((what, b)) + 1)
                    src = ps[:, proj_bank(what, b), :]
                    if k < 2:
                        if b >= 1:
                            act.wait_ge(s_pjv, PROJ_DVE.index((what, b - 1)) + 1)
                        act.activation(th[:, k, :], src, ACT.Tanh, scale=0.5).then_inc(s_zth, 1)
                    else:
                        dst = xp[:, k - 2, KW - 1 + b * TB:KW - 1 + b * TB + TB] if k < 4 else CT[:, toks]
                        act.activation(dst, src, ACT.Copy).then_inc(s_pja, 1)
                for c in (2 * b, 2 * b + 1) if b < 2 else ():
                    act.wait_ge(s_pj, PROJ.index(("T", c)) + 1)
                    act.activation(xnT[:, c * TB:c * TB + TB], ps[:, proj_bank("T", c), :], ACT.Copy
                                   ).then_inc(s_pja, 1)
                for c in {0: (), NB - 1: (NB - 2, NB - 1)}.get(b, (b - 1,)):
                    act.wait_ge(s_xcv, c + 1)
                    if c >= 1:
                        act.wait_ge(s_xc, c)
                    act.activation(thc, xc[:, :, c * TB:c * TB + TB], ACT.Tanh, scale=0.5).then_inc(s_xth, 1)
                if b == 1:
                    act.wait_ge(s_l1w, 16 * 18)
                    act.wait_ge(s_xnd, 1)
                    act.wait_ge(s_pja, PROJ_ACT.index(("T", NB - 1)) + 1)
                for whole, hi, _ in FSPLIT[0:2] if b == 1 else FSPLIT[2:-1] if b == 2 else ():
                    act.activation(hi, whole, ACT.Copy).then_inc(s_fhi, 1)
            act.wait_ge(s_xcv, NB)
            act.activation(fh1h, fh1, ACT.Copy).then_inc(s_fhi, 1)
            with act.Fori(0, NB) as blk_i:
                act.activation(warm[:, 1:2], warm[:, 0:1], ACT.Exp)
                for what, o in ACT_ORDER:
                    if what == "UP":
                        act.wait_ge(s_fu, blk_i * FO + (o + 1))
                        free = FO + o - 1 if o >= 2 else FO - 1 + o
                        act.wait_ge(s_fm, blk_i * FO + free)
                        act.activation(fth[:, o % 2, :], ps[:, ffn_bank(2 * o), :], ACT.Tanh,
                                       scale=w1sh[:, o:o + 1]).then_inc(s_ft, 1)
                    elif what == "GATED":
                        act.wait_ge(s_fg, blk_i * FO + (o + 1))
                        act.wait_ge(s_f2, blk_i * FO + FO)
                        act.activation(fah[:, o, :], fa[:, o, :], ACT.Copy).then_inc(s_fah, 1)
                    elif what == "MID1":
                        act.wait_ge(s_f2, blk_i * FO + (FO + o + 1))
                        act.wait_ge(s_f3, blk_i * FO + FO)
                        act.activation(fb[:, o, :], ps[:, ffn_bank(8 + o), :], ACT.Gelu, scale=h1s[:, o:o + 1]
                                       ).then_inc(s_fg2, 1)
                        act.wait_ge(s_fg2, blk_i * FO + (o + 1))
                        act.activation(fbh[:, o, :], fb[:, o, :], ACT.Copy).then_inc(s_fbh, 1)
                    elif what == "MID2":
                        act.wait_ge(s_f3, blk_i * FO + (FO + o + 1))
                        act.activation(fa[:, o, :], ps[:, ffn_bank(12 + o), :], ACT.Gelu, scale=h2s[:, o:o + 1]
                                       ).then_inc(s_fg3, 1)
                    elif what == "CHUNK":
                        b = o % 2
                        act.wait_ge(s_cd, blk_i * TPB + (o + 1))
                        act.activation(ed[:, b], ed[:, b], ACT.Exp).then_inc(s_ce, 1)
                        act.wait_ge(s_c1, blk_i * TPB + (o + 1))
                        act.wait_ge(s_cm, blk_i * (2 * TPB) + (2 * o + 2))
                        act.wait_ge(s_ch, blk_i * TPB + (o + 1))
                        act.activation(ec[:, b], ps[:, 1, :].rearrange("p (h t) -> p h t", h=NH), ACT.Exp
                                       ).then_inc(s_ce, 1)

        @block.tensor
        def _(pe):
            pe.wait_ge(s_const, 16)
            for b in range(NB):
                for i in range(TPB * b, TPB * b + TPB):
                    pe.wait_ge(s_xn, i + 1)
                    m = pe.transpose(ps[:, b, (i % TPB) * P:(i % TPB) * P + P], xn[:, i, :], ident)
                m.then_inc(s_xnT, 1)
            pe.wait_ge(s_wsc, 1)
            for i in range(NT):
                pe.wait_ge(s_xnTc, i // TPB + 1)
                if i >= 8:
                    pe.wait_ge(s_qkvc, i - 8 + 2 - i % 2)
                m = pe.matmul(ps[:, 4 + (i // 2) % 4, (i % 2) * QKV_W:(i % 2) * QKV_W + QKV_W],
                              xnT[:, i * P:i * P + P], wqkv, start=True, stop=True)
                m.then_inc(s_qkvp, 1)
            pe.wait_ge(s_w0, 16 * 9)
            pe.wait_ge(s_summ, 2)
            for j in range(HC):
                pe.matmul(ps[:, 0, NC * j:NC * j + NC], wk0[:, P * j:P * j + P], summT, start=True, stop=True)
            for j in range(HC):
                m = pe.matmul(ps[:, 0, 256 + NC * j:256 + NC * j + NC], wv0[:, P * j:P * j + P], summT,
                              start=True, stop=True)
            m.then_inc(s_kv, 1)
            pe.wait_ge(s_kbd, 2)
            for j in range(HC):
                kj = kbd[:, j].rearrange("p a c -> p (a c)")
                pe.matmul(ps[:, 1, 64 * j:64 * j + 64], wqT[:, j, :], kj, start=True, stop=True)
                pe.matmul(ps[:, 2, 64 * j:64 * j + 64], bq0[:, j:j + 1].broadcast_to([P, P]), kj,
                          start=True, stop=True)
            for j in range(HC):
                m = pe.matmul(ps[64 * (j % 2):64 * (j % 2) + 64, 3, P * (j // 2):P * (j // 2) + P],
                              vbd[:, j].rearrange("p a c -> p (a c)"), wo0[:, j, :], start=True, stop=True)
            m.then_inc(s_gw, 1)
            pe.wait_ge(s_gc, 3)
            pe.wait_ge(s_idb, 1)
            pe.wait_ge(s_qkvc, NT)
            pe.wait_ge(s_gc, 3)
            for n in (0, 1, 2, 3, 6, 7, 4, 5):
                pe.wait_ge(s_split, min(n // 2, NSPLIT - 1) + 1)
                dst = ps[:, n, :].bitcast(BF16)
                for i in range(8 * (n % 2), 8 * (n % 2) + 8):
                    c = (i % 8) * P
                    if n < 6:
                        m = pe.transpose(dst[:, c:c + P], qs[:, i, n // 2, :], identb)
                    else:
                        m = pe.transpose(dst[0:96, c:c + P],
                                         ks[:, i, :, :].rearrange("p s c -> p (s c)"), identb)
                m.then_inc(s_splT, 1)
            pe.wait_ge(s_splTa, 4)
            pe.wait_ge(s_splTv, 1)
            pe.wait_ge(s_qst, 16 * 2 * NSPLIT)
            pe.wait_ge(s_pad, 4)
            pe.wait_ge(s_krow, 1)
            qst_flat = r2[:, 0:16384].bitcast(BF16)
            kst_flat = r2[:, 16384:20480].bitcast(BF16)
            with pe.Fori(0, NKV) as g:
                pe.wait_ge(s_qgrp, g + 1)
                for k in range(KB + LAG):
                    if k < KB:
                        qb, kt, off = BLOCKS[k]
                        for pair in range(2):
                            n = 2 * k + pair
                            free = PAIRS + n - SBUFS + 1 if n >= SBUFS else last_user(n, SBUFS, PAIRS) + 1
                            pe.wait_ge(s_exp, g * PAIRS + free)
                            for h in range(2):
                                m = pe.matmul(ps[:, 2 * (n % SBUFS) + h, off:TB],
                                              kst_flat[:, bass.ds(g * T + kt * P, P)],
                                              qst_flat[:, bass.ds(g * (REP * T) + ((2 * pair + h) * T + qb * TB + off),
                                                                  TB - off)],
                                              start=True, stop=True)
                            m.then_inc(s_qk, 1)
                    if k >= LAG:
                        v = k - LAG
                        qb, kt, off = BLOCKS[v]
                        if v == 0:
                            pe.wait_ge(s_vc, g + 1)
                        if v == FIRST[qb]:
                            pe.wait_ge(s_accc, g * NB + (qb + 1))
                        if kt >= TPB * qb:
                            pe.wait_ge(s_msk, g * (2 * len(DIAG)) + 2 * (DIAG.index(v) + 1))
                        else:
                            pe.wait_ge(s_exp, g * PAIRS + (PAIRS + 2 * v + 2))
                        for j in range(REP):
                            m = pe.matmul(ps[32 * j:32 * j + 32, 6, off:TB], vc[:, kt, :],
                                          probs[:, (2 * v + j // 2) % PBUFS, j % 2, off:TB],
                                          start=(v == FIRST[qb]), stop=(v == LAST[qb]))
                        m.then_inc(s_pv, 1)
                    for n, (_, what, m) in enumerate(AUX):
                        if AUX[n][0] != k:
                            continue
                        pe.wait_ge(s_mr, g * NAUX + (n + 1))
                        if what == "SCORE":
                            pe.wait_ge(s_xti, g + 1)
                            w = summ_chunks(m)
                            a = pe.matmul(ps[:, SHARED, 0:HEADS * w].rearrange("p (h c) -> p h c", h=HEADS),
                                          xti[:, m, :], gmat[:, :, 0:w], start=True, stop=True)
                        elif what == "TRANSPOSE":
                            pe.wait_ge(s_pr, g * NB + (m + 1))
                            for q in range(4):
                                a = pe.transpose(ps[:, SHARED, P * q:P * q + P], pr[:, m, P * q:P * q + P], ident)
                        elif what == "OUTPUT":
                            for q in range(4):
                                a = pe.matmul(ps[:, SHARED, 0:D], ptr[:, P * q:P * q + P], vw[:, q, :],
                                              start=(q == 0), stop=(q == 3))
                        else:
                            pe.wait_ge(s_accc, g * NB + (m + 2))
                            for i in range(TPB):
                                a = pe.transpose(ps[:, SHARED, P * i:P * i + P], accT[:, m % 2, P * i:P * i + P],
                                                 ident)
                        a.then_inc(s_mf, 1)
            for b in range(NB):
                pe.wait_ge(s_mr, NKV * NAUX + 1)
                for i in range(TPB):
                    m = pe.transpose(ps[:, 4 + b, P * i:P * i + P], att[:, TPB * b + i, :], ident)
                m.then_inc(s_aT, 1)
            pe.wait_ge(s_wrest, 16 * 25)
            for b in range(NB):
                pe.wait_ge(s_aTc, b + 1)
                pe.matmul(ps[:, b, :], wg, oT[:, b * TB:b * TB + TB], start=True, stop=True).then_inc(s_gp, 1)
            for b in range(NB):
                pe.wait_ge(s_og, b + 1)
                for i in range(TPB):
                    t = (TPB * b + i) * P
                    m = pe.matmul(ps[:, 4 + b, P * i:P * i + P], oT[:, t:t + P], wo, start=True, stop=True)
                m.then_inc(s_wo, 1)
            for b in range(NB):
                pe.wait_ge(s_h2, TPB * (b + 1))
                for i in range(TPB):
                    m = pe.transpose(ps[:, b, P * i:P * i + P], h2[:, TPB * b + i, :], ident)
                m.then_inc(s_h2T, 1)
            pe.wait_ge(s_xm, NB)
            for i in range(NT):
                pe.wait_ge(s_h2Tc, i // TPB + 1)
                m = pe.matmul(ps[:, 4, E * i:E * i + E], h2T[:, i * P:i * P + P], wr, start=True, stop=True)
            m.then_inc(s_lg, 1)
            pe.wait_ge(s_oh, 1)
            for i in range(NT):
                m = pe.transpose(ps[0:E, 4 + i // TPB, P * (i % TPB):P * (i % TPB) + P], oh[:, i, :], ident)
            m.then_inc(s_ohT, 1)
            pe.wait_ge(s_wsp, 2)
            pe.wait_ge(s_h2l, NB)
            pe.wait_ge(s_pen, 1)
            pe.wait_ge(s_idb, 2)
            ES = E * FC
            pe.sem_inc(s_dn, ES)
            pe.sem_inc(s_yt, 1)
            with pe.Fori(0, NB) as tb:
                for n in range(ES + 2):
                    if n < ES:
                        e, c = divmod(n, FC)
                        free = ES + n - 2 if n >= 3 else last_user(n, 3, ES) + 1
                        if n == 2:
                            pe.wait_ge(s_ohTc, 1)
                        if n == ES // 2:
                            pe.wait_ge(s_wsp, 3)
                        pe.wait_ge(s_moea, tb * ES + free)
                        toks = bass.ds(tb * TB, TB)
                        b = 2 * (n % 3)
                        halves = [(w1h[:, e, a:a + P], w1l[:, e, a:a + P]) for a in (P * c, HID + P * c)]
                        x = (h2h[:, toks], h2l[:, toks])
                        product(pe, ps[:, b + 1, :], halves[1], x, start=True, stop=False)
                        pe.matmul(ps[:, b + 1, :], onee[:, e, :], pen[:, toks], start=False, stop=True)
                        product(pe, ps[:, b, :], halves[0], x, start=True, stop=True).then_inc(s_up, 1)
                    if n == 0:
                        pe.wait_ge(s_ohTc, 1)
                        pe.wait_ge(s_yc, tb + 1)
                        pe.matmul(ps[:, 6, :], b2, ohT[:, toks], start=True, stop=False)
                    if n >= 2:
                        e, c = divmod(n - 2, FC)
                        pe.wait_ge(s_aml, tb * ES + (n - 1))
                        product(pe, ps[:, 6, :], (w2h[:, e, c, :], w2l[:, e, c, :]),
                                (amh[:, (n - 2) % 3, :], aml[:, (n - 2) % 3, :]),
                                start=False, stop=(n == ES + 1)).then_inc(s_dn, 1)
                pe.wait_ge(s_yc, tb + 2)
                pe.wait_ge(s_ya, tb + 1)
                for i in range(TPB):
                    m = pe.transpose(ps[:, 7, P * i:P * i + P], yT[:, P * i:P * i + P], ident)
                m.then_inc(s_yt, 1)
            pe.wait_ge(s_ya, NB + 1)
            for b in range(NB):
                for i in range(TPB):
                    t = b * TPB + i
                    pe.wait_ge(s_xs, t + 1)
                    m = pe.transpose(ps[:, b, P * i:P * i + P], xs[:, t, :], ident)
                m.then_inc(s_xn2T, 1)
            pe.wait_ge(s_inp, 1)
            pe.wait_ge(s_xn2c, NB)
            for credit, n in ((s_f2, FO), (s_f3, FO), (s_f4, 1), (s_cy, 2), (s_cst, 2), (s_co, 2)):
                pe.sem_inc(credit, n)
            for i in range(NT):
                m = pe.matmul(ps[:, i // 3, 132 * (i % 3):132 * (i % 3) + 132], xsT[:, i * P:i * P + P],
                              inp[:, 640:772], start=True, stop=True)
                if i % 3 == 2 or i == NT - 1:
                    m.then_inc(s_bt, 1)
            for u, (what, b) in enumerate(PROJ):
                if u >= 8:
                    before = PROJ[u - 8]
                    if before in PROJ_ACT:
                        pe.wait_ge(s_pja, PROJ_ACT.index(before) + 1)
                    else:
                        pe.wait_ge(s_pjv, PROJ_DVE.index(before) + 1)
                elif u < 6:
                    pe.wait_ge(s_btc, u + 1)
                if what == "K":
                    pe.wait_ge(s_diag, 1)
                    pe.wait_ge(s_pad, 5)
                    pe.wait_ge(s_pja, PROJ_ACT.index(("x1", b)) + 1)
                    for k in range(KW):
                        m = pe.matmul(ps[:, u % 8, :], cdiag[:, k, :], xp[:, 1, b * TB + k:b * TB + k + TB],
                                      start=(k == 0), stop=(k == KW - 1))
                    m.then_inc(s_pj, 1)
                elif what == "T":
                    for i in range(TPB):
                        pe.wait_ge(s_xn2, TPB * b + i + 1)
                        m = pe.transpose(ps[:, u % 8, P * i:P * i + P], xn[:, TPB * b + i, :], ident)
                    m.then_inc(s_pj, 1)
                elif what == "A":
                    pe.wait_ge(s_av, 1)
                    pe.matmul(ps[:, u % 8, 0:NT * NH], tri, av.rearrange("p i h -> p (i h)"), start=True, stop=True
                              ).then_inc(s_pj, 1)
                else:
                    k = ("z0", "z1", "x0", "x1", "C", "B").index(what)
                    pe.matmul(ps[:, u % 8, :], inp[:, P * k:P * k + P], xsT[:, b * TB:b * TB + TB],
                              start=True, stop=True).then_inc(s_pj, 1)
            pe.wait_ge(s_pja, len(PROJ_ACT))
            pe.wait_ge(s_pjv, len(PROJ_DVE))
            pe.wait_ge(s_fs, 1)
            pe.wait_ge(s_flo, 2)
            with pe.Fori(0, NB) as blk_i:
                toks = bass.ds(blk_i * TB, TB)
                for what, o in LAYER1:
                    if what == "UP":
                        if o >= 2:
                            pe.wait_ge(s_fg, blk_i * FO + (o - 1))
                        if o == 1:
                            pe.wait_ge(s_fr, blk_i + 1)
                        x = (xnTh[:, toks], xnTl[:, toks])
                        for i in range(2):
                            cols_ = slice(FH * i + P * o, FH * i + P * o + P)
                            m = product(pe, ps[:, ffn_bank(2 * o + i), :], (f12hf[:, cols_], f12lf[:, cols_]), x,
                                        start=True, stop=True)
                        m.then_inc(s_fu, 1)
                    elif what == "MID1":
                        out_cols = slice(P * o, P * o + P)
                        pe.wait_ge(s_fh1, 1)
                        pe.wait_ge(s_fg, blk_i * FO + (3 + o // 2))
                        for k in range(FO):
                            pe.wait_ge(s_fal, blk_i * FO + (k + 1))
                            m = product(pe, ps[:, ffn_bank(8 + o), :], (fh1h[:, k, out_cols], fh1l[:, k, out_cols]),
                                        (fah[:, k, :], fal[:, k, :]), start=(k == 0), stop=(k == FO - 1))
                        m.then_inc(s_f2, 1)
                    elif what == "MID2":
                        out_cols = slice(P * o, P * o + P)
                        pe.wait_ge(s_flo, len(FSPLIT) - 1)
                        for k in range(FO):
                            pe.wait_ge(s_fbl, blk_i * FO + (k + 1))
                            m = product(pe, ps[:, ffn_bank(12 + o), :], (fh2h[k][:, out_cols], fh2l[:, k, out_cols]),
                                        (fbh[:, k, :], fbl[:, k, :]), start=(k == 0), stop=(k == FO - 1))
                        m.then_inc(s_f3, 1)
                    elif what == "DOWN":
                        pe.wait_ge(s_fg3, blk_i * FO + 2 * FO)
                        for i in range(TPB):
                            for k in range(FO):
                                m = pe.matmul(ps[:, ffn_bank(16), P * i:P * i + P], fa[:, k, P * i:P * i + P],
                                              f3[:, k, :], start=(k == 0), stop=(k == FO - 1))
                        m.then_inc(s_f4, 1)
                    elif what == "CHUNK":
                        pe.wait_ge(s_stage, blk_i * 4 + 3)
                        pe.wait_ge(s_cx, blk_i * (2 * TPB) + (2 * o + 2))
                        pe.wait_ge(s_ce, blk_i * (2 * TPB) + (2 * o + 2))
                        pe.matmul(ps[:, 0, 0:P], BTs[:, P * o:P * o + P], CT[:, bass.ds(blk_i * TB + o * P, P)],
                                  start=True, stop=True)
                        for m_ in range(MI):
                            pe.transpose(ps[:, 0, P + P * m_:2 * P + P * m_], xcs[:, m_, P * o:P * o + P], ident)
                        for h in range(NH):
                            m = pe.matmul(ps[:, 1, P * h:P * h + P], avs[:, o, h:h + 1].broadcast_to([P, P]), tri,
                                          start=True, stop=True)
                        m.then_inc(s_c1, 1)
                    elif what == "STATE":
                        b = o % 2
                        pe.wait_ge(s_stage, blk_i * 4 + 4)
                        pe.wait_ge(s_cm, blk_i * (2 * TPB) + (2 * o + 6))
                        pe.wait_ge(s_cx, blk_i * (2 * TPB) + (2 * o + 4))
                        pe.wait_ge(s_ch, blk_i * TPB + (o + 2))
                        pe.wait_ge(s_ca, blk_i * TPB + (o + 1))
                        for h in range(NH):
                            dst = ps[PD * (h % 2):PD * (h % 2) + PD, 2, P * (h // 2):P * (h // 2) + P]
                            pe.matmul(dst, dtx[:, b, h, :], mm[:, b, h, :], start=True, stop=False)
                            m = pe.matmul(dst, hst[:, h, :], cs[:, b, h, :], start=False, stop=True)
                        m.then_inc(s_cy, 1)
                        pe.matmul(ps[:, 3, 0:DI], btds[:, o, :], dtw[:, b].rearrange("p h d -> p (h d)"),
                                  start=True, stop=True).then_inc(s_cst, 1)
                    else:
                        pe.wait_ge(s_cg, blk_i * TPB + (o + 2))
                        for m_ in range(MI):
                            m = pe.matmul(ps[:, 2, 2 * P:2 * P + D], yg[:, o % 2, m_, :], owT[:, m_, :],
                                          start=(m_ == 0), stop=(m_ == MI - 1))
                        m.then_inc(s_co, 1)

        @block.vector
        def _(dve):
            step = Steps(dve, s_v)
            for i in range(NT):
                if i % TPB == 0:
                    dve.wait_ge(s_x[i // TPB], 16)
                step.mark(dve.bn_stats(stats[:, i, :], res[:, i, :]))
            step.settle()
            for i in range(NT):
                m = dve.bn_aggr(mv[:, i, :], stats[:, i, :])
            m.then_inc(s_var, 1)
            dve.wait_ge(s_sd, 1)
            step.alone(dve.reciprocal(rstd, sd))
            for i in range(NT):
                dve.tensor_scalar(xn[:, i, :], res[:, i, :], mv[:, i, 0:1], rstd[:, i:i + 1],
                                  ALU.subtract, ALU.mult).then_inc(s_xn, 1)
            step.alone(dve.tensor_tensor(ms, mv[:, :, 1], rstd, ALU.mult))
            dve.tensor_tensor(ms, ms, rstd, ALU.mult).then_inc(s_var, 1)
            dve.wait_ge(s_wqkv, 16 * 5)
            dve.tensor_scalar(wqkv, wqkv, ln1, None, ALU.mult).then_inc(s_wsc, 1)
            dve.wait_ge(s_const, 16)
            dve.tensor_copy(identb, ident).then_inc(s_idb, 1)
            step.alone(dve.tensor_tensor(kw, qn_bc, kn_bc, ALU.mult))
            step.mark(dve.tensor_scalar(kw, kw, QD ** -0.5, None, ALU.mult))
            step.mark(dve.tensor_reduce(mx2[:, 0:1], qn_bc, X_AXIS, ALU.max, apply_absolute_value=True))
            step.mark(dve.tensor_reduce(mx2[:, 1:2], kn_bc, X_AXIS, ALU.max, apply_absolute_value=True))
            step.settle()
            step.alone(dve.tensor_tensor(shift, mx2[:, 0:1], mx2[:, 1:2], ALU.mult))
            dve.tensor_scalar(shift, shift, -(QD ** 0.5), None, ALU.mult).then_inc(s_shift, 1)
            dve.wait_ge(s_sd, 2)
            step.alone(dve.reciprocal(hs, sd2))
            dve.wait_ge(s_xnTc, NB)
            step.mark(dve.tensor_reduce(summT[:, 1:NC],
                                        xnT[:, 1:1 + CHUNK * (NC - 1)].rearrange("p (c t) -> p c t", t=CHUNK),
                                        X_AXIS, ALU.add))
            step.settle()
            step.mark(dve.tensor_scalar(summT[:, 1:NC], summT[:, 1:NC], 1.0 / CHUNK, None, ALU.mult))
            dve.tensor_copy(summT[:, 0:1], xnT[:, 0:1]).then_inc(s_summ, 1)
            step.settle()
            dve.sem_inc(s_summ, 1)
            for i in range(NT):
                dve.wait_ge(s_qkvp, i - i % 2 + 2)
                src = ps[:, 4 + (i // 2) % 4, (i % 2) * QKV_W:(i % 2) * QKV_W + QKV_W]
                dve.scalar_tensor_tensor(qkv[:, i, :], src, hs[:, i:i + 1], bqkv, ALU.mult, ALU.add
                                         ).then_inc(s_qkvc, 1)
            dve.wait_ge(s_qkvc, NT)
            qk = qkv[:, :, 0:160].rearrange("p i (d h) -> p i d h", d=QD)
            c_b = cosT.unsqueeze(3).broadcast_to([P, NT, 4, 20])
            s_b = sinT.unsqueeze(3).broadcast_to([P, NT, 4, 20])
            for half, (wa, wb, op) in enumerate(((c_b, s_b, ALU.subtract), (s_b, c_b, ALU.add))):
                step.mark(dve.tensor_tensor(rot_a, qk[:, :, 0:4, :], wa, ALU.mult))
                step.mark(dve.tensor_tensor(rot_b, qk[:, :, 4:8, :], wb, ALU.mult))
                step.settle()
                m = dve.tensor_tensor(rot[:, :, 4 * half:4 * half + 4, :], rot_a, rot_b, op)
                if half == 0:
                    step.alone(m)
            m.then_inc(s_rot, 1)
            dve.wait_ge(s_kv, 1)
            dve.wait_ge(s_pad, 2)
            for src, bias, bd, scale in ((0, bk0, kbd, HD ** -0.5), (256, bv0, vbd, 1.0)):
                step.alone(dve.tensor_tensor(kvb, ps[:, 0, src:src + 256].rearrange("p (j c) -> p j c", j=HC),
                                             over(bias, NC), ALU.add))
                for a in range(2):
                    step.mark(dve.tensor_scalar(bd[64 * a:64 * a + 64, :, a, :], kvb[64 * a:64 * a + 64], scale, None,
                                                ALU.mult))
                step.settle()
                dve.sem_inc(s_kbd, 1)
            dve.wait_ge(s_vp, 1)
            dve.tensor_copy(vp[:, :, :, 0:QD], qkv[:, :, 160:192].rearrange("p i (g d) -> p i g d", d=QD)
                            ).then_inc(s_vp, 1)
            dve.wait_ge(s_sq, 1)
            dve.tensor_reduce(ssq, sq.rearrange("p i d h -> p i h d"), X_AXIS, ALU.add).then_inc(s_ssq, 1)
            dve.wait_ge(s_qksd, 1)
            step.alone(dve.reciprocal(ssq, rr))
            step.alone(dve.tensor_tensor(rot, rot, ssq.rearrange("p (i h) -> p i h", i=NT).unsqueeze(2).broadcast_to(
                [P, NT, QD, 20]), ALU.mult))
            kr = rot[:, :, :, NQ:20]
            step.alone(dve.tensor_tensor(kr, kr, over(along(kw, NT), NKV),
                                         ALU.mult))
            by_head = lambda split: split.rearrange("p i (d h) -> p i d h", d=QD)
            for s in range(NSPLIT):
                parts = ((by_head(qs[:, :, s, :]), rot[:, :, :, 0:NQ]), (by_head(ks[:, :, s, :]), kr))
                for spl, src in parts:
                    step.mark(dve.tensor_copy(spl, src))
                step.settle()
                dve.sem_inc(s_split, 1)
                if s < NSPLIT - 1:
                    for spl, src in parts:
                        step.mark(dve.tensor_tensor(src, src, spl, ALU.subtract))
                    step.settle()
            dve.wait_ge(s_splT, 8)
            dve.tensor_copy(qT[:, 2, 1024:2048], ps[:, 5, :].bitcast(BF16)).then_inc(s_splTv, 1)
            step.alone(dve.tensor_tensor(res, res, along(bo0_bc, NT), ALU.add))
            dve.wait_ge(s_gc, 3)
            dve.wait_ge(s_wrest, 16 * 25)
            dve.wait_ge(s_xnT, NB)
            step.alone(dve.tensor_tensor(xn, xn, along(bo_bc, NT), ALU.add))
            dve.wait_ge(s_pad, 4)
            dve.wait_ge(s_qst, 16 * 2 * NSPLIT)
            dve.wait_ge(s_vp, 2)
            dve.sem_inc(s_accc, 1)
            dve.sem_inc(s_mr, 1)
            vp_flat = r3[:, 0:2048].rearrange("p (i c) -> p i c", i=NT)
            att_blocks = att
            events = sorted([(k, 3, n) for n, (k, _, _) in enumerate(AUX)]
                            + [(LAST[qb] + LAG, 1, qb) for qb in range(NB)]
                            + [(k + 1, 2, m) for k, m in SUMM_EXP.items()])
            with dve.Fori(0, NKV) as g:
                dve.wait_ge(s_pv, g * KB + KB)
                dve.tensor_copy(vc, vp_flat[:, :, bass.ds(g * 32, 32)]).then_inc(s_vc, 1)
                for k, kind, n in events:
                    if kind == 1:
                        dve.wait_ge(s_pv, g * KB + (KB + LAST[n] + 1))
                        dve.tensor_copy(accT[:, n % 2, :], ps[:, 6, :]).then_inc(s_accc, 1)
                        continue
                    if kind == 2:
                        m, w = n, summ_chunks(n)
                        blk = sc[:, m % 2, :, 0:w]
                        dve.wait_ge(s_ex, g * NB + (m + 1))
                        dve.tensor_reduce(ssm_[:, m % 2, :], blk, X_AXIS, ALU.add).then_inc(s_sm, 1)
                        dve.wait_ge(s_sm, g * 4 * NB + (4 * m + 3))
                        dve.reciprocal(ssm_[:, m % 2, :], ssm_[:, m % 2, :]).then_inc(s_sm, 1)
                        dve.wait_ge(s_sm, g * 4 * NB + (4 * m + 4))
                        dve.tensor_tensor(pr[:, m, :].rearrange("p (h c) -> p h c", h=HEADS)[:, :, 0:w], blk,
                                          over(ssm_[:, m % 2, :], w), ALU.mult).then_inc(s_pr, 1)
                        continue
                    _, what, m = AUX[n]
                    dve.wait_ge(s_mf, g * NAUX + (n + 1))
                    w = summ_chunks(m)
                    if what == "SCORE":
                        blk = sc[:, m % 2, :, 0:w]
                        ended = sc[:, m % 2, :, w - NC // NB:w]
                        dve.tensor_tensor(blk, ps[:, SHARED, 0:HEADS * w].rearrange("p (h c) -> p h c", h=HEADS),
                                          g0[:, :, 0:w], ALU.add).then_inc(s_mr, 1)
                        dve.wait_ge(s_mr, g * NAUX + (n + 2))
                        dve.tensor_tensor(ended, ended, along(cmask[:, bass.ds(g * 8, 8)], HEADS), ALU.add
                                          ).then_inc(s_sm, 1)
                        dve.wait_ge(s_sm, g * 4 * NB + (4 * m + 1))
                        dve.tensor_reduce(smx[:, m % 2, :], blk, X_AXIS, ALU.max).then_inc(s_sm, 1)
                        dve.wait_ge(s_sm, g * 4 * NB + (4 * m + 2))
                        dve.tensor_tensor(blk, blk, over(smx[:, m % 2, :], w), ALU.subtract).then_inc(s_sub, 1)
                    elif what == "TRANSPOSE":
                        dve.tensor_copy(ptr, ps[:, SHARED, :]).then_inc(s_mr, 1)
                    elif what == "OUTPUT":
                        tile = res_flat[:, bass.ds(g * D + m * (TPB * D), D)]
                        dve.tensor_tensor(tile, tile, ps[:, SHARED, 0:D], ALU.add).then_inc(s_mr, 1)
                    else:
                        src = ps[:, SHARED, :].rearrange("p (ij m) -> p ij m", m=32)
                        dve.reciprocal(rden[:, m % 2, :], src[:, :, QD]).then_inc(s_rden, 1)
                        dve.wait_ge(s_rden, g * NB + (m + 1))
                        dve.tensor_tensor(
                            att_blocks[:, TPB * m:TPB * m + TPB, bass.ds(g * 32, 32)].rearrange(
                                "p i (j d) -> p i j d", d=QD),
                            src[:, :, 0:QD].rearrange("p (i j) d -> p i j d", i=TPB),
                            over(rden[:, m % 2, :].rearrange("p (i j) -> p i j", i=TPB), QD), ALU.mult
                            ).then_inc(s_mr, 1)
            for b in range(NB):
                dve.wait_ge(s_gt, b + 1)
                blk = oT[:, b * TB:b * TB + TB]
                dve.tensor_tensor(blk, blk, gate[:, b * TB:b * TB + TB], ALU.mult).then_inc(s_og, 1)
            for b in range(NB):
                dve.wait_ge(s_wo, b + 1)
                blk = xn[:, TPB * b:TPB * b + TPB, :]
                dve.tensor_tensor(blk, blk, ps[:, 4 + b, :].rearrange("p (i d) -> p i d", d=D), ALU.add
                                  ).then_inc(s_xm, 1)
            for b in range(NB):
                dve.wait_ge(s_sq2, b + 1)
                dve.tensor_reduce(ssq2[:, TPB * b:TPB * b + TPB], sqm[:, TPB * b:TPB * b + TPB, :], X_AXIS, ALU.add
                                  ).then_inc(s_ss2, 1)
            dve.wait_ge(s_sd2, 1)
            step.alone(dve.reciprocal(hs2, sdm))
            for i in range(NT):
                dve.tensor_scalar(h2[:, i, :], xn[:, i, :], hs2[:, i:i + 1], None, ALU.mult).then_inc(s_h2, 1)
            step.alone(dve.tensor_tensor(res, res, xn, ALU.add))
            for b in range(NB):
                blk = slice(b * TB, b * TB + TB)
                dve.wait_ge(s_h2s, b + 1)
                dve.tensor_tensor(h2l[:, blk], h2T[:, blk], h2h[:, blk], ALU.subtract).then_inc(s_h2l, 1)
            dve.wait_ge(s_lg, 1)
            step.alone(dve.tensor_tensor(lg, ps[:, 4, 0:P].rearrange("p (i e) -> p i e", e=E), along(br_bc, NT),
                                         ALU.add))
            step.alone(dve.tensor_reduce(lmx, lg, X_AXIS, ALU.max))
            step.alone(dve.tensor_tensor(eq, lg, over(lmx, E), ALU.is_equal))
            step.alone(dve.tensor_tensor(rk, eq, along(rank, NT), ALU.mult))
            step.alone(dve.tensor_reduce(lmx2, rk, X_AXIS, ALU.max))
            dve.tensor_tensor(oh, rk, over(lmx2, E), ALU.is_equal).then_inc(s_oh, 1)
            dve.wait_ge(s_ohT, 1)
            ohT_ps = ps[0:E, 4:8, :].rearrange("p b t -> p (b t)")
            dve.tensor_scalar(pen, ohT_ps, 1.0, BIG, ALU.subtract, ALU.mult).then_inc(s_pen, 1)
            ES = E * FC
            stats_flat = stats.rearrange("p i s -> p (i s)")
            dve.sem_inc(s_moea, ES)
            dve.sem_inc(s_ya, 1)
            with dve.Fori(0, NB) as tb:
                for n in range(ES):
                    e, c = divmod(n, FC)
                    dve.wait_ge(s_sg, tb * ES + (n + 1))
                    free = ES + n - 2 if n >= 3 else last_user(n, 3, ES) + 1
                    dve.wait_ge(s_dn, tb * ES + free)
                    dve.scalar_tensor_tensor(am[:, n % 3, :], ps[:, 2 * (n % 3), :], b1c[:, e, c:c + 1],
                                             sg[:, n % 3, :], ALU.add, ALU.mult).then_inc(s_moea, 1)
                    dve.wait_ge(s_moea, tb * ES + (ES + n + 1))
                    dve.tensor_copy(amh[:, n % 3, :], am[:, n % 3, :]).then_inc(s_amh, 1)
                    dve.wait_ge(s_amh, tb * ES + (n + 1))
                    dve.tensor_tensor(aml[:, n % 3, :], am[:, n % 3, :], amh[:, n % 3, :], ALU.subtract
                                      ).then_inc(s_aml, 1)
                dve.wait_ge(s_yt, tb + 2)
                blk = res_flat[:, bass.ds(tb * TB, TB)]
                dve.tensor_tensor(blk, blk, ps[:, 7, :], ALU.add).then_inc(s_ya, 1)
                dve.wait_ge(s_ya, tb + 2)
                for i in range(TPB):
                    dve.bn_stats(stats_flat[:, bass.ds(tb * (6 * TPB) + 6 * i, 6)],
                                 res_flat[:, bass.ds(tb * TB + i * D, D)]).then_inc(s_bn, 1)
            dve.wait_ge(s_bn, NT)
            for i in range(NT):
                m = dve.bn_aggr(mv[:, i, :], stats[:, i, :])
            m.then_inc(s_var2, 1)
            dve.wait_ge(s_sdl, 1)
            step.alone(dve.reciprocal(rstd, sd))
            step.alone(dve.tensor_tensor(ms, mv[:, :, 1], rstd, ALU.mult))
            dve.tensor_tensor(ms, ms, rstd, ALU.mult).then_inc(s_var2, 1)
            dve.wait_ge(s_sdl, 2)
            step.alone(dve.reciprocal(hs, sd2))
            step.alone(dve.tensor_tensor(hs, hs, rstd, ALU.mult))
            for i in range(NT):
                dve.tensor_scalar(xs[:, i, :], res[:, i, :], mv[:, i, 0:1], hs[:, i:i + 1],
                                  ALU.subtract, ALU.mult).then_inc(s_xs, 1)
            for i in range(NT):
                dve.tensor_scalar(xn[:, i, :], res[:, i, :], mv[:, i, 0:1], rstd[:, i:i + 1],
                                  ALU.subtract, ALU.mult).then_inc(s_xn2, 1)
            for g in range(6):
                n = min(3, NT - 3 * g)
                dve.wait_ge(s_bt, g + 1)
                dve.tensor_copy(btd[:, 3 * g:3 * g + n, :],
                                ps[:, g, 0:132 * n].rearrange("p (i c) -> p i c", c=132)
                                ).then_inc(s_btc, 1)
            dve.wait_ge(s_btc, 6)
            step.alone(dve.tensor_tensor(du, btd[:, :, P:P + NH], along(dtb, NT), ALU.add))
            dve.scalar_tensor_tensor(dl, du, -1.0, du, ALU.mult, ALU.min).then_inc(s_dta, 1)
            for credit, n in ((s_fm, FO), (s_fr, 1), (s_cx, 2), (s_cg, 1), (s_ca, 1), (s_ch, 1)):
                dve.sem_inc(credit, n)
            dve.wait_ge(s_pad, 5)
            for b in range(NB):
                if b == 1:
                    dve.wait_ge(s_dtb, 3)
                    step.alone(dve.scalar_tensor_tensor(dt, du, 0.0, dl, ALU.max, ALU.add))
                    dve.scalar_tensor_tensor(av, dt, -1.0, along(ea, NT), ALU.mult, ALU.mult).then_inc(s_av, 1)
                    dve.wait_ge(s_av, 1)
                    step.alone(dve.tensor_scalar(dt, dt, 0.5, None, ALU.mult))
                toks = slice(b * TB, b * TB + TB)
                for k in (0, 1):
                    dve.wait_ge(s_zth, 2 * b + k + 1)
                    dve.scalar_tensor_tensor(z2[:, k, toks], th[:, k, :], 1.0, ps[:, proj_bank(f"z{k}", b), :],
                                             ALU.add, ALU.mult).then_inc(s_pjv, 1)
                dve.wait_ge(s_pj, PROJ.index(("B", b)) + 1)
                dve.tensor_copy(BT[:, toks], ps[:, proj_bank("B", b), :]).then_inc(s_pjv, 1)

                def conv_from_psum(b):
                    if b not in CONV_ON_PE:
                        conv(dve, step, 1, b)
                        dve.sem_inc(s_xcv, 1)
                        return
                    dve.wait_ge(s_pj, PROJ.index(("K", b)) + 1)
                    dve.tensor_scalar(xc[:, 1, b * TB:b * TB + TB], ps[:, proj_bank("K", b), :], convb[:, 1:2], None,
                                      ALU.add).then_inc(s_pjv, 1)
                    dve.wait_ge(s_pjv, PROJ_DVE.index(("K", b)) + 1)
                    dve.sem_inc(s_xcv, 1)

                def silu(b):
                    blk = xc[:, :, b * TB:b * TB + TB]
                    dve.wait_ge(s_xth, b + 1)
                    dve.scalar_tensor_tensor(blk, thc, 1.0, blk, ALU.add, ALU.mult).then_inc(s_xc, 1)

                if b >= 1:
                    conv_from_psum(b - 1)
                if b == 2:
                    dve.wait_ge(s_pj, PROJ.index(("A", 0)) + 1)
                    dve.tensor_copy(cums, ps[:, proj_bank("A", 0), 0:NT * NH].rearrange("p (i h) -> p i h", i=NT)
                                    ).then_inc(s_pjv, 1)
                dve.wait_ge(s_pja, PROJ_ACT.index(("x1", b)) + 1)
                conv(dve, step, 0, b)
                if b == NB - 1:
                    silu(b - 1)
                    conv_from_psum(b)
                    silu(b)
                elif b >= 1:
                    silu(b - 1)
            dve.wait_ge(s_fhi, len(FSPLIT))
            dve.tensor_tensor(fh1l, fh1, fh1h, ALU.subtract).then_inc(s_fh1, 1)
            cums_f, dt_f = (a.rearrange("p i h -> p (i h)") for a in (cums, dt))
            CSTEPS = 4 * TPB
            with dve.Fori(0, NB) as blk_i:
                steps = 0
                for what, o in DVE_ORDER:
                    b = o % 2
                    chunk4 = bass.ds(blk_i * (TPB * NH) + o * NH, NH)
                    if what == "UP":
                        if o == 0:
                            dve.wait_ge(s_f4, blk_i + 1)
                        dve.wait_ge(s_ft, blk_i * FO + (o + 1))
                        dve.scalar_tensor_tensor(fa[:, o, :], fth[:, o % 2, :], 1.0, ps[:, ffn_bank(2 * o), :],
                                                 ALU.add, ALU.mult).then_inc(s_fm, 1)
                        dve.wait_ge(s_fm, blk_i * FO + (FO + o + 1))
                        dve.scalar_tensor_tensor(fa[:, o, :], fa[:, o, :], s12[:, o:o + 1],
                                                 ps[:, ffn_bank(2 * o + 1), :], ALU.mult, ALU.mult
                                                 ).then_inc(s_fg, 1)
                    elif what == "CHUNK":
                        dve.wait_ge(s_c1, blk_i * TPB + (o + 1))
                        dve.wait_ge(s_cm, blk_i * (2 * TPB) + (2 * o + 2))
                        dve.tensor_tensor(ed[:, b], ps[:, 1, :].rearrange("p (h t) -> p h t", h=NH),
                                          over(cums_f[:, chunk4], P), ALU.subtract).then_inc(s_cstep, 1)
                        steps += 1
                        dve.wait_ge(s_cstep, blk_i * CSTEPS + steps)
                        dve.tensor_scalar(ed[:, b], ed[:, b], 0.0, None, ALU.min).then_inc(s_cd, 1)
                        dve.tensor_tensor(gm[:, b, :], ps[:, 0, 0:P], tri, ALU.mult).then_inc(s_cx, 1)
                    elif what == "GATED":
                        dve.wait_ge(s_fah, blk_i * FO + (o + 1))
                        dve.tensor_tensor(fal[:, o, :], fa[:, o, :], fah[:, o, :], ALU.subtract).then_inc(s_fal, 1)
                    elif what == "MIDDLE":
                        dve.wait_ge(s_fbh, blk_i * FO + (o + 1))
                        dve.tensor_tensor(fbl[:, o, :], fb[:, o, :], fbh[:, o, :], ALU.subtract).then_inc(s_fbl, 1)
                    elif what == "WEIGHT":
                        dve.wait_ge(s_cst, blk_i * TPB + (o + 1))
                        dve.tensor_tensor(dtx[:, b], ps[:, 0, P:P + DI].rearrange("p (h d) -> p h d", h=NH),
                                          over(dt_f[:, chunk4], PD), ALU.mult).then_inc(s_cstep, 1)
                        steps += 1
                        dve.wait_ge(s_cstep, blk_i * CSTEPS + steps)
                        dve.wait_ge(s_ce, blk_i * (2 * TPB) + (2 * o + 3))
                        dve.tensor_tensor(dtw[:, b], dtx[:, b], over(ed[:, b, :, P - 1], PD), ALU.mult
                                          ).then_inc(s_cx, 1)
                    elif what == "STATE":
                        dve.wait_ge(s_cy, blk_i * TPB + (o + 3))
                        dve.wait_ge(s_ce, blk_i * (2 * TPB) + (2 * o + 4))
                        dve.tensor_tensor(hst, hst, over(ec[:, b, :, P - 1], PD), ALU.mult).then_inc(s_cstep, 1)
                        steps += 1
                        dve.wait_ge(s_co, blk_i * TPB + (o + 1))
                        for m_ in range(MI):
                            m = dve.scalar_tensor_tensor(yg[:, b, m_, :], xcs[:, m_, P * o:P * o + P],
                                                         d2[:, m_:m_ + 1], ps[:, 2, P * m_:P * m_ + P],
                                                         ALU.mult, ALU.add)
                        m.then_inc(s_cstep, 1)
                        steps += 1
                        dve.wait_ge(s_cstep, blk_i * CSTEPS + steps)
                        dve.wait_ge(s_cst, blk_i * TPB + (o + 3))
                        dve.tensor_tensor(hst, hst, ps[:, 3, 0:DI].rearrange("p (h d) -> p h d", h=NH), ALU.add
                                          ).then_inc(s_ch, 1)
                        dve.tensor_tensor(yg[:, b], yg[:, b], z2[:, :, bass.ds(blk_i * TB + o * P, P)], ALU.mult
                                          ).then_inc(s_cg, 1)
                    elif what == "PROJECT":
                        dve.wait_ge(s_co, blk_i * TPB + (o + 3))
                        tile = res_flat[:, bass.ds(blk_i * TB + o * D, D)]
                        dve.tensor_tensor(tile, tile, ps[:, 2, 2 * P:2 * P + D], ALU.add).then_inc(s_ca, 1)
                    elif what == "DOWN":
                        dve.wait_ge(s_f4, blk_i + 2)
                        dve.tensor_tensor(fst, ps[:, ffn_bank(16), :].rearrange("p (i d) -> p i d", i=TPB),
                                          along(w3s_bc, TPB), ALU.mult).then_inc(s_fr, 1)
                        dve.wait_ge(s_fr, blk_i + 2)
                        dve.wait_ge(s_ca, blk_i * TPB + (TPB + 1))
                        blk = res_flat[:, bass.ds(blk_i * TB, TB)]
                        dve.tensor_tensor(blk, blk, fst.rearrange("p i d -> p (i d)"), ALU.add).then_inc(s_fin, 1)


def kernel(**inputs):
    import concourse.bacc as bacc
    from concourse.bass_utils import run_bass_kernel_spmd

    f = {k: np.asarray(v) for k, v in inputs.items()}
    row_ = lambda a: a.reshape(1, -1)
    cols = lambda a, n: a.reshape(n, P).T
    inT = f["L1_attn_in_proj_w"].T

    def heads_inner(q, k, v):
        qk = np.concatenate([q.reshape(-1, NQ, QD), k.reshape(-1, NKV, QD)], axis=1)
        return np.concatenate([qk.transpose(0, 2, 1).reshape(len(q), -1), v], axis=1)

    arrays = {
        "x": f["L0_attn_x"][0],
        "a_WqT": f["L0_attn_Wq"].T, "a_Wk": f["L0_attn_Wk"], "a_Wv": f["L0_attn_Wv"], "a_Wo": f["L0_attn_Wo"],
        "a_bq": cols(f["L0_attn_bq"], HC), "a_bk": cols(f["L0_attn_bk"], HC), "a_bv": cols(f["L0_attn_bv"], HC),
        "a_bo": row_(f["L0_attn_bo"]),
        "f_ln1": f["L0_ffn_ln1_w"].reshape(P, 1), "f_ln2": f["L0_ffn_ln2_w"].reshape(P, 1),
        "f_Wqkv": heads_inner(f["L0_ffn_Wq"], f["L0_ffn_Wk"], f["L0_ffn_Wv"]),
        "f_bqkv": heads_inner(row_(f["L0_ffn_bq"]), row_(f["L0_ffn_bk"]), row_(f["L0_ffn_bv"])),
        "f_qn": row_(f["L0_ffn_qn_w"]), "f_kn": row_(f["L0_ffn_kn_w"]),
        "f_Wg": f["L0_ffn_Wg"], "f_bgc": np.tile(f["L0_ffn_bg"], NQ).reshape(P, 1),
        "f_Wo": f["L0_ffn_Wo"], "f_bo": row_(f["L0_ffn_bo"]),
        "f_Wr": f["L0_ffn_Wr"], "f_br": row_(f["L0_ffn_br"]),
        "f_W1": f["L0_ffn_W1"], "f_b1c": f["L0_ffn_b1"].reshape(E, 2 * FC, P).transpose(2, 0, 1).reshape(P, -1),
        "f_W2": f["L0_ffn_W2"], "f_b2": f["L0_ffn_b2"],
        "s_norm": f["L1_attn_norm_w"].reshape(P, 1),
        "s_inT": np.concatenate([inT[:, 0:2 * DI], inT[:, 2 * DI + P:2 * DI + 2 * P],
                                 inT[:, 2 * DI:2 * DI + P], inT[:, 2 * DI + 2 * P:]], axis=1),
        "s_convw": f["L1_attn_conv_w"].reshape(MI, P, KW).transpose(1, 0, 2).reshape(P, -1),
        "s_convb": cols(f["L1_attn_conv_b"], MI),
        "s_D": np.repeat(f["L1_attn_D"], PD).reshape(MI, P).T,
        "s_dtb": row_(f["L1_attn_dt_bias"]), "s_Alog": row_(f["L1_attn_A_log"]),
        "s_outT": f["L1_attn_out_proj_w"].T,
        "g_w1T": f["L1_ffn_w1_w"].T, "g_w2T": f["L1_ffn_w2_w"].T,
        "g_h1T": f["L1_ffn_h1_w"].T, "g_h2T": f["L1_ffn_h2_w"].T, "g_w3T": f["L1_ffn_w3_w"].T,
        "g_w1s": cols(f["L1_ffn_w1_s"], FO), "g_w2s": cols(f["L1_ffn_w2_s"], FO),
        "g_h1s": cols(f["L1_ffn_h1_s"], FO), "g_h2s": cols(f["L1_ffn_h2_s"], FO),
        "g_w3s": row_(f["L1_ffn_w3_s"]),
    }
    inv = (np.float32(1.0) / np.float32(10000.0) ** (np.arange(0, QD, 2, dtype=np.float32) / np.float32(QD))
           ).astype(np.float32)
    ang = np.arange(T, dtype=np.float32)[:, None] * inv[None, :]
    table = lambda a: a.astype(np.float32).reshape(NT, P, 4).transpose(1, 0, 2).reshape(P, -1)
    p_, r_, c_ = np.ogrid[0:P, 0:TPB, 0:NC // NB]
    cmask = np.where(CHUNK * c_ <= P * r_ + p_, 0.0, -BIG).astype(np.float32).reshape(P, -1)
    arrays["consts"] = np.concatenate([np.eye(P, dtype=np.float32), np.triu(np.ones((P, P), np.float32)),
                                       table(np.cos(ang)), table(np.sin(ang))], axis=1)
    arrays["cmask"] = cmask
    arrays["rank"] = np.arange(E, 0, -1, dtype=np.float32).reshape(1, E)

    nc = bacc.Bacc("TRN2", target_bir_lowering=False, num_devices=1)
    arrays = {k: np.ascontiguousarray(v) for k, v in arrays.items()}
    io = {k: nc.dram_tensor(f"in_{k}", a.shape, mybir.dt.from_np(a.dtype), kind="ExternalInput").ap()
          for k, a in arrays.items()}
    out = nc.dram_tensor("out", (T, D), F32, kind="ExternalOutput").ap()
    build(nc, io, out)
    r = run_bass_kernel_spmd(nc, [{f"in_{k}": a for k, a in arrays.items()}], core_ids=[0])
    return r.results[0]["out"].reshape(1, T, D)
```
